# Optimizing a Trainium2 kernel written in Bass

```python
import numpy as np
import jax
import jax.numpy as jnp

def _softmax(x, axis=-1):
    return jax.nn.softmax(x, axis=axis)

def _gelu(x):
    return jax.nn.gelu(x, approximate=True)

def _silu(x):
    return jax.nn.silu(x)

def _sigmoid(x):
    return jax.nn.sigmoid(x)

def _layernorm(x, axis=-1, eps=1e-05):
    m = jnp.mean(x, axis=axis, keepdims=True)
    v = jnp.var(x, axis=axis, keepdims=True)
    return (x - m) / jnp.sqrt(v + eps)

def _scatter_add(tgt, idx, src, axis=0):
    return tgt.at[idx].add(src)

def _segment_sum(src, seg, n):
    return jax.ops.segment_sum(src, seg, n)
kernel_name = 'mk_flamingo_gated_d2_seqx_r8_41317c'

def setup_inputs(seed: int=0):
    np.random.seed(seed)
    _w = jnp.asarray

    def _rec_inputs():
        import jax
        import jax.numpy as jnp
        _rk = jax.random.key(seed)
        x = -0.000125 + 0.9999 * jax.random.normal(jax.random.fold_in(_rk, 1), (8, 128, 512), jnp.float32)
        _lenS = 128 - jax.random.randint(jax.random.fold_in(_rk, 7), (8,), 0, max(1, 128 // 4) + 1, jnp.int32)
        _lenS2 = 128 - jax.random.randint(jax.random.fold_in(_rk, 8), (8,), 0, max(1, 128 // 4) + 1, jnp.int32)
        _ctx_4096P = jax.random.normal(jax.random.fold_in(_rk, 11), (8, 16, 512), jnp.float32)
        _ctx_4096c = jax.random.dirichlet(jax.random.fold_in(_rk, 511), 0.3 * jnp.ones((16,), jnp.float32), (8, 128))
        _ctx_4096t = jnp.einsum('bsk,bkd->bsd', _ctx_4096c, _ctx_4096P)
        _ctx_4096t = _ctx_4096t * jax.lax.rsqrt(jnp.mean(jnp.square(_ctx_4096t)) + 1e-12) * 0.953939
        ctx_4096 = -1.52775e-05 + 0.999936 * (_ctx_4096t + 0.3 * jax.random.normal(jax.random.fold_in(_rk, 611), (8, 128, 512), jnp.float32))
        _validS = jnp.arange(128)[None, :] < _lenS[:, None]
        _validS2 = jnp.arange(128)[None, :] < _lenS2[:, None]
        _causal = jnp.tril(jnp.ones((128, 128), dtype=bool))
        mask_Bx1x4096_ff1 = jnp.where(jnp.ones((8, 1, 512), dtype=bool), 1.0, 0.0).astype(jnp.float32)
        _g = jax.random.normal(jax.random.fold_in(_rk, 9001), (2, 2), jnp.float32)
        _g = jnp.sign(_g) * jnp.maximum(jnp.abs(_g), 1.0) + (_g == 0) * 1.0
        g_xattn = _g[0]
        g_ffn = _g[1]
        return (x, ctx_4096, mask_Bx1x4096_ff1, g_xattn, g_ffn)
    x, ctx_4096, mask_Bx1x4096_ff1, g_xattn, g_ffn = _rec_inputs()

    def _L0_xattn_setup():
        import jax, jax.numpy as jnp
        import numpy as np
        W = 128
        H = 8
        D = 128
        DK = D // 2

        def _to_patches(x):
            b, d, s = x.shape
            np_ = s // W
            return x.reshape(b, d, np_, W).transpose(0, 2, 1, 3).reshape(b * np_, d, W)
        key = jax.random.key(seed)
        ks = jax.random.split(key, 10)
        B, S = (8, 512)
        qk = jax.random.normal(ks[0], (B, D, S), dtype=jnp.float32)
        v = jax.random.normal(ks[1], (B, D, S), dtype=jnp.float32)
        masks = jnp.ones((B, 1, S), dtype=jnp.float32)
        sc = 1.0 / np.sqrt(D)
        Wq = jax.random.normal(ks[2], (DK, D), dtype=jnp.float32) * sc
        bq = jnp.zeros((DK,), dtype=jnp.float32)
        Wk = jax.random.normal(ks[3], (DK, D), dtype=jnp.float32) * sc
        bk = jnp.zeros((DK,), dtype=jnp.float32)
        Wv = jax.random.normal(ks[4], (DK, D), dtype=jnp.float32) * sc
        bv = jnp.zeros((DK,), dtype=jnp.float32)
        Wo = jax.random.normal(ks[5], (D, DK), dtype=jnp.float32) * (1.0 / np.sqrt(DK))
        bo = jnp.zeros((D,), dtype=jnp.float32)
        return dict(qk=qk, v=v, masks=masks, Wq=Wq, bq=bq, Wk=Wk, bk=bk, Wv=Wv, bv=bv, Wo=Wo, bo=bo)
    _L0_xattn_all = _L0_xattn_setup()
    _L0_xattn_in = {k: v for k, v in _L0_xattn_all.items() if k in ('Wq', 'bq', 'Wk', 'bk', 'Wv', 'bv', 'Wo', 'bo')}
    del _L0_xattn_all

    def _L0_ffn_setup():
        import jax, jax.numpy as jnp
        import numpy as np
        FP8_MAX = 448.0

        def quantize_fp8(x, scale):
            return jnp.clip(x / scale, -FP8_MAX, FP8_MAX).astype(jnp.float8_e4m3fn)
        key = jax.random.key(seed)
        k1, k2 = jax.random.split(key)
        B, S, D_IN, D_OUT = (4, 256, 512, 512)
        x = jax.random.normal(k1, (B, S, D_IN), dtype=jnp.float32)
        w = jax.random.normal(k2, (D_OUT, D_IN), dtype=jnp.float32) * 0.02
        return {'x': x, 'w': w, 'input_scale': jnp.float32(0.02), 'weight_scale': jnp.float32(0.005), 'output_scale': jnp.float32(0.05)}
    _L0_ffn_all = _L0_ffn_setup()
    _L0_ffn_in = {k: v for k, v in _L0_ffn_all.items() if k in ('w', 'input_scale', 'weight_scale', 'output_scale')}
    del _L0_ffn_all

    def _L1_xattn_setup():
        import jax, jax.numpy as jnp
        import numpy as np
        HIDDEN = 512
        N_HEADS = 32
        N_KV_HEADS = 8
        HEAD_DIM = HIDDEN // N_HEADS
        N_REP = N_HEADS // N_KV_HEADS
        EPS = 1e-05

        def _rmsnorm(x, w):
            xf = x.astype(jnp.float32)
            var = jnp.mean(xf * xf, axis=-1, keepdims=True)
            return (xf * jax.lax.rsqrt(var + EPS)).astype(x.dtype) * w
        key = jax.random.key(seed)
        ks = jax.random.split(key, 7)
        B, Q, K = (2, 128, 256)
        scale = 0.02
        return {'hidden_states': jax.random.normal(ks[0], (B, Q, HIDDEN), jnp.float32), 'encoder_hidden_states': jax.random.normal(ks[1], (B, K, HIDDEN), jnp.float32), 'wq': jax.random.normal(ks[2], (N_HEADS * HEAD_DIM, HIDDEN), jnp.float32) * scale, 'wk': jax.random.normal(ks[3], (N_KV_HEADS * HEAD_DIM, HIDDEN), jnp.float32) * scale, 'wv': jax.random.normal(ks[4], (N_KV_HEADS * HEAD_DIM, HIDDEN), jnp.float32) * scale, 'wo': jax.random.normal(ks[5], (HIDDEN, N_HEADS * HEAD_DIM), jnp.float32) * scale, 'ln_w': jnp.ones((HIDDEN,), jnp.float32)}
    _L1_xattn_all = _L1_xattn_setup()
    _L1_xattn_in = {k: v for k, v in _L1_xattn_all.items() if k in ('wq', 'wk', 'wv', 'wo', 'ln_w')}
    del _L1_xattn_all

    def _L1_ffn_setup():
        import jax, jax.numpy as jnp
        import numpy as np
        ALPHA = 32
        R = 16
        SCALING = ALPHA / R
        key = jax.random.key(seed)
        k1, k2, k3, k4 = jax.random.split(key, 4)
        B_, S, D = (4, 256, 512)
        H, r, O = (8, R, 512)
        x = jax.random.normal(k1, (B_, S, D), dtype=jnp.float32)
        A = jax.random.normal(k2, (H, r, D), dtype=jnp.float32) * 0.02
        Bm = jax.random.normal(k3, (H, O, r), dtype=jnp.float32) * 0.02
        Wr = jax.random.normal(k4, (H, D), dtype=jnp.float32) * 0.02
        br = jnp.zeros((H,), dtype=jnp.float32)
        return {'x': x, 'A': A, 'B': Bm, 'Wr': Wr, 'br': br}
    _L1_ffn_all = _L1_ffn_setup()
    _L1_ffn_in = {k: v for k, v in _L1_ffn_all.items() if k in ('A', 'B', 'Wr', 'br')}
    del _L1_ffn_all
    return {'x': x, 'ctx_4096': ctx_4096, 'mask_Bx1x4096_ff1': mask_Bx1x4096_ff1, 'g_xattn': g_xattn, 'g_ffn': g_ffn, 'L0_xattn_Wq': _L0_xattn_in['Wq'], 'L0_xattn_bq': _L0_xattn_in['bq'], 'L0_xattn_Wk': _L0_xattn_in['Wk'], 'L0_xattn_bk': _L0_xattn_in['bk'], 'L0_xattn_Wv': _L0_xattn_in['Wv'], 'L0_xattn_bv': _L0_xattn_in['bv'], 'L0_xattn_Wo': _L0_xattn_in['Wo'], 'L0_xattn_bo': _L0_xattn_in['bo'], 'L0_ffn_w': _L0_ffn_in['w'], 'L0_ffn_input_scale': _L0_ffn_in['input_scale'], 'L0_ffn_weight_scale': _L0_ffn_in['weight_scale'], 'L0_ffn_output_scale': _L0_ffn_in['output_scale'], 'L1_xattn_wq': _L1_xattn_in['wq'], 'L1_xattn_wk': _L1_xattn_in['wk'], 'L1_xattn_wv': _L1_xattn_in['wv'], 'L1_xattn_wo': _L1_xattn_in['wo'], 'L1_xattn_ln_w': _L1_xattn_in['ln_w'], 'L1_ffn_A': _L1_ffn_in['A'], 'L1_ffn_B': _L1_ffn_in['B'], 'L1_ffn_Wr': _L1_ffn_in['Wr'], 'L1_ffn_br': _L1_ffn_in['br']}

def reference(x, ctx_4096, mask_Bx1x4096_ff1, g_xattn, g_ffn, L0_xattn_Wq, L0_xattn_bq, L0_xattn_Wk, L0_xattn_bk, L0_xattn_Wv, L0_xattn_bv, L0_xattn_Wo, L0_xattn_bo, L0_ffn_w, L0_ffn_input_scale, L0_ffn_weight_scale, L0_ffn_output_scale, L1_xattn_wq, L1_xattn_wk, L1_xattn_wv, L1_xattn_wo, L1_xattn_ln_w, L1_ffn_A, L1_ffn_B, L1_ffn_Wr, L1_ffn_br):
    import jax
    import jax.numpy as jnp

    def _L0_xattn_ref(qk, v, masks, Wq, bq, Wk, bk, Wv, bv, Wo, bo):
        import jax, jax.numpy as jnp
        import numpy as np
        W = 128
        H = 8
        D = 128
        DK = D // 2

        def _to_patches(x):
            b, d, s = x.shape
            np_ = s // W
            return x.reshape(b, d, np_, W).transpose(0, 2, 1, 3).reshape(b * np_, d, W)
        B, _, S = qk.shape
        np_ = S // W
        qp = _to_patches(qk)
        vp = _to_patches(v)
        mp = _to_patches(masks)
        q = jnp.einsum('ed,bdw->bew', Wq, qp) + bq[:, None]
        k = jnp.einsum('ed,bdw->bew', Wk, qp) + bk[:, None]
        val = jnp.einsum('ed,bdw->bew', Wv, vp) + bv[:, None]
        BN = q.shape[0]
        dh = DK // H
        qh = q.reshape(BN, H, dh, W)
        kh = k.reshape(BN, H, dh, W)
        vh = val.reshape(BN, H, dh, W)
        scores = jnp.einsum('bhdi,bhdj->bhij', qh, kh) / jnp.sqrt(jnp.asarray(dh, qh.dtype))
        scores = jnp.where(mp[:, :, None, :] > 0, scores, jnp.asarray(-1000000000.0, scores.dtype))
        attn = jax.nn.softmax(scores, axis=-1)
        o = jnp.einsum('bhij,bhdj->bhdi', attn, vh).reshape(BN, DK, W)
        o = jax.nn.gelu(o, approximate=False)
        out = jnp.einsum('de,bew->bdw', Wo, o) + bo[:, None]
        out = out.reshape(B, np_, D, W).transpose(0, 2, 1, 3).reshape(B, D, S)
        out = out * masks
        return out

    def _L0_ffn_ref(x, w, input_scale, weight_scale, output_scale):
        import jax, jax.numpy as jnp
        import numpy as np
        FP8_MAX = 448.0

        def quantize_fp8(x, scale):
            return jnp.clip(x / scale, -FP8_MAX, FP8_MAX).astype(jnp.float8_e4m3fn)
        out_dtype = x.dtype
        q_in = quantize_fp8(x, input_scale)
        q_w = quantize_fp8(w, weight_scale)
        a = q_in.astype(out_dtype) * input_scale
        b = q_w.astype(out_dtype) * weight_scale
        out = jnp.einsum('bsk,nk->bsn', a, b).astype(out_dtype)
        q_out = quantize_fp8(out, output_scale)
        out = q_out.astype(out_dtype) * output_scale
        return out

    def _L1_xattn_ref(hidden_states, encoder_hidden_states, wq, wk, wv, wo, ln_w):
        import jax, jax.numpy as jnp
        import numpy as np
        HIDDEN = 512
        N_HEADS = 32
        N_KV_HEADS = 8
        HEAD_DIM = HIDDEN // N_HEADS
        N_REP = N_HEADS // N_KV_HEADS
        EPS = 1e-05

        def _rmsnorm(x, w):
            xf = x.astype(jnp.float32)
            var = jnp.mean(xf * xf, axis=-1, keepdims=True)
            return (xf * jax.lax.rsqrt(var + EPS)).astype(x.dtype) * w
        B, Qlen, _ = hidden_states.shape
        _, Klen, _ = encoder_hidden_states.shape
        x = _rmsnorm(hidden_states, ln_w)
        q = jnp.einsum('bqd,hd->bqh', x, wq).reshape(B, Qlen, N_HEADS, HEAD_DIM)
        k = jnp.einsum('bkd,hd->bkh', encoder_hidden_states, wk).reshape(B, Klen, N_KV_HEADS, HEAD_DIM)
        v = jnp.einsum('bkd,hd->bkh', encoder_hidden_states, wv).reshape(B, Klen, N_KV_HEADS, HEAD_DIM)
        q = q.transpose(0, 2, 1, 3)
        k = k.transpose(0, 2, 1, 3)
        v = v.transpose(0, 2, 1, 3)
        k = jnp.repeat(k, N_REP, axis=1)
        v = jnp.repeat(v, N_REP, axis=1)
        scores = jnp.einsum('bhqd,bhkd->bhqk', q, k) / np.sqrt(HEAD_DIM).astype(np.float32)
        attn = jax.nn.softmax(scores.astype(jnp.float32), axis=-1).astype(q.dtype)
        out = jnp.einsum('bhqk,bhkd->bhqd', attn, v)
        out = out.transpose(0, 2, 1, 3).reshape(B, Qlen, HIDDEN)
        return jnp.einsum('bqh,dh->bqd', out, wo)

    def _L1_ffn_ref(x, A, B, Wr, br):
        import jax, jax.numpy as jnp
        import numpy as np
        ALPHA = 32
        R = 16
        SCALING = ALPHA / R
        H = A.shape[0]
        router_logits = jnp.einsum('bsd,hd->bsh', x, Wr) + br
        scores = H * jax.nn.softmax(router_logits, axis=-1)
        low = jnp.einsum('bsd,hrd->bshr', x, A)
        out = jnp.einsum('bshr,hor,bsh->bso', low, B, scores)
        return SCALING * out
    x = x + jnp.tanh(g_xattn[0]) * _L0_xattn_ref(_layernorm(x, axis=-1), ctx_4096, mask_Bx1x4096_ff1, L0_xattn_Wq, L0_xattn_bq, L0_xattn_Wk, L0_xattn_bk, L0_xattn_Wv, L0_xattn_bv, L0_xattn_Wo, L0_xattn_bo)
    x = x + jnp.tanh(g_ffn[0]) * _L0_ffn_ref(_layernorm(x, axis=-1), L0_ffn_w, L0_ffn_input_scale, L0_ffn_weight_scale, L0_ffn_output_scale)
    x = x + jnp.tanh(g_xattn[1]) * _L1_xattn_ref(_layernorm(x, axis=-1), ctx_4096, L1_xattn_wq, L1_xattn_wk, L1_xattn_wv, L1_xattn_wo, L1_xattn_ln_w)
    x = x + jnp.tanh(g_ffn[1]) * _L1_ffn_ref(_layernorm(x, axis=-1), L1_ffn_A, L1_ffn_B, L1_ffn_Wr, L1_ffn_br)
    return x

_drawn_inputs = setup_inputs


def setup_inputs(seed=0):
    import zlib

    import numpy as np

    out = dict(_drawn_inputs(seed))
    spreads = {'g_ffn': (-1.0, 0.6),
     'L0_xattn_bq': (0.0, 0.64),
     'L0_xattn_bk': (0.0, 0.8),
     'L0_xattn_bv': (0.0, 0.1),
     'L0_xattn_bo': (0.0, 0.1),
     'L1_xattn_ln_w': (1.0, 0.6),
     'L1_ffn_br': (0.0, 0.579)}
    factors = {'L1_xattn_wq': 7.965, 'L1_xattn_wk': 8.0}
    for name, (base, spread) in spreads.items():
        noise = np.random.default_rng([zlib.crc32(name.encode()), seed]).standard_normal(out[name].shape)
        drawn = base * np.exp(spread * noise) if base else spread * noise
        out[name] = jnp.asarray(drawn.astype(out[name].dtype))
    for name, factor in factors.items():
        out[name] = (out[name] * factor).astype(out[name].dtype)
    return out
```

```python
from contextlib import ExitStack

import concourse.bass as bass
from concourse import mybir
from concourse.alu_op_type import AluOpType as ALU

ACT = mybir.ActivationFunctionType
AX_X = mybir.AxisListType.X
F32 = mybir.dt.float32
BF16 = mybir.dt.bfloat16
I32 = mybir.dt.int32

P = 128
BATCH = 8
DM = 512
NCH = DM // P
WIN = DM // P
H0 = 8
DH0 = 8
E0 = H0 * DH0
KV = 8
REP = 4
DH1 = 16
HQ = KV * REP
EXPERTS = 8
RANK = 16
LOW = EXPERTS * RANK
EXPERT_GAIN = EXPERTS * 2.0
EPS = 1e-5
FP8_MAX = 448.0
FP8_LEAST = 2.0 ** -6
FP8_STEP = 1.5 * 2.0 ** 20
MASKED = 998244352.0

PAIRS = [(0, 0), (0, 1), (0, 2), (1, 0), (1, 1), (2, 0)]
ROWS0 = len(PAIRS) * DH0
ROWS1 = len(PAIRS) * DH1
ROW_MASK = 64
ROW_MAX = 96
assert ROWS0 <= ROW_MASK and ROWS1 <= ROW_MAX

LAG2 = 1
LAG3 = 2
TILES = 8
SLOTS = BATCH + LAG3
FIRST = 2 * LAG3


def flamingo_block(nc, t):
    with ExitStack() as ctx:
        def sb(name, shape, dt=F32):
            return ctx.enter_context(nc.sbuf_tensor(name, shape, dt))

        def bank(name):
            return ctx.enter_context(nc.psum_tensor(name, [P, DM], F32))

        def sem(name):
            return ctx.enter_context(nc.semaphore(name))

        ident = sb("ident", [P, P])
        identb = sb("identb", [P, P], BF16)
        wqk0 = sb("wqk0", [P, 2 * E0])
        wv0 = sb("wv0", [P, E0])
        wo0 = sb("wo0", [P, 2, P])
        cols = sb("cols", [P, 4 + NCH])
        BQK, BV, BO, QROW, LNW = 0, 1, 2, 3, 4
        row = sb("row", [P, 15])
        wf8 = sb("wf8", [P, NCH, DM])
        wf8q = sb("wf8q", [P, NCH, DM], BF16)
        wq1 = sb("wq1", [P, NCH, DM])
        wk1 = sb("wk1", [P, NCH, P])
        wv1 = sb("wv1", [P, NCH, P])
        wo1 = sb("wo1", [P, NCH, DM])
        wlow = sb("wlow", [P, NCH, LOW + EXPERTS])
        wup = sb("wup", [P, DM])
        gain = sb("gain", [P, 4])
        fac = sb("fac", [P, 8])
        INV_IN, INV_W, INV_OUT, F_OUT, G_OUT, G_UP, PROD = range(7)
        halfm = sb("halfm", [P, 1])

        xa = sb("xa", [P, 2, DM])
        ctxa = sb("ctxa", [P, 2, DM])
        maska = sb("maska", [P, 2, DM])
        keep = sb("keep", [P, DM])
        mrow = sb("mrow", [P, DM], BF16)
        st0 = sb("st0", [P, 6]); mv0 = sb("mv0", [P, 2]); rs0 = sb("rs0", [P, 2])
        xln0 = sb("xln0", [P, DM])
        qk = sb("qk", [P, DM]); qkr = sb("qkr", [P, DM])
        s0 = sb("s0", [P, 3, DM], BF16)
        Q0 = sb("Q0", [P, H0, DM], BF16)
        K0 = sb("K0", [P, H0, DM], BF16)
        V0 = sb("V0", [P, WIN, H0, DH0 + 1])
        nm0 = sb("nm0", [P, H0, WIN])
        nh0 = sb("nh0", [P, 2, H0, WIN], BF16)
        mt0 = sb("mt0", [2 * H0 * WIN, P], BF16)
        AT = sb("AT", [P, 4, DM])
        os0 = sb("os0", [P, DM]); rc0 = sb("rc0", [P, 16])
        on0 = sb("on0", [P, WIN, E0])
        G = sb("G", [P, 2, 2, P])
        xb = sb("xb", [P, 2, DM])
        maskb = sb("maskb", [P, 2, DM])
        ctxt = sb("ctxt", [P, 2, NCH, P])
        xr = sb("xr", [P, DM]); x1 = sb("x1", [P, DM])
        st1 = sb("st1", [P, 6]); mv1 = sb("mv1", [P, 2]); rs1 = sb("rs1", [P, 3])
        ya = sb("ya", [P, DM]); yc = sb("yc", [P, DM]); ye = sb("ye", [P, DM])
        ym = sb("ym", [P, DM]); yt = sb("yt", [P, DM]); yq = sb("yq", [P, DM], BF16)
        yqt = sb("yqt", [P, NCH, P], BF16)
        za = sb("za", [P, DM]); zc = sb("zc", [P, DM]); ze = sb("ze", [P, DM])
        zm = sb("zm", [P, DM]); zt = sb("zt", [P, DM]); zq = sb("zq", [P, DM])
        x2 = sb("x2", [P, 2, DM])
        st2 = sb("st2", [P, 6]); mv2 = sb("mv2", [P, 2]); rs2 = sb("rs2", [P, 8])
        xh = sb("xh", [P, DM]); xht = sb("xht", [P, NCH, P])
        s1q = sb("s1q", [P, 3, DM], BF16); q1r = sb("q1r", [P, DM])
        s1k = sb("s1k", [P, 3, P], BF16); k1r = sb("k1r", [P, P])
        Q1 = sb("Q1", [P, 2, KV, DM], BF16)
        K1 = sb("K1", [P, 2, KV, P], BF16)
        V1 = sb("V1", [P, 2, KV, DH1 + 1])
        nm1 = sb("nm1", [P, HQ]); nh1 = sb("nh1", [P, 2, HQ], BF16)
        mt1 = sb("mt1", [2 * HQ, P], BF16)
        os1 = sb("os1", [P, DM]); rc1 = sb("rc1", [P, 16])
        on1 = sb("on1", [P, KV, REP, DH1]); ont1 = sb("ont1", [P, NCH, P])
        x3 = sb("x3", [P, DM])
        st3 = sb("st3", [P, 6]); mv3 = sb("mv3", [P, 2]); rs3 = sb("rs3", [P, 2])
        xl = sb("xl", [P, DM]); xlt = sb("xlt", [P, NCH, P])
        lg = sb("lg", [P, EXPERTS]); nml = sb("nml", [P, 1]); el = sb("el", [P, EXPERTS])
        sl = sb("sl", [P, 1]); rl = sb("rl", [P, 1]); wl = sb("wl", [P, EXPERTS])
        ls = sb("ls", [P, LOW]); lst = sb("lst", [P, P])
        xo = sb("xo", [P, 2, DM])

        SC = [bank("SC0"), bank("SC1")]
        ST = [bank("ST0"), bank("ST1")]
        O = bank("O")
        PA, PB, PC = bank("PA"), bank("PB"), bank("PC")
        PAb = PA[:, :].bitcast(BF16)
        PBb = PB[:, :].bitcast(BF16)
        PCb = PC[:, :].bitcast(BF16)

        w_early = sem("w_early"); w_late = sem("w_late")
        zeroed = sem("zeroed"); gains_ok = sem("gains_ok"); fac_ok = sem("fac_ok")
        w8_step = sem("w8_step"); wq1_ok = sem("wq1_ok"); idb_ok = sem("idb_ok")
        sp_mark = sem("sp_mark"); pe_mark = sem("pe_mark"); dve_mark = sem("dve_mark"); pool_mark = sem("pool_mark")
        o_clear = sem("o_clear")
        names = """ld_xa ld_ctxa ld_maska st0 mv0 ve0 rs0 xln0 keep mrow mrow_in qk_mm qk qk_hi qk_r qk_mid
        qk_lo qk_out q0_in k0_in v0_mm v0 nm0 nh0 nl0 mt0_mm mt0 mt0_out mt0_in os0 ot0_mm rc0 on0
        ont0_mm gelu
        ld_xb ld_maskb ld_ctxt k1_hi k1_r k1_mid k1_lo k1_out k1_in v1_mm v1 y_mm xr x1 st1 mv1 ve1
        rs1 rsi1 ya yc ye ym yt yq yqt_mm yqt z_mm za zc ze zm zt zq x2 st2 mv2 rs2 xh xht_mm xht
        q1_mm q1_hi q1_r q1_mid q1_lo q1_out q1_in
        nm1 nh1 nl1 mt1_mm mt1 mt1_out mt1_in os1 ot1_mm rc1 on1 ont1_mm ont1 wo_mm x3 st3 mv3 ve3 rs3
        xl xlt_mm xlt lg_mm lg nml el rl wl ls ls_mm lst up_mm xo out
        sc_ready sc_read st_ready st_read pv_done o_read""".split()
        S = {n: sem("s_" + n) for n in names}

        d_qk = nc.dram_tensor("d_qk", [3, 2 * E0, DM], BF16, kind="Internal").ap()
        d_m0 = nc.dram_tensor("d_m0", [2, H0 * WIN * P], BF16, kind="Internal").ap()
        d_q1 = nc.dram_tensor("d_q1", [3, P, DM], BF16, kind="Internal").ap()
        d_k1 = nc.dram_tensor("d_k1", [3, P, P], BF16, kind="Internal").ap()
        d_m1 = nc.dram_tensor("d_m1", [2, HQ * P], BF16, kind="Internal").ap()

        def tiles_before(u):
            if isinstance(u, int):
                return TILES * min(u, BATCH) + TILES * min(max(u - LAG3, 0), BATCH)
            return u * (2 * TILES) - TILES * LAG3

        def tile_no(u, stage, tile):
            first = tiles_before(u) + tile
            if stage == 1 and not (isinstance(u, int) and u < LAG3):
                return first + TILES
            return first

        def at_least(eng, name, value):
            if not (isinstance(value, int) and value <= 0):
                eng.wait_ge(S[name], value)

        def stand(eng, mark):
            eng.sem_inc(mark, 1)

        def slots(eng, run):
            for u in range(FIRST):
                run(u, u % 2, True, u >= LAG2, u >= LAG3)
            with eng.Fori(0, (BATCH - FIRST) // 2) as i:
                for par in range(2):
                    run(i * 2 + (FIRST + par), par, True, True, True)
            for u in range(BATCH, SLOTS):
                run(u, u % 2, False, u - LAG2 < BATCH, True)

        block = ctx.enter_context(nc.Block())

        @block.sync
        def _(sp):
            early = [(wqk0, "wqk0"), (cols, "cols"), (wv0, "wv0"), (ident, "ident")]
            for dst, name in early:
                sp.dma_start(dst[:, :], t[name]).then_inc(w_early, 16)
            sp.dma_start(wo0[:, :, :], t["wo0"]).then_inc(w_early, 16)
            sp.dma_start(row[:, :], t["row"].partition_broadcast(P)).then_inc(w_early, 16)

            def after(name, value):
                if not (isinstance(value, int) and value <= 0):
                    sp.wait_ge(S[name], value)
                    sp.sem_inc(sp_mark, 1)

            def loads1(b, par):
                if not (isinstance(b, int) and b < 2):
                    after("xln0", b - 1)
                    after("v0_mm", b - 1)
                    after("keep", b - 1)
                sp.dma_start(xa[:, par, :], t["x"][b, :, :]).then_inc(S["ld_xa"], 16)
                sp.dma_start(ctxa[:, par, :], t["ctx"][b, :, :]).then_inc(S["ld_ctxa"], 16)
                sp.dma_start(maska[:, par, :], t["mask"][b, :].partition_broadcast(P))\
                    .then_inc(S["ld_maska"], 16)

            def loads2(b, par):
                if not (isinstance(b, int) and b < 2):
                    after("x1", b - 1)
                    after("xr", b - 1)
                    after("v1_mm", b - 1)
                sp.dma_start(ctxt[:, par, :, :], t["ctxt"][b, :, :, :]).then_inc(S["ld_ctxt"], 16)
                sp.dma_start(xb[:, par, :], t["x"][b, :, :]).then_inc(S["ld_xb"], 16)
                sp.dma_start(maskb[:, par, :], t["mask"][b, :].partition_broadcast(P))\
                    .then_inc(S["ld_maskb"], 16)

            def relay_qk0(b):
                after("qk_hi", b + 1)
                after("qk_mid", b + 1)
                after("qk_lo", b + 1)
                sp.dma_start(d_qk.rearrange("a r w -> r a w"), s0[:, :, :]).then_inc(S["qk_out"], 16)
                after("st_ready", tiles_before(b))
                after("qk_out", (b + 1) * 16)
                for c, (pq, pk) in enumerate(PAIRS):
                    r = slice(c * DH0, (c + 1) * DH0)
                    sp.dma_start(Q0[r, :, :], d_qk[pq, 0:E0, :].rearrange("(h d) w -> d h w", d=DH0))\
                        .then_inc(S["q0_in"], 16)
                    sp.dma_start(K0[r, :, :], d_qk[pk, E0:2 * E0, :].rearrange("(h d) w -> d h w", d=DH0))\
                        .then_inc(S["k0_in"], 16)
                after("mrow", b + 1)
                for h in range(H0):
                    sp.dma_start(K0[ROW_MASK:ROW_MASK + 1, h, :], mrow[E0:E0 + 1, :])\
                        .then_inc(S["mrow_in"], 16)

            def relay_m0(b):
                after("mt0", b + 1)
                sp.dma_start(d_m0.rearrange("a (r i) -> (a r) i", i=P), mt0[:, :]).then_inc(S["mt0_out"], 16)
                after("mt0_out", (b + 1) * 16)
                sp.dma_start(Q0[ROW_MAX:ROW_MAX + 2, :, :], d_m0.rearrange("a (h w) -> a h w", h=H0))\
                    .then_inc(S["mt0_in"], 16)

            def relay_k1(b, par):
                after("k1_hi", b + 1)
                after("k1_mid", b + 1)
                after("k1_lo", b + 1)
                sp.dma_start(d_k1.rearrange("a r w -> r a w"), s1k[:, :, :]).then_inc(S["k1_out"], 16)
                after("k1_out", (b + 1) * 16)
                for c, (_, pk) in enumerate(PAIRS):
                    sp.dma_start(K1[c * DH1:(c + 1) * DH1, par, :, :],
                                 d_k1[pk, :, :].rearrange("(k d) w -> d k w", d=DH1)).then_inc(S["k1_in"], 16)

            def relay_q1(b, par):
                after("q1_hi", b + 1)
                after("q1_mid", b + 1)
                after("q1_lo", b + 1)
                sp.dma_start(d_q1.rearrange("a r w -> r a w"), s1q[:, :, :]).then_inc(S["q1_out"], 16)
                after("q1_out", (b + 1) * 16)
                for c, (pq, _) in enumerate(PAIRS):
                    sp.dma_start(Q1[c * DH1:(c + 1) * DH1, par, :, :],
                                 d_q1[pq, :, :].rearrange("(k d) w -> d k w", d=DH1)).then_inc(S["q1_in"], 16)

            def relay_m1(b, par):
                after("mt1", b + 1)
                sp.dma_start(d_m1.rearrange("a (r i) -> (a r) i", i=P), mt1[:, :]).then_inc(S["mt1_out"], 16)
                after("mt1_out", (b + 1) * 16)
                sp.dma_start(Q1[ROW_MAX:ROW_MAX + 2, par, :, :], d_m1.rearrange("a (k w) -> a k w", k=KV))\
                    .then_inc(S["mt1_in"], 16)

            def store(b, par):
                after("xo", b + 1)
                sp.dma_start(t["out"][b, :, :], xo[:, par, :]).then_inc(S["out"], 16)

            def run(u, par, one, two, three):
                if one:
                    loads1(u, par)
                if two:
                    loads2(u - LAG2, 1 - par)
                if isinstance(u, int) and u == 0:
                    for dst, name in ((wk1, "wk1"), (wv1, "wv1"), (wf8, "wf8"), (wq1, "wq1"), (wo1, "wo1"),
                                      (wlow, "wlow")):
                        sp.dma_start(dst[:, :, :], t[name]).then_inc(w_late, 16)
                    sp.dma_start(wup[:, :], t["wup"]).then_inc(w_late, 16)
                    sp.wait_ge(zeroed, 8)
                if two:
                    relay_k1(u - LAG2, 1 - par)
                if one:
                    relay_qk0(u)
                if three:
                    relay_m1(u - LAG3, par)
                if one:
                    relay_m0(u)
                if two:
                    relay_q1(u - LAG2, 1 - par)
                if three:
                    store(u - LAG3, par)

            slots(sp, run)
            sp.wait_ge(S["out"], BATCH * 16)

        @block.tensor
        def _(pe):
            mm = pe.matmul

            def qk_mm(b, par):
                pe.wait_ge(S["xln0"], b + 1)
                if not (isinstance(b, int) and b < 1):
                    pe.wait_ge(S["gelu"], b)
                mm(PA[:, :], wqk0[:, :], xln0[:, :], start=True, stop=True).then_inc(S["qk_mm"], 1)

            def v0_mm(b, par):
                pe.wait_ge(S["ld_ctxa"], (b + 1) * 16)
                pe.wait_ge(S["qk"], b + 1)
                for w in range(WIN):
                    last = mm(PA[:, w * E0:(w + 1) * E0], ctxa[:, par, w * P:(w + 1) * P], wv0[:, :],
                              start=True, stop=True)
                last.then_inc(S["v0_mm"], 1)

            def k1_mm(b, par):
                pe.wait_ge(S["ld_ctxt"], (b + 1) * 16)
                if not (isinstance(b, int) and b < 1):
                    pe.wait_ge(S["q1_r"], b)
                for c in range(NCH):
                    last = mm(PB[:, 0:P], wk1[:, c, :], ctxt[:, par, c, :], start=c == 0, stop=c == NCH - 1)
                for c in range(NCH):
                    last = mm(PB[:, P:2 * P], ctxt[:, par, c, :], wv1[:, c, :], start=c == 0, stop=c == NCH - 1)
                last.then_inc(S["v1_mm"], 1)

            def sc0(u):
                pe.wait_ge(S["q0_in"], (u + 1) * 16 * len(PAIRS))
                pe.wait_ge(S["k0_in"], (u + 1) * 16 * len(PAIRS))
                pe.wait_ge(S["mrow_in"], (u + 1) * 16 * H0)
                for tile in range(TILES):
                    at_least(pe, "sc_read", tile_no(u, 1, tile) - 1)
                    w, h0 = tile // 2, tile % 2 * 4
                    for g in range(4):
                        last = mm(SC[tile % 2][:, g * P:(g + 1) * P], Q0[0:ROW_MAX, h0 + g, w * P:(w + 1) * P],
                                  K0[0:ROW_MAX, h0 + g, w * P:(w + 1) * P], start=True, stop=True)
                    last.then_inc(S["sc_ready"], 1)

            def sc1(u, b, par):
                pe.wait_ge(S["q1_in"], (b + 1) * 16 * len(PAIRS))
                pe.wait_ge(S["k1_in"], (b + 1) * 16 * len(PAIRS))
                for kv in range(KV):
                    at_least(pe, "sc_read", tile_no(u, 3, kv) - 1)
                    for r in range(REP):
                        last = mm(SC[kv % 2][:, r * P:(r + 1) * P], Q1[0:ROW_MAX, par, kv, r * P:(r + 1) * P],
                                  K1[0:ROW_MAX, par, kv, :], start=True, stop=True)
                    last.then_inc(S["sc_ready"], 1)

            def mt0_mm(b):
                pe.wait_ge(S["nl0"], b + 1)
                pe.wait_ge(S["v0"], b + 1)
                stand(pe, pe_mark)
                pe.transpose(PAb[0:2 * H0 * WIN, 0:P], nh0[:, :, :, :].rearrange("p a h w -> p (a h w)"),
                             identb[:, :]).then_inc(S["mt0_mm"], 1)

            def mt1_mm(b):
                pe.wait_ge(S["nl1"], b + 1)
                if not (isinstance(b, int) and b < 1):
                    pe.wait_ge(S["xo"], b)
                stand(pe, pe_mark)
                pe.transpose(PCb[0:2 * HQ, 0:P], nh1[:, :, :].rearrange("p a h -> p (a h)"),
                             identb[:, :]).then_inc(S["mt1_mm"], 1)

            def st0(u, tile):
                at_least(pe, "st_read", tile_no(u, 1, tile) - 1)
                w, h0 = tile // 2, tile % 2 * 4
                for g in range(4):
                    last = mm(ST[tile % 2][:, g * P:(g + 1) * P], K0[:, h0 + g, w * P:(w + 1) * P],
                              Q0[:, h0 + g, w * P:(w + 1) * P], start=True, stop=True)
                last.then_inc(S["st_ready"], 1)

            def pv0(u, tile):
                pe.wait_ge(S["st_read"], tile_no(u, 1, tile) + 1)
                if tile % 4 == 0:
                    at_least(pe, "o_read", half_no(u, 1, tile // 4))
                w, h0 = tile // 2, tile % 2 * 4
                for g in range(4):
                    last = mm(O[32 * g:32 * g + DH0 + 1, tile % 4 * P:(tile % 4 + 1) * P], V0[:, w, h0 + g, :],
                              AT[:, tile % 4, g * P:(g + 1) * P], start=True, stop=True)
                last.then_inc(S["pv_done"], 1)

            def half_no(u, stage, half):
                n = tiles_before(u)
                n = n // 4 if isinstance(n, int) else u * (TILES // 2) - (TILES // 4) * LAG3
                if stage == 1 and not (isinstance(u, int) and u < LAG3):
                    n = n + TILES // 4
                return n + half

            def ot0_mm(b, half):
                pe.wait_ge(S["os0"], b * 2 + (half + 1))
                if half == 0:
                    pe.wait_ge(S["mt0"], b + 1)
                else:
                    pe.wait_ge(S["on0"], b * 2 + 1)
                for k in range(4):
                    last = pe.transpose(PA[:, k * P:(k + 1) * P], os0[:, k * P:(k + 1) * P], ident[:, :])
                last.then_inc(S["ot0_mm"], 1)

            def attend0(u):
                pe.wait_ge(S["mt0_in"], (u + 1) * 16)
                st0(u, 0)
                for tile in range(TILES):
                    if tile + 1 < TILES:
                        st0(u, tile + 1)
                    pv0(u, tile)
                    if tile == 5:
                        ot0_mm(u, 0)
                ot0_mm(u, 1)

            def ont0_mm(b):
                pe.wait_ge(S["on0"], b * 2 + 2)
                for k in range(2):
                    last = pe.transpose(PA[:, k * P:(k + 1) * P],
                                        on0[:, 2 * k:2 * k + 2, :].rearrange("p w e -> p (w e)"), ident[:, :])
                last.then_inc(S["ont0_mm"], 1)

            def st1(u, par, kv):
                at_least(pe, "st_read", tile_no(u, 3, kv) - 1)
                mm(ST[kv % 2][:, :], K1[:, par, kv, :], Q1[:, par, kv, :], start=True, stop=True)\
                    .then_inc(S["st_ready"], 1)

            def pv1(u, par, kv):
                pe.wait_ge(S["st_read"], tile_no(u, 3, kv) + 1)
                if kv % 4 == 0:
                    at_least(pe, "o_read", half_no(u, 3, kv // 4))
                g = kv % 4
                mm(O[32 * g:32 * g + DH1 + 1, :], V1[:, par, kv, :], AT[:, kv % 4, :],
                   start=True, stop=True).then_inc(S["pv_done"], 1)

            def ot1_mm(b, half):
                pe.wait_ge(S["os1"], b * 2 + (half + 1))
                if half == 0:
                    pe.wait_ge(S["mt1"], b + 1)
                else:
                    pe.wait_ge(S["on1"], b * 2 + 1)
                for r in range(REP):
                    last = pe.transpose(PC[:, r * P:(r + 1) * P], os1[:, r * P:(r + 1) * P], ident[:, :])
                last.then_inc(S["ot1_mm"], 1)

            def attend1(u, b, par):
                pe.wait_ge(S["mt1_in"], (b + 1) * 16)
                pe.wait_ge(S["v1"], b + 1)
                st1(u, par, 0)
                for kv in range(KV):
                    if kv + 1 < KV:
                        st1(u, par, kv + 1)
                    pv1(u, par, kv)
                    if kv == 5:
                        ot1_mm(b, 0)
                ot1_mm(b, 1)

            def y_mm(b, par):
                pe.wait_ge(S["gelu"], b + 1)
                pe.wait_ge(S["v1"], b + 1)
                pe.wait_ge(S["k1_r"], b + 1)
                out = PB[:, :].rearrange("p (a o i) -> p a o i", a=2, o=2)
                for o in range(2):
                    last = mm(out[:, :, o, :], wo0[:, o, :], G[:, par, :, :],
                              start=True, stop=True)
                last.then_inc(S["y_mm"], 1)

            def yqt_mm(b):
                pe.wait_ge(S["yq"], b + 1)
                for c in range(NCH):
                    last = pe.transpose(PBb[:, c * P:(c + 1) * P], yq[:, c * P:(c + 1) * P], identb[:, :])
                last.then_inc(S["yqt_mm"], 1)

            def z_mm(b):
                pe.wait_ge(S["yqt"], b + 1)
                for c in range(NCH):
                    last = mm(PB[:, :], yqt[:, c, :], wf8q[:, c, :], start=c == 0, stop=c == NCH - 1)
                last.then_inc(S["z_mm"], 1)

            def xht_mm(b):
                pe.wait_ge(S["xh"], b + 1)
                pe.wait_ge(S["za"], b + 1)
                for c in range(NCH):
                    last = pe.transpose(PB[:, c * P:(c + 1) * P], xh[:, c * P:(c + 1) * P], ident[:, :])
                last.then_inc(S["xht_mm"], 1)

            def q1_mm(b):
                pe.wait_ge(S["xht"], b + 1)
                for r in range(REP):
                    for c in range(NCH):
                        last = mm(PB[:, r * P:(r + 1) * P], wq1[:, c, r * P:(r + 1) * P], xht[:, c, :],
                                  start=c == 0, stop=c == NCH - 1)
                last.then_inc(S["q1_mm"], 1)

            def ont1_mm(b):
                pe.wait_ge(S["on1"], b * 2 + 2)
                flat = on1[:, :, :, :].rearrange("p k r d -> p (k r d)")
                for c in range(NCH):
                    last = pe.transpose(PC[:, c * P:(c + 1) * P], flat[:, c * P:(c + 1) * P], ident[:, :])
                last.then_inc(S["ont1_mm"], 1)

            def wo_mm(b):
                pe.wait_ge(S["ont1"], b + 1)
                for c in range(NCH):
                    last = mm(PC[:, :], ont1[:, c, :], wo1[:, c, :], start=c == 0, stop=c == NCH - 1)
                last.then_inc(S["wo_mm"], 1)

            def xlt_mm(b):
                pe.wait_ge(S["xl"], b + 1)
                for c in range(NCH):
                    last = pe.transpose(PC[:, c * P:(c + 1) * P], xl[:, c * P:(c + 1) * P], ident[:, :])
                last.then_inc(S["xlt_mm"], 1)

            def lg_mm(b):
                pe.wait_ge(S["xlt"], b + 1)
                for c in range(NCH):
                    last = mm(PC[:, 0:LOW + EXPERTS], xlt[:, c, :], wlow[:, c, :], start=c == 0, stop=c == NCH - 1)
                last.then_inc(S["lg_mm"], 1)

            def up_mm(b):
                pe.wait_ge(S["ls"], b + 1)
                pe.transpose(PC[:, 0:P], ls[:, :], ident[:, :]).then_inc(S["ls_mm"], 1)
                pe.wait_ge(S["lst"], b + 1)
                mm(PC[:, :], lst[:, :], wup[:, :], start=True, stop=True).then_inc(S["up_mm"], 1)

            pe.wait_ge(w_early, 16 * 6)
            pe.wait_ge(o_clear, 1)
            pe.wait_ge(idb_ok, 1)

            def run(u, par, one, two, three):
                b2, b3 = u - LAG2, u - LAG3
                if isinstance(u, int) and u == LAG2:
                    pe.wait_ge(w_late, 16 * 7)
                    pe.wait_ge(wq1_ok, 1)
                    pe.wait_ge(w8_step, 6)
                if one:
                    qk_mm(u, par)
                    v0_mm(u, par)
                if two:
                    k1_mm(b2, 1 - par)
                if three:
                    sc1(u, b3, par)
                if two:
                    y_mm(b2, 1 - par)
                if three:
                    mt1_mm(b3)
                if one:
                    sc0(u)
                if two:
                    yqt_mm(b2)
                    z_mm(b2)
                if one:
                    mt0_mm(u)
                if three:
                    attend1(u, b3, par)
                    ont1_mm(b3)
                    wo_mm(b3)
                if two:
                    xht_mm(b2)
                    q1_mm(b2)
                if one:
                    attend0(u)
                    ont0_mm(u)
                if three:
                    xlt_mm(b3)
                    lg_mm(b3)
                    up_mm(b3)

            slots(pe, run)

        @block.scalar
        def _(act):
            act.wait_ge(w_early, 16 * 6)
            act.activation(gain[:, :], row[:, 0:4], ACT.Tanh).then_inc(gains_ok, 1)

            def qk_parts(b):
                act.wait_ge(S["qk"], b + 1)
                if not (isinstance(b, int) and b < 1):
                    act.wait_ge(S["qk_out"], b * 16)
                act.activation(s0[:, 0, :], qk[:, :], ACT.Copy).then_inc(S["qk_hi"], 1)
                act.wait_ge(S["qk_r"], b + 1)
                act.activation(s0[:, 1, :], qkr[:, :], ACT.Copy).then_inc(S["qk_mid"], 1)

            def v0(b):
                act.wait_ge(S["v0_mm"], b + 1)
                if not (isinstance(b, int) and b < 1):
                    act.wait_ge(S["os0"], b * 2)
                act.activation(V0[:, :, :, 0:DH0],
                               PA[:, 0:WIN * E0].rearrange("p (w h d) -> p w h d", w=WIN, h=H0),
                               ACT.Copy).then_inc(S["v0"], 1)

            def kv1(b, par):
                act.wait_ge(S["v1_mm"], b + 1)
                if not (isinstance(b, int) and b < 1):
                    act.wait_ge(S["k1_out"], b * 16)
                act.activation(s1k[:, 0, :], PB[:, 0:P], ACT.Copy).then_inc(S["k1_hi"], 1)
                act.activation(V1[:, par, :, 0:DH1], PB[:, P:2 * P].rearrange("p (k d) -> p k d", k=KV),
                               ACT.Copy).then_inc(S["v1"], 1)
                act.wait_ge(S["k1_r"], b + 1)
                act.activation(s1k[:, 1, :], k1r[:, :], ACT.Copy).then_inc(S["k1_mid"], 1)

            def mt0_copy(b):
                act.wait_ge(S["mt0_mm"], b + 1)
                if not (isinstance(b, int) and b < 1):
                    act.wait_ge(S["mt0_out"], b * 16)
                act.activation(mt0[:, :], PAb[0:2 * H0 * WIN, 0:P], ACT.Copy).then_inc(S["mt0"], 1)

            def mt1_copy(b):
                act.wait_ge(S["mt1_mm"], b + 1)
                if not (isinstance(b, int) and b < 1):
                    act.wait_ge(S["mt1_out"], b * 16)
                act.activation(mt1[:, :], PCb[0:2 * HQ, 0:P], ACT.Copy).then_inc(S["mt1"], 1)

            def exps(u, stage, dh):
                for tile in range(TILES):
                    n = tile_no(u, stage, tile)
                    act.wait_ge(S["st_ready"], n + 1)
                    at_least(act, "pv_done", n - 3)
                    act.activation(AT[:, tile % 4, :], ST[tile % 2][:, :], ACT.Exp, scale=float(dh) ** -0.5)\
                        .then_inc(S["st_read"], 1)
                    if tile == 5:
                        out_copy(u, stage, 0)
                out_copy(u, stage, 1)

            def out_copy(u, stage, half):
                n = tile_no(u, stage, 4 * half + 4)
                act.wait_ge(S["pv_done"], n)
                b = u if stage == 1 else u - LAG3
                dst, done, read = (os0, "os0", "ot0_mm") if stage == 1 else (os1, "os1", "ot1_mm")
                if not (isinstance(b, int) and b == 0 and half == 0):
                    act.wait_ge(S[read], b * 2 + half)
                act.activation(dst[:, :], O[:, :], ACT.Copy).then_inc(S[done], 1)
                act.wait_ge(S[done], b * 2 + (half + 1))
                act.sem_inc(S["o_read"], 1)

            def gelu(b, par):
                act.wait_ge(S["ont0_mm"], b + 1)
                if not (isinstance(b, int) and b < 2):
                    act.wait_ge(S["y_mm"], b - 1)
                act.activation(G[:, par, :, :], PA[:, 0:2 * P].rearrange("p (a i) -> p a i", a=2), ACT.Gelu,
                               bias=cols[:, BV:BV + 1]).then_inc(S["gelu"], 1)

            def yqt_copy(b):
                act.wait_ge(S["yqt_mm"], b + 1)
                act.activation(yqt[:, :, :], PBb[:, 0:DM].rearrange("p (c i) -> p c i", c=NCH), ACT.Copy)\
                    .then_inc(S["yqt"], 1)

            def za_copy(b):
                act.wait_ge(S["z_mm"], b + 1)
                act.activation(za[:, :], PB[:, :], ACT.Copy, scale=fac[:, F_OUT:F_OUT + 1]).then_inc(S["za"], 1)

            def xht_copy(b):
                act.wait_ge(S["xht_mm"], b + 1)
                act.activation(xht[:, :, :], PB[:, :].rearrange("p (c i) -> p c i", c=NCH), ACT.Copy)\
                    .then_inc(S["xht"], 1)

            def q1_parts(b):
                act.wait_ge(S["q1_mm"], b + 1)
                if not (isinstance(b, int) and b < 1):
                    act.wait_ge(S["q1_out"], b * 16)
                act.activation(s1q[:, 0, :], PB[:, :], ACT.Copy).then_inc(S["q1_hi"], 1)
                act.wait_ge(S["q1_r"], b + 1)
                act.activation(s1q[:, 1, :], q1r[:, :], ACT.Copy).then_inc(S["q1_mid"], 1)

            def ont1_copy(b):
                act.wait_ge(S["ont1_mm"], b + 1)
                act.activation(ont1[:, :, :], PC[:, :].rearrange("p (c i) -> p c i", c=NCH), ACT.Copy)\
                    .then_inc(S["ont1"], 1)

            def xlt_copy(b):
                act.wait_ge(S["xlt_mm"], b + 1)
                act.activation(xlt[:, :, :], PC[:, :].rearrange("p (c i) -> p c i", c=NCH), ACT.Copy)\
                    .then_inc(S["xlt"], 1)

            def router_exp(b):
                act.wait_ge(S["nml"], b + 1)
                act.activation(el[:, :], lg[:, :], ACT.Exp, bias=nml[:, 0:1], accum_out=sl[:, 0:1])\
                    .then_inc(S["el"], 1)

            def lst_copy(b):
                act.wait_ge(S["ls_mm"], b + 1)
                act.activation(lst[:, :], PC[:, 0:P], ACT.Copy).then_inc(S["lst"], 1)

            act.wait_ge(fac_ok, 7)

            def run(u, par, one, two, three):
                b2, b3 = u - LAG2, u - LAG3
                if one:
                    qk_parts(u)
                    v0(u)
                if two:
                    kv1(b2, 1 - par)
                if three:
                    mt1_copy(b3)
                if two:
                    yqt_copy(b2)
                if one:
                    mt0_copy(u)
                if two:
                    za_copy(b2)
                if three:
                    exps(u, 3, DH1)
                    ont1_copy(b3)
                if two:
                    xht_copy(b2)
                    q1_parts(b2)
                if one:
                    exps(u, 1, DH0)
                if three:
                    xlt_copy(b3)
                    router_exp(b3)
                    lst_copy(b3)
                if one:
                    gelu(u, par)

            slots(act, run)

        @block.vector
        def _(dve):
            dve.memset(O[:, :], 0.0).then_inc(o_clear, 1)
            dve.wait_ge(w_early, 16 * 6)
            dve.tensor_copy(identb[:, :], ident[:, :]).then_inc(idb_ok, 1)
            for k, s in ((INV_IN, 4), (INV_W, 5), (INV_OUT, 6)):
                dve.reciprocal(fac[:, k:k + 1], row[:, s:s + 1]).then_inc(fac_ok, 1)
            dve.tensor_tensor(fac[:, PROD:PROD + 1], row[:, 4:5], row[:, 5:6], ALU.mult).then_inc(fac_ok, 1)
            dve.wait_ge(fac_ok, 4)
            dve.wait_ge(gains_ok, 1)
            dve.tensor_tensor(fac[:, F_OUT:F_OUT + 1], fac[:, PROD:PROD + 1], fac[:, INV_OUT:INV_OUT + 1],
                              ALU.mult).then_inc(fac_ok, 1)
            dve.tensor_tensor(fac[:, G_OUT:G_OUT + 1], gain[:, 2:3], row[:, 6:7], ALU.mult).then_inc(fac_ok, 1)
            dve.tensor_scalar(fac[:, G_UP:G_UP + 1], gain[:, 3:4], EXPERT_GAIN, None, ALU.mult).then_inc(fac_ok, 1)
            dve.wait_ge(fac_ok, 7)

            def binade(dst, src):
                return dve.tensor_scalar(dst.bitcast(I32), src.bitcast(I32), 0x7F800000, None, ALU.bitwise_and)

            def rounder(dst, src):
                return dve.tensor_scalar(dst, src, FP8_LEAST, FP8_STEP, ALU.max, ALU.mult)

            def stats(x, st, mv, s_st, s_mv, b):
                dve.bn_stats(st[:, :], x).then_inc(S[s_st], 1)
                dve.wait_ge(S[s_st], b + 1)
                stand(dve, dve_mark)
                dve.bn_aggr(mv[:, :], st[:, :]).then_inc(S[s_mv], 1)

            def ln0(b, par):
                dve.wait_ge(S["ld_xa"], (b + 1) * 16)
                stats(xa[:, par, :], st0, mv0, "st0", "mv0", b)
                dve.wait_ge(S["rs0"], b + 1)
                if not (isinstance(b, int) and b < 1):
                    dve.wait_ge(S["qk_mm"], b)
                dve.tensor_scalar(xln0[:, :], xa[:, par, :], mv0[:, 0:1], rs0[:, 1:2], ALU.subtract, ALU.mult)\
                    .then_inc(S["xln0"], 1)

            def qk_bias(b):
                dve.wait_ge(S["qk_mm"], b + 1)
                dve.wait_ge(S["keep"], b + 1)
                if not (isinstance(b, int) and b < 1):
                    dve.wait_ge(S["qk_r"], b)
                dve.scalar_tensor_tensor(out=qk[:, :], in0=PA[:, :], scalar=cols[:, BQK:BQK + 1], in1=keep[:, :],
                                         op0=ALU.add, op1=ALU.mult).then_inc(S["qk"], 1)

            def maxima(u, stage):
                for tile in range(TILES):
                    dve.wait_ge(S["sc_ready"], tile_no(u, stage, tile) + 1)
                    if stage == 1:
                        w, h0 = tile // 2, tile % 2 * 4
                        dst = nm0[:, h0:h0 + 4, w]
                    else:
                        dst = nm1[:, tile * REP:(tile + 1) * REP]
                    dve.tensor_reduce(dst, SC[tile % 2][:, :].rearrange("p (g j) -> p g j", g=4), AX_X, ALU.max,
                                      negate=True).then_inc(S["sc_read"], 1)

            def minus_max(u, b, stage):
                nm, nh, mt, hi, lo = (nm0, nh0, "mt0_mm", "nh0", "nl0") if stage == 1 else \
                    (nm1, nh1, "mt1_mm", "nh1", "nl1")
                dve.wait_ge(S["sc_read"], tile_no(u, stage, TILES))
                if not (isinstance(b, int) and b < 1):
                    dve.wait_ge(S[mt], b)
                if stage == 1:
                    src, h, l = nm[:, :, :], nh[:, 0, :, :], nh[:, 1, :, :]
                else:
                    src, h, l = nm[:, :], nh[:, 0, :], nh[:, 1, :]
                dve.tensor_copy(h, src).then_inc(S[hi], 1)
                dve.wait_ge(S[hi], b + 1)
                dve.tensor_tensor(l, src, h, ALU.subtract).then_inc(S[lo], 1)

            def norm0(b, half):
                dve.wait_ge(S["ot0_mm"], b * 2 + (half + 1))
                if half == 0 and not (isinstance(b, int) and b < 1):
                    dve.wait_ge(S["ont0_mm"], b)
                src = PA[:, :].rearrange("p (w h d) -> p w h d", w=2, h=H0)
                rc = rc0[:, :].rearrange("p (w h) -> p w h", w=2)
                dve.reciprocal(rc, src[:, :, :, DH0]).then_inc(S["rc0"], 1)
                dve.wait_ge(S["rc0"], b * 2 + (half + 1))
                dve.tensor_tensor(on0[:, 2 * half:2 * half + 2, :].rearrange("p w (h d) -> p w h d", h=H0),
                                  src[:, :, :, 0:DH0],
                                  rc.unsqueeze(3).to_broadcast([P, 2, H0, DH0]), ALU.mult)\
                    .then_inc(S["on0"], 1)

            def norm1(b, half):
                dve.wait_ge(S["ot1_mm"], b * 2 + (half + 1))
                if half == 0 and not (isinstance(b, int) and b < 1):
                    dve.wait_ge(S["ont1_mm"], b)
                src = PC[:, :].rearrange("p (r g d) -> p g r d", r=REP, g=4)
                rc = rc1[:, :].rearrange("p (g r) -> p g r", g=4)
                dve.reciprocal(rc, src[:, :, :, DH1]).then_inc(S["rc1"], 1)
                dve.wait_ge(S["rc1"], b * 2 + (half + 1))
                dve.tensor_tensor(on1[:, 4 * half:4 * half + 4, :, :], src[:, :, :, 0:DH1],
                                  rc.unsqueeze(3).to_broadcast([P, 4, REP, DH1]), ALU.mult)\
                    .then_inc(S["on1"], 1)

            def k1_rest(b):
                dve.wait_ge(S["k1_hi"], b + 1)
                dve.wait_ge(S["v1"], b + 1)
                if not (isinstance(b, int) and b < 1):
                    dve.wait_ge(S["k1_lo"], b)
                dve.tensor_tensor(k1r[:, :], PB[:, 0:P], s1k[:, 0, :], ALU.subtract).then_inc(S["k1_r"], 1)

            def add_attention0(b, par):
                dve.wait_ge(S["y_mm"], b + 1)
                dve.wait_ge(S["ld_maskb"], (b + 1) * 16)
                dve.scalar_tensor_tensor(out=xr[:, :], in0=PB[:, :], scalar=cols[:, BO:BO + 1],
                                         in1=maskb[:, par, :], op0=ALU.add, op1=ALU.mult).then_inc(S["xr"], 1)
                dve.wait_ge(S["xr"], b + 1)
                dve.wait_ge(S["ld_xb"], (b + 1) * 16)
                dve.scalar_tensor_tensor(out=x1[:, :], in0=xr[:, :], scalar=gain[:, 0:1], in1=xb[:, par, :],
                                         op0=ALU.mult, op1=ALU.add).then_inc(S["x1"], 1)
                dve.wait_ge(S["x1"], b + 1)
                stats(x1[:, :], st1, mv1, "st1", "mv1", b)
                dve.wait_ge(S["rsi1"], b + 1)
                if not (isinstance(b, int) and b < 1):
                    dve.wait_ge(S["yt"], b)
                dve.tensor_scalar(ya[:, :], x1[:, :], mv1[:, 0:1], rs1[:, 2:3], ALU.subtract, ALU.mult)\
                    .then_inc(S["ya"], 1)

            def quant_in(b):
                dve.wait_ge(S["yc"], b + 1)
                if not (isinstance(b, int) and b < 1):
                    dve.wait_ge(S["yq"], b)
                binade(ye[:, :], yc[:, :]).then_inc(S["ye"], 1)
                dve.wait_ge(S["ye"], b + 1)
                rounder(ym[:, :], ye[:, :]).then_inc(S["ym"], 1)

            def quant_out(b):
                dve.wait_ge(S["zc"], b + 1)
                if not (isinstance(b, int) and b < 1):
                    dve.wait_ge(S["zq"], b)
                binade(ze[:, :], zc[:, :]).then_inc(S["ze"], 1)
                dve.wait_ge(S["ze"], b + 1)
                rounder(zm[:, :], ze[:, :]).then_inc(S["zm"], 1)

            def add_ffn0(b, par):
                dve.wait_ge(S["zq"], b + 1)
                if not (isinstance(b, int) and b < 2):
                    dve.wait_ge(S["x3"], b - 1)
                dve.scalar_tensor_tensor(out=x2[:, par, :], in0=zq[:, :], scalar=fac[:, G_OUT:G_OUT + 1],
                                         in1=x1[:, :], op0=ALU.mult, op1=ALU.add).then_inc(S["x2"], 1)
                dve.wait_ge(S["x2"], b + 1)
                stats(x2[:, par, :], st2, mv2, "st2", "mv2", b)
                dve.wait_ge(S["rs2"], b * 7 + 7)
                if not (isinstance(b, int) and b < 1):
                    dve.wait_ge(S["xht_mm"], b)
                dve.tensor_scalar(xh[:, :], x2[:, par, :], mv2[:, 0:1], rs2[:, 6:7], ALU.subtract, ALU.mult)\
                    .then_inc(S["xh"], 1)

            def q1_rest(b):
                dve.wait_ge(S["q1_hi"], b + 1)
                if not (isinstance(b, int) and b < 1):
                    dve.wait_ge(S["q1_lo"], b)
                dve.tensor_tensor(q1r[:, :], PB[:, :], s1q[:, 0, :], ALU.subtract).then_inc(S["q1_r"], 1)

            def add_attention1(b, par):
                dve.wait_ge(S["wo_mm"], b + 1)
                dve.scalar_tensor_tensor(out=x3[:, :], in0=PC[:, :], scalar=gain[:, 1:2], in1=x2[:, par, :],
                                         op0=ALU.mult, op1=ALU.add).then_inc(S["x3"], 1)
                dve.wait_ge(S["x3"], b + 1)
                stats(x3[:, :], st3, mv3, "st3", "mv3", b)
                dve.wait_ge(S["rs3"], b + 1)
                if not (isinstance(b, int) and b < 1):
                    dve.wait_ge(S["xlt_mm"], b)
                dve.tensor_scalar(xl[:, :], x3[:, :], mv3[:, 0:1], rs3[:, 1:2], ALU.subtract, ALU.mult)\
                    .then_inc(S["xl"], 1)

            def router(b):
                dve.wait_ge(S["lg_mm"], b + 1)
                if not (isinstance(b, int) and b < 1):
                    dve.wait_ge(S["el"], b)
                dve.tensor_tensor(lg[:, :], PC[:, LOW:LOW + EXPERTS], row[:, 7:15], ALU.add).then_inc(S["lg"], 1)
                dve.wait_ge(S["lg"], b + 1)
                dve.tensor_reduce(nml[:, :], lg[:, :], AX_X, ALU.max, negate=True).then_inc(S["nml"], 1)
                dve.wait_ge(S["el"], b + 1)
                dve.reciprocal(rl[:, :], sl[:, :]).then_inc(S["rl"], 1)
                dve.wait_ge(S["rl"], b + 1)
                dve.tensor_scalar(wl[:, :], el[:, :], rl[:, 0:1], None, ALU.mult).then_inc(S["wl"], 1)
                dve.wait_ge(S["wl"], b + 1)
                if not (isinstance(b, int) and b < 1):
                    dve.wait_ge(S["ls_mm"], b)
                dve.tensor_tensor(ls[:, :].rearrange("p (e r) -> p e r", e=EXPERTS),
                                  PC[:, 0:LOW].rearrange("p (e r) -> p e r", e=EXPERTS),
                                  wl[:, :].unsqueeze(2).to_broadcast([P, EXPERTS, RANK]), ALU.mult)\
                    .then_inc(S["ls"], 1)

            def add_ffn1(b, par):
                dve.wait_ge(S["up_mm"], b + 1)
                if not (isinstance(b, int) and b < 2):
                    dve.wait_ge(S["out"], b * 16 - 16)
                dve.scalar_tensor_tensor(out=xo[:, par, :], in0=PC[:, :], scalar=fac[:, G_UP:G_UP + 1],
                                         in1=x3[:, :], op0=ALU.mult, op1=ALU.add).then_inc(S["xo"], 1)

            def weights():
                dve.wait_ge(w_late, 16 * 7)
                for c in range(NCH):
                    last = dve.tensor_scalar(wq1[:, c, :], wq1[:, c, :], cols[:, LNW + c:LNW + c + 1], None, ALU.mult)
                last.then_inc(wq1_ok, 1)
                w = wf8[:, :, :].rearrange("p c n -> p (c n)")
                dve.tensor_scalar(w, w, fac[:, INV_W:INV_W + 1], FP8_MAX, ALU.mult, ALU.min).then_inc(w8_step, 1)
                dve.wait_ge(w8_step, 1)
                dve.tensor_scalar(w, w, -FP8_MAX, None, ALU.max).then_inc(w8_step, 1)
                dve.wait_ge(w8_step, 2)
                big = Q1[:, :, :, :].rearrange("p a k n -> p (a k n)").bitcast(F32)
                e, m = big[:, 0:NCH * DM], big[:, NCH * DM:2 * NCH * DM]
                binade(e, w).then_inc(w8_step, 1)
                dve.wait_ge(w8_step, 3)
                rounder(m, e).then_inc(w8_step, 1)
                dve.wait_ge(w8_step, 4)
                dve.tensor_tensor(w, w, m, ALU.add).then_inc(w8_step, 1)
                dve.wait_ge(w8_step, 5)
                dve.tensor_tensor(wf8q[:, :, :].rearrange("p c n -> p (c n)"), w, m, ALU.subtract)\
                    .then_inc(w8_step, 1)
                dve.wait_ge(w8_step, 6)
                dve.memset(Q1[ROW_MAX:P, :, :, :], 0.0).then_inc(w8_step, 1)

            def run(u, par, one, two, three):
                b2, b3 = u - LAG2, u - LAG3
                if one:
                    ln0(u, par)
                    qk_bias(u)
                if isinstance(u, int) and u == 0:
                    weights()
                if two:
                    k1_rest(b2)
                if three:
                    maxima(u, 3)
                    minus_max(u, b3, 3)
                if two:
                    add_attention0(b2, 1 - par)
                if one:
                    maxima(u, 1)
                    minus_max(u, u, 1)
                if two:
                    quant_in(b2)
                    quant_out(b2)
                if three:
                    norm1(b3, 0)
                if two:
                    add_ffn0(b2, 1 - par)
                if three:
                    norm1(b3, 1)
                    add_attention1(b3, par)
                if two:
                    q1_rest(b2)
                if one:
                    norm0(u, 0)
                    norm0(u, 1)
                if three:
                    router(b3)
                    add_ffn1(b3, par)

            slots(dve, run)

        @block.gpsimd
        def _(pool):
            fills = [(Q0[:, :, :], 0.0), (K0[:, :, :], 0.0), (V0[:, :, :, DH0:DH0 + 1], 1.0),
                     (V1[:, :, :, DH1:DH1 + 1], 1.0), (halfm[:, :], -0.5), (K1[ROW_MAX:P, :, :, :], 1.0),
                     (Q0[ROW_MASK:ROW_MAX, :, :], 1.0), (K0[ROW_MAX:P, :, :], 1.0)]
            for n, (part, value) in enumerate(fills):
                if n:
                    pool.wait_ge(zeroed, n)
                pool.memset(part, value).then_inc(zeroed, 1)
            pool.wait_ge(zeroed, len(fills))
            pool.wait_ge(w_early, 16 * 6)

            def rsqrt(dst, mid, var, s_mid, s_dst, b):
                pool.wait_ge(S[s_mid.replace("ve", "mv")], b + 1)
                stand(pool, pool_mark)
                pool.tensor_scalar(mid, var, EPS, None, ALU.add).then_inc(S[s_mid], 1)
                pool.wait_ge(S[s_mid], b + 1)
                pool.tensor_tensor(dst, mid, halfm[:, :], ALU.pow).then_inc(S[s_dst], 1)

            def keep_rows(b, par):
                pool.wait_ge(S["ld_maska"], (b + 1) * 16)
                if not (isinstance(b, int) and b < 1):
                    pool.wait_ge(S["qk"], b)
                    pool.wait_ge(S["mrow_in"], b * 16 * H0)
                stand(pool, pool_mark)
                pool.tensor_scalar(keep[:, :], maska[:, par, :], 0.0, cols[:, QROW:QROW + 1], ALU.is_gt, ALU.max)\
                    .then_inc(S["keep"], 1)
                pool.wait_ge(S["keep"], b + 1)
                stand(pool, pool_mark)
                pool.tensor_scalar(mrow[:, :], keep[:, :], -1.0, MASKED, ALU.add, ALU.mult).then_inc(S["mrow"], 1)

            def qk_rest(b):
                pool.wait_ge(S["qk_hi"], b + 1)
                if not (isinstance(b, int) and b < 1):
                    pool.wait_ge(S["qk_mid"], b)
                pool.tensor_tensor(qkr[:, :], qk[:, :], s0[:, 0, :], ALU.subtract).then_inc(S["qk_r"], 1)
                pool.wait_ge(S["qk_mid"], b + 1)
                pool.tensor_tensor(s0[:, 2, :], qkr[:, :], s0[:, 1, :], ALU.subtract).then_inc(S["qk_lo"], 1)

            def k1_low(b):
                pool.wait_ge(S["k1_mid"], b + 1)
                pool.tensor_tensor(s1k[:, 2, :], k1r[:, :], s1k[:, 1, :], ALU.subtract).then_inc(S["k1_lo"], 1)

            def q1_low(b):
                pool.wait_ge(S["q1_mid"], b + 1)
                pool.tensor_tensor(s1q[:, 2, :], q1r[:, :], s1q[:, 1, :], ALU.subtract).then_inc(S["q1_lo"], 1)

            def norm1(b):
                rsqrt(rs1[:, 1:2], rs1[:, 0:1], mv1[:, 1:2], "ve1", "rs1", b)
                pool.wait_ge(S["rs1"], b + 1)
                pool.tensor_tensor(rs1[:, 2:3], rs1[:, 1:2], fac[:, INV_IN:INV_IN + 1], ALU.mult)\
                    .then_inc(S["rsi1"], 1)

            def clip_in(b):
                pool.wait_ge(S["ya"], b + 1)
                stand(pool, pool_mark)
                pool.tensor_scalar(yc[:, :], ya[:, :], FP8_MAX, -FP8_MAX, ALU.min, ALU.max).then_inc(S["yc"], 1)

            def round_in(b):
                pool.wait_ge(S["ym"], b + 1)
                pool.tensor_tensor(yt[:, :], yc[:, :], ym[:, :], ALU.add).then_inc(S["yt"], 1)
                pool.wait_ge(S["yt"], b + 1)
                if not (isinstance(b, int) and b < 1):
                    pool.wait_ge(S["yqt_mm"], b)
                pool.tensor_tensor(yq[:, :], yt[:, :], ym[:, :], ALU.subtract).then_inc(S["yq"], 1)

            def clip_out(b):
                pool.wait_ge(S["za"], b + 1)
                stand(pool, pool_mark)
                pool.tensor_scalar(zc[:, :], za[:, :], FP8_MAX, -FP8_MAX, ALU.min, ALU.max).then_inc(S["zc"], 1)

            def round_out(b):
                pool.wait_ge(S["zm"], b + 1)
                pool.tensor_tensor(zt[:, :], zc[:, :], zm[:, :], ALU.add).then_inc(S["zt"], 1)
                pool.wait_ge(S["zt"], b + 1)
                if not (isinstance(b, int) and b < 1):
                    pool.wait_ge(S["x2"], b)
                pool.tensor_tensor(zq[:, :], zt[:, :], zm[:, :], ALU.subtract).then_inc(S["zq"], 1)

            def norm2(b):
                r = rs2
                pool.wait_ge(S["mv2"], b + 1)
                stand(pool, pool_mark)
                pool.tensor_scalar(r[:, 0:1], mv2[:, 1:2], EPS, None, ALU.add).then_inc(S["rs2"], 1)
                pool.wait_ge(S["rs2"], b * 7 + 1)
                pool.tensor_tensor(r[:, 1:2], r[:, 0:1], halfm[:, :], ALU.pow).then_inc(S["rs2"], 1)
                pool.wait_ge(S["rs2"], b * 7 + 2)
                pool.tensor_tensor(r[:, 2:3], r[:, 1:2], r[:, 1:2], ALU.mult).then_inc(S["rs2"], 1)
                pool.wait_ge(S["rs2"], b * 7 + 3)
                pool.tensor_tensor(r[:, 3:4], mv2[:, 1:2], r[:, 2:3], ALU.mult).then_inc(S["rs2"], 1)
                pool.wait_ge(S["rs2"], b * 7 + 4)
                stand(pool, pool_mark)
                pool.tensor_scalar(r[:, 4:5], r[:, 3:4], EPS, None, ALU.add).then_inc(S["rs2"], 1)
                pool.wait_ge(S["rs2"], b * 7 + 5)
                pool.tensor_tensor(r[:, 5:6], r[:, 4:5], halfm[:, :], ALU.pow).then_inc(S["rs2"], 1)
                pool.wait_ge(S["rs2"], b * 7 + 6)
                pool.tensor_tensor(r[:, 6:7], r[:, 5:6], r[:, 1:2], ALU.mult).then_inc(S["rs2"], 1)

            pool.wait_ge(fac_ok, 7)

            def run(u, par, one, two, three):
                b2, b3 = u - LAG2, u - LAG3
                if one:
                    keep_rows(u, par)
                    rsqrt(rs0[:, 1:2], rs0[:, 0:1], mv0[:, 1:2], "ve0", "rs0", u)
                    qk_rest(u)
                if two:
                    k1_low(b2)
                    norm1(b2)
                    clip_in(b2)
                    round_in(b2)
                    clip_out(b2)
                    round_out(b2)
                    norm2(b2)
                if three:
                    rsqrt(rs3[:, 1:2], rs3[:, 0:1], mv3[:, 1:2], "ve3", "rs3", b3)
                if two:
                    q1_low(b2)

            slots(pool, run)


_SPECS = ["x", "ctx", "ctxt", "mask", "ident", "wqk0", "wv0", "wo0", "cols", "row", "wf8", "wq1", "wk1", "wv1",
          "wo1", "wlow", "wup"]


def kernel(**inputs):
    import numpy as np
    import concourse.bacc as bacc
    from concourse.bass_utils import run_bass_kernel_spmd

    a = {k: np.asarray(v) for k, v in inputs.items()}

    def chunks(w):
        return w.T.reshape(NCH, P, w.shape[0]).transpose(1, 0, 2)

    def col(*parts):
        return np.concatenate([np.asarray(p).reshape(-1) for p in parts]).reshape(P, 1)

    rows_q = np.concatenate([np.ones(E0, np.float32), np.zeros(E0, np.float32)])
    wq1 = a["L1_xattn_wq"].reshape(KV, REP, DH1, DM).transpose(1, 0, 2, 3).reshape(DM, DM)
    wo0 = a["L0_xattn_Wo"].T
    zero0 = np.zeros_like(wo0)
    low = np.concatenate([a["L1_ffn_A"].reshape(LOW, DM), a["L1_ffn_Wr"]], axis=0)
    arrays = {
        "x": a["x"],
        "ctx": a["ctx_4096"],
        "ctxt": a["ctx_4096"].transpose(0, 2, 1).reshape(BATCH, NCH, P, P).transpose(0, 2, 1, 3),
        "mask": a["mask_Bx1x4096_ff1"].reshape(BATCH, DM),
        "ident": np.eye(P, dtype=np.float32),
        "wqk0": np.concatenate([a["L0_xattn_Wq"].T, a["L0_xattn_Wk"].T], axis=1),
        "wv0": a["L0_xattn_Wv"].T,
        "wo0": np.stack([np.concatenate([wo0, zero0]), np.concatenate([zero0, wo0])], axis=1),
        "cols": np.concatenate([col(a["L0_xattn_bq"], a["L0_xattn_bk"]), col(a["L0_xattn_bv"], a["L0_xattn_bv"]),
                                col(a["L0_xattn_bo"]), col(rows_q), a["L1_xattn_ln_w"].reshape(NCH, P).T], axis=1),
        "row": np.concatenate([a["g_xattn"], a["g_ffn"], a["L0_ffn_input_scale"].reshape(1),
                               a["L0_ffn_weight_scale"].reshape(1), a["L0_ffn_output_scale"].reshape(1),
                               a["L1_ffn_br"]]),
        "wf8": chunks(a["L0_ffn_w"]),
        "wq1": chunks(wq1),
        "wk1": chunks(a["L1_xattn_wk"]),
        "wv1": chunks(a["L1_xattn_wv"]),
        "wo1": chunks(a["L1_xattn_wo"]),
        "wlow": chunks(low),
        "wup": a["L1_ffn_B"].transpose(0, 2, 1).reshape(LOW, DM),
    }
    arrays = {k: np.ascontiguousarray(v) for k, v in arrays.items()}
    nc = bacc.Bacc("TRN2", target_bir_lowering=False, num_devices=1)
    t = {k: nc.dram_tensor("in_" + k, arrays[k].shape, F32, kind="ExternalInput").ap() for k in _SPECS}
    t["out"] = nc.dram_tensor("out_x", (BATCH, P, DM), F32, kind="ExternalOutput").ap()
    flamingo_block(nc, t)
    r = run_bass_kernel_spmd(nc, [{"in_" + k: arrays[k] for k in _SPECS}], core_ids=[0])
    return r.results[0]["out_x"]
```

```python
from contextlib import ExitStack

import concourse.bass as bass
from concourse import mybir
from concourse.alu_op_type import AluOpType as ALU

ACT = mybir.ActivationFunctionType
AX_X = mybir.AxisListType.X
F32 = mybir.dt.float32
BF16 = mybir.dt.bfloat16
I32 = mybir.dt.int32

P = 128
BATCH = 8
DM = 512
NCH = DM // P
WIN = DM // P
H0 = 8
DH0 = 8
E0 = H0 * DH0
KV = 8
REP = 4
DH1 = 16
HQ = KV * REP
EXPERTS = 8
RANK = 16
LOW = EXPERTS * RANK
EXPERT_GAIN = EXPERTS * 2.0
EPS = 1e-5
FP8_MAX = 448.0
FP8_LEAST = 2.0 ** -6
FP8_STEP = 1.5 * 2.0 ** 20
MASKED = 998244352.0

PAIRS = [(0, 1), (0, 0), (0, 2), (1, 0), (1, 1), (2, 0)]
ROWS0 = len(PAIRS) * DH0
ROWS1 = len(PAIRS) * DH1
ROW_MASK = 64
ROW_MAX = 96
assert ROWS0 <= ROW_MASK and ROWS1 <= ROW_MAX

TILES = 8
SC0_LAG, ST0_LAG, SC1_LAG, ST1_LAG = 1, 1, 3, 3
LAST = 4
SLOTS = BATCH + LAST
FILLS = 8
HEAD = 2


def flamingo_block(nc, t):
    with ExitStack() as ctx:
        def sb(name, shape, dt=F32):
            return ctx.enter_context(nc.sbuf_tensor(name, shape, dt))

        def bank(name):
            return ctx.enter_context(nc.psum_tensor(name, [P, DM], F32))

        def sem(name):
            return ctx.enter_context(nc.semaphore(name))

        ident = sb("ident", [P, P])
        identb = sb("identb", [P, P], BF16)
        wqk0 = sb("wqk0", [P, 2 * E0])
        wv0 = sb("wv0", [P, E0])
        wo0 = sb("wo0", [P, 2, P])
        cols = sb("cols", [P, 4 + NCH])
        BQK, BV, BO, QROW, LNW = 0, 1, 2, 3, 4
        row = sb("row", [P, 15])
        wf8 = sb("wf8", [P, NCH, DM])
        wf8q = sb("wf8q", [P, NCH, DM], BF16)
        wq1 = sb("wq1", [P, NCH, DM])
        wk1 = sb("wk1", [P, NCH, P])
        wv1 = sb("wv1", [P, NCH, P])
        wo1 = sb("wo1", [P, NCH, DM])
        wlow = sb("wlow", [P, NCH, LOW + EXPERTS])
        wup = sb("wup", [P, DM])
        gain = sb("gain", [P, 4])
        fac = sb("fac", [P, 8])
        INV_IN, INV_W, INV_OUT, F_OUT, G_OUT, G_UP, PROD = range(7)
        halfm = sb("halfm", [P, 1])

        xa = sb("xa", [P, 2, DM])
        ctxa = sb("ctxa", [P, 2, DM])
        maska = sb("maska", [P, 2, DM])
        keep = sb("keep", [P, DM])
        mrow = sb("mrow", [P, DM], BF16)
        st0 = sb("st0", [P, 6]); mv0 = sb("mv0", [P, 2]); rs0 = sb("rs0", [P, 2])
        xln0 = sb("xln0", [P, DM])
        qk = sb("qk", [P, DM]); qkr = sb("qkr", [P, DM])
        s0 = sb("s0", [P, 3, DM], BF16)
        Q0 = sb("Q0", [P, 2, H0, DM], BF16)
        K0 = sb("K0", [P, 2, H0, DM], BF16)
        V0 = sb("V0", [P, 2, WIN, H0, DH0 + 1])
        nm0 = sb("nm0", [P, H0, WIN])
        nh0 = sb("nh0", [P, 2, H0, WIN], BF16)
        mt0 = sb("mt0", [2 * H0 * WIN, P], BF16)
        AT = sb("AT", [P, 4, DM])
        os0 = sb("os0", [P, DM]); rc0 = sb("rc0", [P, 16])
        on0 = sb("on0", [P, WIN, E0])
        G = sb("G", [P, 2, 2, P])
        xb = sb("xb", [P, 2, DM])
        maskb = sb("maskb", [P, 2, DM])
        ctxt = sb("ctxt", [P, 2, NCH, P])
        xr = sb("xr", [P, DM]); x1 = sb("x1", [P, 2, DM])
        st1 = sb("st1", [P, 6]); mv1 = sb("mv1", [P, 2]); rs1 = sb("rs1", [P, 3])
        ya = sb("ya", [P, DM]); ye = sb("ye", [P, DM])
        yt = sb("yt", [P, DM]); yq = sb("yq", [P, DM], BF16)
        yqt = sb("yqt", [P, NCH, P], BF16)
        za = sb("za", [P, DM]); ze = sb("ze", [P, DM])
        zt = sb("zt", [P, DM]); zq = sb("zq", [P, DM])
        x2 = sb("x2", [P, 2, DM])
        st2 = sb("st2", [P, 6]); mv2 = sb("mv2", [P, 2]); rs2 = sb("rs2", [P, 8])
        xh = sb("xh", [P, DM]); xht = sb("xht", [P, NCH, P])
        s1q = sb("s1q", [P, 3, DM], BF16); q1r = sb("q1r", [P, DM])
        s1k = sb("s1k", [P, 3, P], BF16); k1r = sb("k1r", [P, P])
        Q1 = sb("Q1", [P, 2, KV, DM], BF16)
        K1 = sb("K1", [P, 2, KV, P], BF16)
        V1 = sb("V1", [P, 2, KV, DH1 + 1])
        nm1 = sb("nm1", [P, HQ]); nh1 = sb("nh1", [P, 2, HQ], BF16)
        mt1 = sb("mt1", [2 * HQ, P], BF16)
        os1 = sb("os1", [P, DM]); rc1 = sb("rc1", [P, 16])
        on1 = sb("on1", [P, KV, REP, DH1]); ont1 = sb("ont1", [P, NCH, P])
        x3 = sb("x3", [P, DM])
        st3 = sb("st3", [P, 6]); mv3 = sb("mv3", [P, 2]); rs3 = sb("rs3", [P, 2])
        xl = sb("xl", [P, DM]); xlt = sb("xlt", [P, NCH, P])
        lg = sb("lg", [P, EXPERTS]); nml = sb("nml", [P, 1]); el = sb("el", [P, EXPERTS])
        sl = sb("sl", [P, 1]); rl = sb("rl", [P, 1]); wl = sb("wl", [P, EXPERTS])
        ls = sb("ls", [P, LOW]); lst = sb("lst", [P, P])
        xo = sb("xo", [P, 2, DM])

        SC = [bank("SC0"), bank("SC1")]
        ST = [bank("ST0"), bank("ST1")]
        O = bank("O")
        PA, PB, PC = bank("PA"), bank("PB"), bank("PC")
        MT0 = Y = QP1 = OT1 = WO = PA[:, :]
        OT0 = Z = XLT = LG = LS = UP = PB[:, :]
        QK = V0P = ONT0 = KV1 = YQT = XHT = MT1 = ONT1 = PC[:, :]

        w_early = sem("w_early"); w_late = sem("w_late")
        zeroed = sem("zeroed"); gains_ok = sem("gains_ok"); fac_ok = sem("fac_ok")
        w8_step = sem("w8_step"); wq1_ok = sem("wq1_ok"); idb_ok = sem("idb_ok")
        o_clear = sem("o_clear")
        sp_mark = sem("sp_mark"); pe_mark = sem("pe_mark"); dve_mark = sem("dve_mark"); pool_mark = sem("pool_mark")

        D = 16
        PER = dict(
            st0=1, mv0=1, ve0=1, rs0=1, xln0=1, keep=1, mrow=1, mrow_in=D,
            qk_mm=1, qk=1, qk_hi=1, qk_r=1, qk_mid=1, qk_lo=1, qk_out=6 * D, q0_in=D, k0_in=D,
            v0_mm=1, v0=1, nh0=1, nl0=1, mt0_mm=1, mt0=1, mt0_out=D, mt0_in=D,
            os0=2, ot0_mm=2, rc0=2, on0=2, ont0_mm=1, gelu=1,
            kv1_mm=1, k1_hi=1, k1_r=1, k1_mid=1, k1_lo=1, k1_out=3 * D, k1_in=D,
            v1=1, y_mm=1, xr=1, x1=1, st1=1, mv1=1, ve1=1, rs1=1, rsi1=1,
            ya=1, yc=1, ye=1, ym=1, yt=1, yq=1, yqt_mm=1, yqt=1, z_mm=1,
            za=1, zc=1, ze=1, zm=1, zt=1, zq=1, x2=1, st2=1, mv2=1, rs2=7, xh=1, xht_mm=1, xht=1,
            q1_mm=1, q1_hi=1, q1_r=1, q1_mid=1, q1_lo=1, q1_out=3 * D, q1_in=D,
            nh1=1, nl1=1, mt1_mm=1, mt1=1, mt1_out=D, mt1_in=D, os1=2, ot1_mm=2, rc1=2, on1=2,
            ont1_mm=1, ont1=1, wo_mm=1, x3=1, st3=1, mv3=1, ve3=1, rs3=1,
            xl=1, xlt_mm=1, xlt=1, lg_mm=1, lg=1, nml=1, el=1, rl=1, wl=1, ls=1, ls_mm=1, lst=1, up_mm=1,
            xo=1, out=D, st0_done=1, st1_done=1)
        S = {n: sem("s_" + n) for n in PER}
        LD = {n: [sem(n + "_even"), sem(n + "_odd")] for n in
              ("ld_xa", "ld_ctxa", "ld_maska", "ld_xb", "ld_maskb", "ld_ctxt")}
        sc_ready, sc_read = sem("sc_ready"), sem("sc_read")
        st_ready, st_read = sem("st_ready"), sem("st_read")
        pv_done, o_read = sem("pv_done"), sem("o_read")

        d_q0 = nc.dram_tensor("d_q0", [len(PAIRS), E0, DM], BF16, kind="Internal").ap()
        d_k0 = nc.dram_tensor("d_k0", [len(PAIRS), E0, DM], BF16, kind="Internal").ap()
        d_m0 = nc.dram_tensor("d_m0", [2, H0 * WIN * P], BF16, kind="Internal").ap()
        d_q1 = nc.dram_tensor("d_q1", [len(PAIRS), P, DM], BF16, kind="Internal").ap()
        d_k1 = nc.dram_tensor("d_k1", [len(PAIRS), P, P], BF16, kind="Internal").ap()
        d_m1 = nc.dram_tensor("d_m1", [2, HQ * P], BF16, kind="Internal").ap()

        RAISED = """xln0 keep v0_mm kv1_mm xr x1 q0_in k0_in st0_done st1_done gelu q1_r xo qk_out os0 k1_out
        mt0_out mt1_out ot0_mm ot1_mm y_mm zt q1_out qk_mm qk_r mt0_mm mt1_mm ont0_mm
        ont1_mm k1_lo yq zq x3 xht_mm q1_lo xlt_mm el ls_mm out nl0 nl1 mt0_in mt1_in q1_in k1_in ya z_mm xh q1_mm wo_mm xl lg_mm wl up_mm qk mrow_in qk_mid qk_lo
        yqt_mm x2 v0 k1_r mt0 on0 yqt za xht mt1 on1 ont1 xlt ls lst""".split()

        def ready(eng, name, b, k=None):
            per = PER[name]
            eng.wait_ge(S[name], b * per + ((HEAD * per if name in RAISED else 0) + (per if k is None else k)))

        def loaded(eng, name, b, par):
            eng.wait_ge(LD[name][par], b * 8 + (16 - 8 * par))

        def freed(eng, name, b, back):
            per = PER[name]
            assert name in RAISED and back <= HEAD
            eng.wait_ge(S[name], b * per + (HEAD - back + 1) * per)

        def at_least(eng, s, value):
            if not (isinstance(value, int) and value <= 0):
                eng.wait_ge(s, value)

        def count(b, layer, lag0, lag1):
            own, other = (lag0, lag1) if layer == 0 else (lag1, lag0)
            if isinstance(b, int):
                seen = b + own - other + (1 if layer == 0 else 0)
                return TILES * (b + min(max(seen, 0), BATCH))
            return b * (2 * TILES) + TILES * (own - other + (1 if layer == 0 else 0))

        def sc_no(b, layer):
            return count(b, layer, SC0_LAG, SC1_LAG)

        def st_no(b, layer):
            return count(b, layer, ST0_LAG, ST1_LAG)

        def half_no(b, layer):
            n = st_no(b, layer)
            if isinstance(b, int):
                return n // 4
            own, other = (ST0_LAG, ST1_LAG) if layer == 0 else (ST1_LAG, ST0_LAG)
            return b * (2 * TILES // 4) + TILES // 4 * (own - other + (1 if layer == 0 else 0))

        def take(pe, u, *readers):
            def done(name, lag, k=None, b=None):
                ready(pe, name, u - lag if b is None else b, k)
            if isinstance(u, int):
                live = [r for r in readers if 0 <= u - r[1] < BATCH]
                for r in live[:1]:
                    done(*r)
                if not live:
                    for r in readers:
                        if u - r[1] >= BATCH:
                            ready(pe, r[0], BATCH - 1)
                return
            for r in readers:
                done(*r)
                if r[1] <= LAST:
                    break

        def step(f, u, par, lag, *args):
            b = u - lag
            if not isinstance(b, int) or 0 <= b < BATCH:
                f(b, (par - lag) % 2, *args)

        def slots(eng, slot):
            for u in range(LAST):
                slot(u, u % 2)
            with eng.Fori(0, (BATCH - LAST) // 2) as i:
                for par in range(2):
                    slot(i * 2 + (LAST + par), par)
            for u in range(BATCH, SLOTS):
                slot(u, u % 2)

        block = ctx.enter_context(nc.Block())

        @block.sync
        def _(sp):
            def settle():
                sp.sem_inc(sp_mark, 1)

            def ld_a(b, par):
                freed(sp, "xln0", b, 2)
                settle()
                sp.dma_start(xa[:, par, :], t["x"][b, :, :]).then_inc(LD["ld_xa"][par], 16)
                freed(sp, "keep", b, 2)
                settle()
                sp.dma_start(maska[:, par, :], t["mask"][b, :].partition_broadcast(P)).then_inc(LD["ld_maska"][par], 16)
                freed(sp, "v0_mm", b, 2)
                settle()
                sp.dma_start(ctxa[:, par, :], t["ctx"][b, :, :]).then_inc(LD["ld_ctxa"][par], 16)

            def ld_b(b, par):
                freed(sp, "kv1_mm", b, 2)
                settle()
                sp.dma_start(ctxt[:, par, :, :], t["ctxt"][b, :, :, :]).then_inc(LD["ld_ctxt"][par], 16)
                freed(sp, "xr", b, 2)
                settle()
                sp.dma_start(maskb[:, par, :], t["mask"][b, :].partition_broadcast(P)).then_inc(LD["ld_maskb"][par], 16)
                freed(sp, "x1", b, 2)
                settle()
                sp.dma_start(xb[:, par, :], t["x"][b, :, :]).then_inc(LD["ld_xb"][par], 16)

            def part(src, n):
                p, w = src.shape
                return src.unsqueeze(1).to_broadcast([p, n, w])

            def qk0_out(b, par, k):
                ready(sp, ("qk_hi", "qk_mid", "qk_lo")[k], b)
                if k == 0:
                    freed(sp, "q0_in", b, 1)
                    freed(sp, "k0_in", b, 1)
                settle()
                first = (slice(0, 3), slice(3, 5), slice(5, 6))[k]
                second = (slice(1, 6, 2), slice(0, 5, 4), slice(2, 3))[k]
                sp.dma_start(d_q0[first, :, :].rearrange("c r w -> r c w"), part(s0[0:E0, k, :], 3 - k))\
                    .then_inc(S["qk_out"], 16)
                sp.dma_start(d_k0[second, :, :].rearrange("c r w -> r c w"), part(s0[E0:P, k, :], 3 - k))\
                    .then_inc(S["qk_out"], 16)

            def qk0_in(b, par):
                freed(sp, "st0_done", b, 2)
                ready(sp, "qk_out", b)
                settle()
                sp.dma_start(Q0[0:ROWS0, par, :, :], d_q0.rearrange("c (d h) w -> (c d) h w", h=H0))\
                    .then_inc(S["q0_in"], 16)
                sp.dma_start(K0[0:ROWS0, par, :, :], d_k0.rearrange("c (d h) w -> (c d) h w", h=H0))\
                    .then_inc(S["k0_in"], 16)

            def mask_in(b, par):
                ready(sp, "mrow", b)
                freed(sp, "st0_done", b, 2)
                settle()
                sp.dma_start(K0[ROW_MASK:ROW_MASK + 1, par, :, :], part(mrow[E0:E0 + 1, :], H0))\
                    .then_inc(S["mrow_in"], 16)

            def m0_row(b, par):
                freed(sp, "mt0_in", b, 1)
                ready(sp, "mt0", b)
                settle()
                sp.dma_start(d_m0.rearrange("a (r i) -> (a r) i", i=P), mt0[:, :]).then_inc(S["mt0_out"], 16)
                ready(sp, "mt0_out", b)
                settle()
                sp.dma_start(Q0[ROW_MAX:ROW_MAX + 2, par, :, :], d_m0.rearrange("a (h w) -> a h w", h=H0))\
                    .then_inc(S["mt0_in"], 16)

            def k1_out(b, par):
                freed(sp, "k1_in", b, 1)
                ready(sp, "k1_lo", b)
                settle()
                for k, blocks in enumerate((slice(1, 6, 2), slice(0, 5, 4), slice(2, 3))):
                    sp.dma_start(d_k1[blocks, :, :].rearrange("c r w -> r c w"), part(s1k[:, k, :], 3 - k))\
                        .then_inc(S["k1_out"], 16)
                freed(sp, "st1_done", b, 2)
                ready(sp, "k1_out", b)
                settle()
                sp.dma_start(K1[0:ROWS1, par, :, :], d_k1.rearrange("c (d k) w -> (c d) k w", k=KV))\
                    .then_inc(S["k1_in"], 16)

            def q1_out(b, par, k):
                ready(sp, ("q1_hi", "q1_mid", "q1_lo")[k], b)
                if k == 0:
                    freed(sp, "q1_in", b, 1)
                settle()
                blocks = (slice(0, 3), slice(3, 5), slice(5, 6))[k]
                sp.dma_start(d_q1[blocks, :, :].rearrange("c r w -> r c w"), part(s1q[:, k, :], 3 - k))\
                    .then_inc(S["q1_out"], 16)

            def q1_in(b, par):
                freed(sp, "st1_done", b, 2)
                ready(sp, "q1_out", b)
                settle()
                sp.dma_start(Q1[0:ROWS1, par, :, :], d_q1.rearrange("c (d k) w -> (c d) k w", k=KV))\
                    .then_inc(S["q1_in"], 16)

            def m1_row(b, par):
                freed(sp, "mt1_in", b, 1)
                ready(sp, "mt1", b)
                settle()
                sp.dma_start(d_m1.rearrange("a (r i) -> (a r) i", i=P), mt1[:, :]).then_inc(S["mt1_out"], 16)
                ready(sp, "mt1_out", b)
                settle()
                sp.dma_start(Q1[ROW_MAX:ROW_MAX + 2, par, :, :], d_m1.rearrange("a (k w) -> a k w", k=KV))\
                    .then_inc(S["mt1_in"], 16)

            def store(b, par):
                ready(sp, "xo", b)
                settle()
                sp.dma_start(t["out"][b, :, :], xo[:, par, :]).then_inc(S["out"], 16)

            for name in RAISED:
                sp.sem_inc(S[name], HEAD * PER[name])
            sp.dma_start(cols[:, :], t["cols"]).then_inc(w_early, 16)
            sp.dma_start(wqk0[:, :], t["wqk0"]).then_inc(w_early, 16)
            sp.dma_start(row[:, :], t["row"].partition_broadcast(P)).then_inc(w_early, 16)
            sp.dma_start(wv0[:, :], t["wv0"]).then_inc(w_early, 16)
            sp.dma_start(ident[:, :], t["ident"]).then_inc(w_early, 16)
            sp.dma_start(wo0[:, :, :], t["wo0"]).then_inc(w_early, 16)

            def late_weights(b, par):
                for dst, name in ((wf8, "wf8"), (wq1, "wq1"), (wk1, "wk1"), (wv1, "wv1"), (wo1, "wo1"),
                                  (wlow, "wlow")):
                    sp.dma_start(dst[:, :, :], t[name]).then_inc(w_late, 16)
                sp.dma_start(wup[:, :], t["wup"]).then_inc(w_late, 16)
                sp.wait_ge(zeroed, FILLS)

            def slot(u, par):
                step(ld_a, u, par, 0)
                step(qk0_out, u, par, 1, 0)
                step(qk0_out, u, par, 1, 1)
                for k in range(0, 3):
                    step(q1_out, u, par, 3, k)
                step(q1_in, u, par, 3)
                step(qk0_out, u, par, 1, 2)
                step(qk0_in, u, par, 1)
                step(mask_in, u, par, 1)
                if isinstance(u, int) and u == 0:
                    late_weights(0, 0)
                step(ld_b, u, par, 1)
                step(m1_row, u, par, 3)
                step(k1_out, u, par, 2)
                step(m0_row, u, par, 1)
                step(store, u, par, 4)

            slots(sp, slot)
            sp.wait_ge(S["out"], (BATCH + HEAD) * 16)

        @block.tensor
        def _(pe):
            mm = pe.matmul

            def qk_mm(b, par):
                ready(pe, "xln0", b)
                mm(QK[:, :], wqk0[:, :], xln0[:, :], start=True, stop=True).then_inc(S["qk_mm"], 1)

            def v0_mm(b, par):
                loaded(pe, "ld_ctxa", b, par)
                for w in range(WIN):
                    last = mm(V0P[:, w * E0:(w + 1) * E0], ctxa[:, par, w * P:(w + 1) * P], wv0[:, :],
                              start=True, stop=True)
                last.then_inc(S["v0_mm"], 1)

            def kv1_mm(b, par):
                loaded(pe, "ld_ctxt", b, par)
                for c in range(NCH):
                    last = mm(KV1[:, 0:P], wk1[:, c, :], ctxt[:, par, c, :], start=c == 0, stop=c == NCH - 1)
                for c in range(NCH):
                    last = mm(KV1[:, P:2 * P], ctxt[:, par, c, :], wv1[:, c, :], start=c == 0, stop=c == NCH - 1)
                last.then_inc(S["kv1_mm"], 1)

            def sc0(b, par, tile):
                if tile == 0:
                    ready(pe, "q0_in", b)
                    ready(pe, "k0_in", b)
                    ready(pe, "mrow_in", b)
                at_least(pe, sc_read, sc_no(b, 0) + (tile - 1))
                w, h0 = tile // 2, tile % 2 * 4
                for g in range(4):
                    last = mm(SC[tile % 2][:, g * P:(g + 1) * P], Q0[0:ROW_MAX, par, h0 + g, w * P:(w + 1) * P],
                              K0[0:ROW_MAX, par, h0 + g, w * P:(w + 1) * P], start=True, stop=True)
                last.then_inc(sc_ready, 1)

            def sc1(b, par, kv):
                if kv == 0:
                    ready(pe, "q1_in", b)
                    ready(pe, "k1_in", b)
                at_least(pe, sc_read, sc_no(b, 1) + (kv - 1))
                for r in range(REP):
                    last = mm(SC[kv % 2][:, r * P:(r + 1) * P], Q1[0:ROW_MAX, par, kv, r * P:(r + 1) * P],
                              K1[0:ROW_MAX, par, kv, :], start=True, stop=True)
                last.then_inc(sc_ready, 1)

            def mt0_mm(b, par):
                ready(pe, "nl0", b)
                pe.sem_inc(pe_mark, 1)
                pe.transpose(MT0.bitcast(BF16)[0:2 * H0 * WIN, 0:P], nh0[:, :, :, :].rearrange("p a h w -> p (a h w)"),
                             identb[:, :]).then_inc(S["mt0_mm"], 1)

            def mt1_mm(b, par):
                ready(pe, "nl1", b)
                pe.sem_inc(pe_mark, 1)
                pe.transpose(MT1.bitcast(BF16)[0:2 * HQ, 0:P], nh1[:, :, :].rearrange("p a h -> p (a h)"),
                             identb[:, :]).then_inc(S["mt1_mm"], 1)

            def att0(b, par, k):
                if k < TILES:
                    if k == 0:
                        ready(pe, "mt0_in", b)
                    at_least(pe, st_read, st_no(b, 0) + (k - 1))
                    w, h0 = k // 2, k % 2 * 4
                    for g in range(4):
                        last = mm(ST[k % 2][:, g * P:(g + 1) * P], K0[:, par, h0 + g, w * P:(w + 1) * P],
                                  Q0[:, par, h0 + g, w * P:(w + 1) * P], start=True, stop=True)
                    last.then_inc(st_ready, 1)
                if k > 0:
                    k -= 1
                    w, h0 = k // 2, k % 2 * 4
                    pe.wait_ge(st_read, st_no(b, 0) + (k + 1))
                    if k % 4 == 0:
                        at_least(pe, o_read, half_no(b, 0) + k // 4)
                    for g in range(4):
                        last = mm(O[32 * g:32 * g + DH0 + 1, k % 4 * P:(k % 4 + 1) * P], V0[:, par, w, h0 + g, :],
                                  AT[:, k % 4, g * P:(g + 1) * P], start=True, stop=True)
                    last.then_inc(pv_done, 1)

            def att1(b, par, k):
                if k < TILES:
                    if k == 0:
                        ready(pe, "mt1_in", b)
                        ready(pe, "v1", b)
                    at_least(pe, st_read, st_no(b, 1) + (k - 1))
                    mm(ST[k % 2][:, :], K1[:, par, k, :], Q1[:, par, k, :], start=True, stop=True)\
                        .then_inc(st_ready, 1)
                if k > 0:
                    k -= 1
                    pe.wait_ge(st_read, st_no(b, 1) + (k + 1))
                    if k % 4 == 0:
                        at_least(pe, o_read, half_no(b, 1) + k // 4)
                    g = k % 4
                    mm(O[32 * g:32 * g + DH1 + 1, :], V1[:, par, k, :], AT[:, k % 4, :],
                       start=True, stop=True).then_inc(pv_done, 1)

            def ot0_mm(b, par, half):
                ready(pe, "os0", b, half + 1)
                for k in range(4):
                    last = pe.transpose(OT0[:, k * P:(k + 1) * P], os0[:, k * P:(k + 1) * P], ident[:, :])
                last.then_inc(S["ot0_mm"], 1)

            def ot1_mm(b, par, half):
                ready(pe, "os1", b, half + 1)
                for r in range(REP):
                    last = pe.transpose(OT1[:, r * P:(r + 1) * P], os1[:, r * P:(r + 1) * P], ident[:, :])
                last.then_inc(S["ot1_mm"], 1)

            def ont0_mm(b, par):
                ready(pe, "on0", b)
                for k in range(2):
                    last = pe.transpose(ONT0[:, k * P:(k + 1) * P],
                                        on0[:, 2 * k:2 * k + 2, :].rearrange("p w e -> p (w e)"), ident[:, :])
                last.then_inc(S["ont0_mm"], 1)

            def y_mm(b, par):
                ready(pe, "gelu", b)
                out = Y[:, :].rearrange("p (a o i) -> p a o i", a=2, o=2)
                for o in range(2):
                    last = mm(out[:, :, o, :], wo0[:, o, :], G[:, par, :, :], start=True, stop=True)
                last.then_inc(S["y_mm"], 1)

            def yqt_mm(b, par):
                ready(pe, "yq", b)
                for c in range(NCH):
                    last = pe.transpose(YQT.bitcast(BF16)[:, c * P:(c + 1) * P], yq[:, c * P:(c + 1) * P], identb[:, :])
                last.then_inc(S["yqt_mm"], 1)

            def z_mm(b, par):
                ready(pe, "yqt", b)
                for c in range(NCH):
                    last = mm(Z[:, :], yqt[:, c, :], wf8q[:, c, :], start=c == 0, stop=c == NCH - 1)
                last.then_inc(S["z_mm"], 1)

            def xht_mm(b, par):
                ready(pe, "xh", b)
                for c in range(NCH):
                    last = pe.transpose(XHT[:, c * P:(c + 1) * P], xh[:, c * P:(c + 1) * P], ident[:, :])
                last.then_inc(S["xht_mm"], 1)

            def q1_mm(b, par):
                ready(pe, "xht", b)
                for r in range(REP):
                    for c in range(NCH):
                        last = mm(QP1[:, r * P:(r + 1) * P], wq1[:, c, r * P:(r + 1) * P], xht[:, c, :],
                                  start=c == 0, stop=c == NCH - 1)
                last.then_inc(S["q1_mm"], 1)

            def ont1_mm(b, par):
                ready(pe, "on1", b)
                flat = on1[:, :, :, :].rearrange("p k r d -> p (k r d)")
                for c in range(NCH):
                    last = pe.transpose(ONT1[:, c * P:(c + 1) * P], flat[:, c * P:(c + 1) * P], ident[:, :])
                last.then_inc(S["ont1_mm"], 1)

            def wo_mm(b, par):
                ready(pe, "ont1", b)
                for c in range(NCH):
                    last = mm(WO[:, :], ont1[:, c, :], wo1[:, c, :], start=c == 0, stop=c == NCH - 1)
                last.then_inc(S["wo_mm"], 1)

            def xlt_mm(b, par):
                ready(pe, "xl", b)
                for c in range(NCH):
                    last = pe.transpose(XLT[:, c * P:(c + 1) * P], xl[:, c * P:(c + 1) * P], ident[:, :])
                last.then_inc(S["xlt_mm"], 1)

            def lg_mm(b, par):
                ready(pe, "xlt", b)
                for c in range(NCH):
                    last = mm(LG[:, 0:LOW + EXPERTS], xlt[:, c, :], wlow[:, c, :], start=c == 0, stop=c == NCH - 1)
                last.then_inc(S["lg_mm"], 1)

            def ls_mm(b, par):
                ready(pe, "ls", b)
                pe.transpose(LS[:, 0:P], ls[:, :], ident[:, :]).then_inc(S["ls_mm"], 1)

            def up_mm(b, par):
                ready(pe, "lst", b)
                mm(UP[:, :], lst[:, :], wup[:, :], start=True, stop=True).then_inc(S["up_mm"], 1)

            def late_weights(b, par):
                pe.wait_ge(w_late, 16 * 7)
                pe.wait_ge(wq1_ok, 1)
                pe.wait_ge(w8_step, 6)

            pe.wait_ge(w_early, 16 * 6)
            pe.wait_ge(o_clear, 1)
            pe.wait_ge(idb_ok, 1)

            def slot(u, par):
                step(sc1, u, par, 3, 0)
                step(sc1, u, par, 3, 1)
                take(pe, u, ("on0", 2, 1), ("xo", 5), ("lst", 5), ("za", 3), ("ls", 5), ("xlt", 5), ("on0", 3,
                     2))
                step(ot0_mm, u, par, 2, 1)
                step(sc1, u, par, 3, 2)
                step(sc1, u, par, 3, 3)
                take(pe, u, ("k1_r", 2), ("xht", 3), ("ont1", 4), ("v0", 2), ("yqt", 3), ("qk", 1), ("mt1", 4),
                     ("gelu", 3))
                step(ont0_mm, u, par, 2)
                step(sc1, u, par, 3, 4)
                take(pe, u, ("on0", 2, 2), ("on0", 2, 1), ("xo", 5), ("lst", 5), ("za", 3), ("ls", 5), ("xlt",
                     5))
                step(xlt_mm, u, par, 4)
                for k in range(5, 8):
                    step(sc1, u, par, 3, k)
                take(pe, u, ("q1_r", 3), ("x3", 4), ("mt0", 2), ("on1", 4, 2), ("on1", 4, 1), ("xr", 3))
                step(y_mm, u, par, 2)
                step(sc0, u, par, 1, 0)
                take(pe, u, ("gelu", 2), ("k1_r", 2), ("xht", 3), ("ont1", 4), ("v0", 2), ("yqt", 3), ("qk", 1),
                     ("mt1", 4))
                step(mt1_mm, u, par, 3)
                step(sc0, u, par, 1, 1)
                take(pe, u, ("xlt", 4), ("on0", 2, 2), ("on0", 2, 1), ("xo", 5), ("lst", 5), ("za", 3), ("ls",
                     5))
                step(lg_mm, u, par, 4)
                take(pe, u, ("mt1", 3), ("gelu", 2), ("k1_r", 2), ("xht", 3), ("ont1", 4), ("v0", 2), ("yqt",
                     3), ("qk", 1))
                step(qk_mm, u, par, 0)
                step(sc0, u, par, 1, 2)
                step(sc0, u, par, 1, 3)
                for k in range(0, 5):
                    step(att1, u, par, 3, k)
                step(sc0, u, par, 1, 4)
                take(pe, u, ("qk", 0), ("mt1", 3), ("gelu", 2), ("k1_r", 2), ("xht", 3), ("ont1", 4), ("v0", 2),
                     ("yqt", 3))
                step(yqt_mm, u, par, 2)
                step(sc0, u, par, 1, 5)
                step(att1, u, par, 3, 5)
                take(pe, u, ("ls", 4), ("xlt", 4), ("on0", 2, 2), ("on0", 2, 1), ("xo", 5), ("lst", 5), ("za",
                     3))
                step(z_mm, u, par, 2)
                step(att1, u, par, 3, 6)
                take(pe, u, ("yqt", 2), ("qk", 0), ("mt1", 3), ("gelu", 2), ("k1_r", 2), ("xht", 3), ("ont1",
                     4), ("v0", 2))
                step(v0_mm, u, par, 1)
                step(sc0, u, par, 1, 6)
                step(att1, u, par, 3, 7)
                take(pe, u, ("xr", 2), ("q1_r", 3), ("x3", 4), ("mt0", 2), ("on1", 4, 2), ("on1", 4, 1))
                step(ot1_mm, u, par, 3, 0)
                step(sc0, u, par, 1, 7)
                step(att1, u, par, 3, 8)
                take(pe, u, ("za", 2), ("ls", 4), ("xlt", 4), ("on0", 2, 2), ("on0", 2, 1), ("xo", 5), ("lst",
                     5))
                step(ls_mm, u, par, 4)
                take(pe, u, ("on1", 3, 1), ("xr", 2), ("q1_r", 3), ("x3", 4), ("mt0", 2), ("on1", 4, 2))
                step(ot1_mm, u, par, 3, 1)
                take(pe, u, ("v0", 1), ("yqt", 2), ("qk", 0), ("mt1", 3), ("gelu", 2), ("k1_r", 2), ("xht", 3),
                     ("ont1", 4))
                step(ont1_mm, u, par, 3)
                take(pe, u, ("on1", 3, 2), ("on1", 3, 1), ("xr", 2), ("q1_r", 3), ("x3", 4), ("mt0", 2))
                step(mt0_mm, u, par, 1)
                take(pe, u, ("lst", 4), ("za", 2), ("ls", 4), ("xlt", 4), ("on0", 2, 2), ("on0", 2, 1), ("xo",
                     5))
                step(up_mm, u, par, 4)
                take(pe, u, ("mt0", 1), ("on1", 3, 2), ("on1", 3, 1), ("xr", 2), ("q1_r", 3), ("x3", 4))
                step(wo_mm, u, par, 3)
                take(pe, u, ("ont1", 3), ("v0", 1), ("yqt", 2), ("qk", 0), ("mt1", 3), ("gelu", 2), ("k1_r", 2),
                     ("xht", 3))
                step(xht_mm, u, par, 2)
                step(att0, u, par, 1, 0)
                take(pe, u, ("x3", 3), ("mt0", 1), ("on1", 3, 2), ("on1", 3, 1), ("xr", 2), ("q1_r", 3))
                step(q1_mm, u, par, 2)
                take(pe, u, ("xht", 2), ("ont1", 3), ("v0", 1), ("yqt", 2), ("qk", 0), ("mt1", 3), ("gelu", 2),
                     ("k1_r", 2))
                step(kv1_mm, u, par, 1)
                for k in range(1, 8):
                    step(att0, u, par, 1, k)
                take(pe, u, ("xo", 4), ("lst", 4), ("za", 2), ("ls", 4), ("xlt", 4), ("on0", 2, 2), ("on0", 2,
                     1))
                step(ot0_mm, u, par, 1, 0)
                step(att0, u, par, 1, 8)
                if isinstance(u, int) and u == 2:
                    late_weights(0, 0)

            slots(pe, slot)

        @block.scalar
        def _(act):
            def qk_hi(b, par):
                ready(act, "qk", b)
                freed(act, "qk_out", b, 1)
                act.activation(s0[:, 0, :], qk[:, :], ACT.Copy).then_inc(S["qk_hi"], 1)

            def qk_mid(b, par):
                ready(act, "qk_r", b)
                act.activation(s0[:, 1, :], qkr[:, :], ACT.Copy).then_inc(S["qk_mid"], 1)

            def v0(b, par):
                ready(act, "v0_mm", b)
                freed(act, "os0", b, 2)
                act.activation(V0[:, par, :, :, 0:DH0],
                               V0P[:, 0:WIN * E0].rearrange("p (w h d) -> p w h d", w=WIN, h=H0),
                               ACT.Copy).then_inc(S["v0"], 1)

            def k1_hi(b, par):
                ready(act, "kv1_mm", b)
                freed(act, "k1_out", b, 1)
                act.activation(s1k[:, 0, :], KV1[:, 0:P], ACT.Copy).then_inc(S["k1_hi"], 1)
                freed(act, "st1_done", b, 2)
                act.activation(V1[:, par, :, 0:DH1], KV1[:, P:2 * P].rearrange("p (k d) -> p k d", k=KV),
                               ACT.Copy).then_inc(S["v1"], 1)

            def k1_mid(b, par):
                ready(act, "k1_r", b)
                act.activation(s1k[:, 1, :], k1r[:, :], ACT.Copy).then_inc(S["k1_mid"], 1)

            def mt0_copy(b, par):
                ready(act, "mt0_mm", b)
                freed(act, "mt0_out", b, 1)
                act.activation(mt0[:, :], MT0.bitcast(BF16)[0:2 * H0 * WIN, 0:P], ACT.Copy).then_inc(S["mt0"], 1)

            def mt1_copy(b, par):
                ready(act, "mt1_mm", b)
                freed(act, "mt1_out", b, 1)
                act.activation(mt1[:, :], MT1.bitcast(BF16)[0:2 * HQ, 0:P], ACT.Copy).then_inc(S["mt1"], 1)

            def exp_tile(b, layer, tile, dh):
                n = st_no(b, layer)
                act.wait_ge(st_ready, n + (tile + 1))
                at_least(act, pv_done, n + (tile - 3))
                act.activation(AT[:, tile % 4, :], ST[tile % 2][:, :], ACT.Exp, scale=float(dh) ** -0.5)\
                    .then_inc(st_read, 1)

            def exp0(b, par, tile):
                exp_tile(b, 0, tile, DH0)

            def exp1(b, par, tile):
                exp_tile(b, 1, tile, DH1)

            def os0_copy(b, par, half):
                act.wait_ge(pv_done, st_no(b, 0) + (4 * half + 4))
                if half == 0:
                    freed(act, "ot0_mm", b, 1)
                else:
                    ready(act, "ot0_mm", b, 1)
                act.activation(os0[:, :], O[:, :], ACT.Copy).then_inc(S["os0"], 1)
                ready(act, "os0", b, half + 1)
                act.sem_inc(o_read, 1)
                if half == 1:
                    act.sem_inc(S["st0_done"], 1)

            def os1_copy(b, par, half):
                act.wait_ge(pv_done, st_no(b, 1) + (4 * half + 4))
                if half == 0:
                    freed(act, "ot1_mm", b, 1)
                else:
                    ready(act, "ot1_mm", b, 1)
                act.activation(os1[:, :], O[:, :], ACT.Copy).then_inc(S["os1"], 1)
                ready(act, "os1", b, half + 1)
                act.sem_inc(o_read, 1)
                if half == 1:
                    act.sem_inc(S["st1_done"], 1)

            def gelu(b, par):
                ready(act, "ont0_mm", b)
                freed(act, "y_mm", b, 2)
                act.activation(G[:, par, :, :], ONT0[:, 0:2 * P].rearrange("p (a i) -> p a i", a=2), ACT.Gelu,
                               bias=cols[:, BV:BV + 1]).then_inc(S["gelu"], 1)

            def yqt_copy(b, par):
                ready(act, "yqt_mm", b)
                freed(act, "z_mm", b, 1)
                act.activation(yqt[:, :, :], YQT.bitcast(BF16)[:, 0:DM].rearrange("p (c i) -> p c i", c=NCH), ACT.Copy)\
                    .then_inc(S["yqt"], 1)

            def za_copy(b, par):
                ready(act, "z_mm", b)
                freed(act, "zt", b, 1)
                act.activation(za[:, :], Z[:, :], ACT.Copy, scale=fac[:, F_OUT:F_OUT + 1]).then_inc(S["za"], 1)

            def xht_copy(b, par):
                ready(act, "xht_mm", b)
                freed(act, "q1_mm", b, 1)
                act.activation(xht[:, :, :], XHT[:, :].rearrange("p (c i) -> p c i", c=NCH), ACT.Copy)\
                    .then_inc(S["xht"], 1)

            def q1_hi(b, par):
                ready(act, "q1_mm", b)
                freed(act, "q1_out", b, 1)
                act.activation(s1q[:, 0, :], QP1[:, :], ACT.Copy).then_inc(S["q1_hi"], 1)

            def q1_mid(b, par):
                ready(act, "q1_r", b)
                act.activation(s1q[:, 1, :], q1r[:, :], ACT.Copy).then_inc(S["q1_mid"], 1)

            def ont1_copy(b, par):
                ready(act, "ont1_mm", b)
                freed(act, "wo_mm", b, 1)
                act.activation(ont1[:, :, :], ONT1[:, :].rearrange("p (c i) -> p c i", c=NCH), ACT.Copy)\
                    .then_inc(S["ont1"], 1)

            def xlt_copy(b, par):
                ready(act, "xlt_mm", b)
                freed(act, "lg_mm", b, 1)
                act.activation(xlt[:, :, :], XLT[:, :].rearrange("p (c i) -> p c i", c=NCH), ACT.Copy)\
                    .then_inc(S["xlt"], 1)

            def router_exp(b, par):
                ready(act, "nml", b)
                freed(act, "wl", b, 1)
                act.activation(el[:, :], lg[:, :], ACT.Exp, bias=nml[:, 0:1], accum_out=sl[:, 0:1])\
                    .then_inc(S["el"], 1)

            def lst_copy(b, par):
                ready(act, "ls_mm", b)
                freed(act, "up_mm", b, 1)
                act.activation(lst[:, :], LS[:, 0:P], ACT.Copy).then_inc(S["lst"], 1)

            act.wait_ge(w_early, 16 * 6)
            act.activation(gain[:, :], row[:, 0:4], ACT.Tanh).then_inc(gains_ok, 1)
            act.wait_ge(fac_ok, 7)

            def slot(u, par):
                step(gelu, u, par, 2)
                step(mt1_copy, u, par, 3)
                step(k1_mid, u, par, 2)
                step(xlt_copy, u, par, 4)
                step(router_exp, u, par, 4)
                for k in range(0, 5):
                    step(exp1, u, par, 3, k)
                step(os1_copy, u, par, 3, 0)
                step(yqt_copy, u, par, 2)
                step(exp1, u, par, 3, 5)
                step(za_copy, u, par, 2)
                step(exp1, u, par, 3, 6)
                step(exp1, u, par, 3, 7)
                step(os1_copy, u, par, 3, 1)
                step(v0, u, par, 1)
                step(qk_hi, u, par, 0)
                step(lst_copy, u, par, 4)
                step(mt0_copy, u, par, 1)
                step(ont1_copy, u, par, 3)
                step(qk_mid, u, par, 0)
                step(xht_copy, u, par, 2)
                step(exp0, u, par, 1, 0)
                step(q1_hi, u, par, 2)
                step(q1_mid, u, par, 2)
                for k in range(1, 5):
                    step(exp0, u, par, 1, k)
                step(os0_copy, u, par, 1, 0)
                for k in range(5, 8):
                    step(exp0, u, par, 1, k)
                step(k1_hi, u, par, 1)
                step(os0_copy, u, par, 1, 1)

            slots(act, slot)

        @block.vector
        def _(dve):
            def binade(dst, src):
                return dve.tensor_scalar(dst.bitcast(I32), src.bitcast(I32), 0x7F800000, None, ALU.bitwise_and)

            def rounder(dst, src):
                return dve.tensor_scalar(dst, src, FP8_LEAST, FP8_STEP, ALU.max, ALU.mult)

            def stats(x, st, mv, s_st, s_mv, b):
                dve.bn_stats(st[:, :], x).then_inc(S[s_st], 1)
                ready(dve, s_st, b)
                dve.sem_inc(dve_mark, 1)
                dve.bn_aggr(mv[:, :], st[:, :]).then_inc(S[s_mv], 1)

            def ln0_stats(b, par):
                freed(dve, "xln0", b, 1)
                loaded(dve, "ld_xa", b, par)
                stats(xa[:, par, :], st0, mv0, "st0", "mv0", b)

            def ln0(b, par):
                ready(dve, "rs0", b)
                freed(dve, "qk_mm", b, 1)
                dve.tensor_scalar(xln0[:, :], xa[:, par, :], mv0[:, 0:1], rs0[:, 1:2], ALU.subtract, ALU.mult)\
                    .then_inc(S["xln0"], 1)

            def qk_bias(b, par):
                ready(dve, "keep", b)
                freed(dve, "qk_r", b, 1)
                ready(dve, "qk_mm", b)
                dve.scalar_tensor_tensor(out=qk[:, :], in0=QK[:, :], scalar=cols[:, BQK:BQK + 1], in1=keep[:, :],
                                         op0=ALU.add, op1=ALU.mult).then_inc(S["qk"], 1)

            def max_tile(b, layer, tile, dst):
                if tile == 0:
                    freed(dve, ("nl0", "nl1")[layer], b, 1)
                dve.wait_ge(sc_ready, sc_no(b, layer) + (tile + 1))
                dve.tensor_reduce(dst, SC[tile % 2][:, :].rearrange("p (g j) -> p g j", g=4), AX_X, ALU.max,
                                  negate=True).then_inc(sc_read, 1)

            def max0(b, par, tile):
                max_tile(b, 0, tile, nm0[:, tile % 2 * 4:tile % 2 * 4 + 4, tile // 2])

            def max1(b, par, tile):
                max_tile(b, 1, tile, nm1[:, tile * REP:(tile + 1) * REP])

            def minus_max0(b, par):
                freed(dve, "mt0_mm", b, 1)
                dve.wait_ge(sc_read, sc_no(b, 0) + TILES)
                dve.tensor_copy(nh0[:, 0, :, :], nm0[:, :, :]).then_inc(S["nh0"], 1)
                ready(dve, "nh0", b)
                dve.tensor_tensor(nh0[:, 1, :, :], nm0[:, :, :], nh0[:, 0, :, :], ALU.subtract)\
                    .then_inc(S["nl0"], 1)

            def minus_max1(b, par):
                freed(dve, "mt1_mm", b, 1)
                dve.wait_ge(sc_read, sc_no(b, 1) + TILES)
                dve.tensor_copy(nh1[:, 0, :], nm1[:, :]).then_inc(S["nh1"], 1)
                ready(dve, "nh1", b)
                dve.tensor_tensor(nh1[:, 1, :], nm1[:, :], nh1[:, 0, :], ALU.subtract).then_inc(S["nl1"], 1)

            def norm0(b, par, half):
                if half == 0:
                    freed(dve, "ont0_mm", b, 1)
                ready(dve, "ot0_mm", b, half + 1)
                src = OT0[:, :].rearrange("p (w h d) -> p w h d", w=2, h=H0)
                rc = rc0[:, :].rearrange("p (w h) -> p w h", w=2)
                dve.reciprocal(rc, src[:, :, :, DH0]).then_inc(S["rc0"], 1)
                ready(dve, "rc0", b, half + 1)
                dve.tensor_tensor(on0[:, 2 * half:2 * half + 2, :].rearrange("p w (h d) -> p w h d", h=H0),
                                  src[:, :, :, 0:DH0],
                                  rc.unsqueeze(3).to_broadcast([P, 2, H0, DH0]), ALU.mult)\
                    .then_inc(S["on0"], 1)

            def norm1(b, par, half):
                if half == 0:
                    freed(dve, "ont1_mm", b, 1)
                ready(dve, "ot1_mm", b, half + 1)
                src = OT1[:, :].rearrange("p (r g d) -> p g r d", r=REP, g=4)
                rc = rc1[:, :].rearrange("p (g r) -> p g r", g=4)
                dve.reciprocal(rc, src[:, :, :, DH1]).then_inc(S["rc1"], 1)
                ready(dve, "rc1", b, half + 1)
                dve.tensor_tensor(on1[:, 4 * half:4 * half + 4, :, :], src[:, :, :, 0:DH1],
                                  rc.unsqueeze(3).to_broadcast([P, 4, REP, DH1]), ALU.mult)\
                    .then_inc(S["on1"], 1)

            def k1_rest(b, par):
                ready(dve, "v1", b)
                freed(dve, "k1_lo", b, 1)
                ready(dve, "k1_hi", b)
                dve.tensor_tensor(k1r[:, :], KV1[:, 0:P], s1k[:, 0, :], ALU.subtract).then_inc(S["k1_r"], 1)

            def add_att0(b, par):
                loaded(dve, "ld_maskb", b, par)
                ready(dve, "y_mm", b)
                dve.scalar_tensor_tensor(out=xr[:, :], in0=Y[:, :], scalar=cols[:, BO:BO + 1],
                                         in1=maskb[:, par, :], op0=ALU.add, op1=ALU.mult).then_inc(S["xr"], 1)
                loaded(dve, "ld_xb", b, par)
                ready(dve, "xr", b)
                freed(dve, "x2", b, 2)
                freed(dve, "ya", b, 1)
                dve.scalar_tensor_tensor(out=x1[:, par, :], in0=xr[:, :], scalar=gain[:, 0:1], in1=xb[:, par, :],
                                         op0=ALU.mult, op1=ALU.add).then_inc(S["x1"], 1)
                ready(dve, "x1", b)
                stats(x1[:, par, :], st1, mv1, "st1", "mv1", b)

            def quant_in(b, par):
                freed(dve, "yq", b, 1)
                ready(dve, "rsi1", b)
                dve.tensor_scalar(ya[:, :], x1[:, par, :], mv1[:, 0:1], rs1[:, 2:3], ALU.subtract, ALU.mult)\
                    .then_inc(S["ya"], 1)
                ready(dve, "ya", b)
                dve.tensor_scalar(ya[:, :], ya[:, :], FP8_MAX, -FP8_MAX, ALU.min, ALU.max).then_inc(S["yc"], 1)
                ready(dve, "yc", b)
                binade(ye[:, :], ya[:, :]).then_inc(S["ye"], 1)
                ready(dve, "ye", b)
                rounder(ye[:, :], ye[:, :]).then_inc(S["ym"], 1)

            def quant_out(b, par):
                freed(dve, "zq", b, 1)
                ready(dve, "za", b)
                dve.tensor_scalar(za[:, :], za[:, :], FP8_MAX, -FP8_MAX, ALU.min, ALU.max).then_inc(S["zc"], 1)
                ready(dve, "zc", b)
                binade(ze[:, :], za[:, :]).then_inc(S["ze"], 1)
                ready(dve, "ze", b)
                rounder(ze[:, :], ze[:, :]).then_inc(S["zm"], 1)

            def add_ffn0(b, par):
                freed(dve, "x3", b, 2)
                freed(dve, "xh", b, 1)
                ready(dve, "zq", b)
                dve.scalar_tensor_tensor(out=x2[:, par, :], in0=zq[:, :], scalar=fac[:, G_OUT:G_OUT + 1],
                                         in1=x1[:, par, :], op0=ALU.mult, op1=ALU.add).then_inc(S["x2"], 1)
                ready(dve, "x2", b)
                stats(x2[:, par, :], st2, mv2, "st2", "mv2", b)

            def ln2(b, par):
                freed(dve, "xht_mm", b, 1)
                ready(dve, "rs2", b)
                dve.tensor_scalar(xh[:, :], x2[:, par, :], mv2[:, 0:1], rs2[:, 6:7], ALU.subtract, ALU.mult)\
                    .then_inc(S["xh"], 1)

            def q1_rest(b, par):
                freed(dve, "q1_lo", b, 1)
                ready(dve, "q1_hi", b)
                dve.tensor_tensor(q1r[:, :], QP1[:, :], s1q[:, 0, :], ALU.subtract).then_inc(S["q1_r"], 1)

            def add_att1(b, par):
                freed(dve, "xo", b, 1)
                freed(dve, "xl", b, 1)
                ready(dve, "wo_mm", b)
                dve.scalar_tensor_tensor(out=x3[:, :], in0=WO[:, :], scalar=gain[:, 1:2], in1=x2[:, par, :],
                                         op0=ALU.mult, op1=ALU.add).then_inc(S["x3"], 1)
                ready(dve, "x3", b)
                stats(x3[:, :], st3, mv3, "st3", "mv3", b)

            def ln3(b, par):
                freed(dve, "xlt_mm", b, 1)
                ready(dve, "rs3", b)
                dve.tensor_scalar(xl[:, :], x3[:, :], mv3[:, 0:1], rs3[:, 1:2], ALU.subtract, ALU.mult)\
                    .then_inc(S["xl"], 1)

            def router_max(b, par):
                freed(dve, "el", b, 1)
                ready(dve, "lg_mm", b)
                dve.tensor_tensor(lg[:, :], LG[:, LOW:LOW + EXPERTS], row[:, 7:15], ALU.add).then_inc(S["lg"], 1)
                ready(dve, "lg", b)
                dve.tensor_reduce(nml[:, :], lg[:, :], AX_X, ALU.max, negate=True).then_inc(S["nml"], 1)

            def router_weigh(b, par):
                ready(dve, "el", b)
                dve.reciprocal(rl[:, :], sl[:, :]).then_inc(S["rl"], 1)
                ready(dve, "rl", b)
                dve.tensor_scalar(wl[:, :], el[:, :], rl[:, 0:1], None, ALU.mult).then_inc(S["wl"], 1)
                freed(dve, "ls_mm", b, 1)
                ready(dve, "wl", b)
                dve.tensor_tensor(ls[:, :].rearrange("p (e r) -> p e r", e=EXPERTS),
                                  LG[:, 0:LOW].rearrange("p (e r) -> p e r", e=EXPERTS),
                                  wl[:, :].unsqueeze(2).to_broadcast([P, EXPERTS, RANK]), ALU.mult)\
                    .then_inc(S["ls"], 1)

            def add_ffn1(b, par):
                freed(dve, "out", b, 2)
                ready(dve, "up_mm", b)
                dve.scalar_tensor_tensor(out=xo[:, par, :], in0=UP[:, :], scalar=fac[:, G_UP:G_UP + 1],
                                         in1=x3[:, :], op0=ALU.mult, op1=ALU.add).then_inc(S["xo"], 1)

            def weights(b, par):
                dve.wait_ge(w_late, 16 * 7)
                for c in range(NCH):
                    last = dve.tensor_scalar(wq1[:, c, :], wq1[:, c, :], cols[:, LNW + c:LNW + c + 1], None, ALU.mult)
                last.then_inc(wq1_ok, 1)
                w = wf8[:, :, :].rearrange("p c n -> p (c n)")
                dve.tensor_scalar(w, w, fac[:, INV_W:INV_W + 1], FP8_MAX, ALU.mult, ALU.min).then_inc(w8_step, 1)
                dve.wait_ge(w8_step, 1)
                dve.tensor_scalar(w, w, -FP8_MAX, None, ALU.max).then_inc(w8_step, 1)
                dve.wait_ge(w8_step, 2)
                m = Q1[:, :, :, :].rearrange("p a k n -> p (a k n)").bitcast(F32)[:, 0:NCH * DM]
                binade(m, w).then_inc(w8_step, 1)
                dve.wait_ge(w8_step, 3)
                rounder(m, m).then_inc(w8_step, 1)
                dve.wait_ge(w8_step, 4)
                dve.tensor_tensor(w, w, m, ALU.add).then_inc(w8_step, 1)
                dve.wait_ge(w8_step, 5)
                dve.tensor_tensor(wf8q[:, :, :].rearrange("p c n -> p (c n)"), w, m, ALU.subtract)\
                    .then_inc(w8_step, 1)
                dve.wait_ge(w8_step, 6)
                dve.memset(Q1[ROW_MAX:P, :, :, :], 0.0).then_inc(w8_step, 1)

            dve.memset(O[:, :], 0.0).then_inc(o_clear, 1)
            dve.wait_ge(w_early, 16 * 6)
            dve.tensor_copy(identb[:, :], ident[:, :]).then_inc(idb_ok, 1)
            for k, s in ((INV_IN, 4), (INV_W, 5), (INV_OUT, 6)):
                dve.reciprocal(fac[:, k:k + 1], row[:, s:s + 1]).then_inc(fac_ok, 1)
            dve.tensor_tensor(fac[:, PROD:PROD + 1], row[:, 4:5], row[:, 5:6], ALU.mult).then_inc(fac_ok, 1)
            dve.wait_ge(fac_ok, 4)
            dve.wait_ge(gains_ok, 1)
            dve.tensor_tensor(fac[:, F_OUT:F_OUT + 1], fac[:, PROD:PROD + 1], fac[:, INV_OUT:INV_OUT + 1],
                              ALU.mult).then_inc(fac_ok, 1)
            dve.tensor_tensor(fac[:, G_OUT:G_OUT + 1], gain[:, 2:3], row[:, 6:7], ALU.mult).then_inc(fac_ok, 1)
            dve.tensor_scalar(fac[:, G_UP:G_UP + 1], gain[:, 3:4], EXPERT_GAIN, None, ALU.mult).then_inc(fac_ok, 1)
            dve.wait_ge(fac_ok, 7)

            def slot(u, par):
                step(ln2, u, par, 3)
                step(add_att1, u, par, 4)
                step(q1_rest, u, par, 3)
                step(ln3, u, par, 4)
                step(ln0_stats, u, par, 0)
                step(k1_rest, u, par, 2)
                step(norm0, u, par, 2, 0)
                if isinstance(u, int) and u == 1:
                    weights(0, 0)
                step(max1, u, par, 3, 0)
                step(norm0, u, par, 2, 1)
                for k in range(1, 8):
                    step(max1, u, par, 3, k)
                step(minus_max1, u, par, 3)
                step(ln0, u, par, 0)
                step(add_att0, u, par, 2)
                step(router_max, u, par, 4)
                step(max0, u, par, 1, 0)
                step(max0, u, par, 1, 1)
                step(quant_in, u, par, 2)
                step(qk_bias, u, par, 0)
                step(max0, u, par, 1, 2)
                step(router_weigh, u, par, 4)
                for k in range(3, 6):
                    step(max0, u, par, 1, k)
                step(quant_out, u, par, 2)
                step(max0, u, par, 1, 6)
                step(norm1, u, par, 3, 0)
                step(max0, u, par, 1, 7)
                step(norm1, u, par, 3, 1)
                step(minus_max0, u, par, 1)
                step(add_ffn0, u, par, 2)
                step(add_ffn1, u, par, 4)

            slots(dve, slot)

        @block.gpsimd
        def _(pool):
            def rsqrt(rs, mv, s_mv, s_ve, s_rs, b):
                ready(pool, s_mv, b)
                pool.sem_inc(pool_mark, 1)
                pool.tensor_scalar(rs[:, 0:1], mv[:, 1:2], EPS, None, ALU.add).then_inc(S[s_ve], 1)
                ready(pool, s_ve, b)
                pool.tensor_tensor(rs[:, 1:2], rs[:, 0:1], halfm[:, :], ALU.pow).then_inc(S[s_rs], 1)

            def keep_rows(b, par):
                freed(pool, "qk", b, 1)
                freed(pool, "mrow_in", b, 1)
                loaded(pool, "ld_maska", b, par)
                pool.sem_inc(pool_mark, 1)
                pool.tensor_scalar(keep[:, :], maska[:, par, :], 0.0, cols[:, QROW:QROW + 1], ALU.is_gt, ALU.max)\
                    .then_inc(S["keep"], 1)
                ready(pool, "keep", b)
                pool.sem_inc(pool_mark, 1)
                pool.tensor_scalar(mrow[:, :], keep[:, :], -1.0, MASKED, ALU.add, ALU.mult).then_inc(S["mrow"], 1)

            def rs0_(b, par):
                rsqrt(rs0, mv0, "mv0", "ve0", "rs0", b)

            def rs3_(b, par):
                rsqrt(rs3, mv3, "mv3", "ve3", "rs3", b)

            def qk_rest(b, par):
                freed(pool, "qk_mid", b, 1)
                freed(pool, "qk_lo", b, 1)
                ready(pool, "qk_hi", b)
                pool.tensor_tensor(qkr[:, :], qk[:, :], s0[:, 0, :], ALU.subtract).then_inc(S["qk_r"], 1)

            def qk_low(b, par):
                ready(pool, "qk_mid", b)
                pool.tensor_tensor(s0[:, 2, :], qkr[:, :], s0[:, 1, :], ALU.subtract).then_inc(S["qk_lo"], 1)

            def k1_low(b, par):
                ready(pool, "k1_mid", b)
                pool.tensor_tensor(s1k[:, 2, :], k1r[:, :], s1k[:, 1, :], ALU.subtract).then_inc(S["k1_lo"], 1)

            def q1_low(b, par):
                ready(pool, "q1_mid", b)
                pool.tensor_tensor(s1q[:, 2, :], q1r[:, :], s1q[:, 1, :], ALU.subtract).then_inc(S["q1_lo"], 1)

            def rs1_(b, par):
                rsqrt(rs1, mv1, "mv1", "ve1", "rs1", b)
                ready(pool, "rs1", b)
                pool.tensor_tensor(rs1[:, 2:3], rs1[:, 1:2], fac[:, INV_IN:INV_IN + 1], ALU.mult)\
                    .then_inc(S["rsi1"], 1)

            def round_in(b, par):
                ready(pool, "ym", b)
                pool.tensor_tensor(yt[:, :], ya[:, :], ye[:, :], ALU.add).then_inc(S["yt"], 1)
                freed(pool, "yqt_mm", b, 1)
                ready(pool, "yt", b)
                pool.tensor_tensor(yq[:, :], yt[:, :], ye[:, :], ALU.subtract).then_inc(S["yq"], 1)

            def round_out(b, par):
                ready(pool, "zm", b)
                pool.tensor_tensor(zt[:, :], za[:, :], ze[:, :], ALU.add).then_inc(S["zt"], 1)
                freed(pool, "x2", b, 1)
                ready(pool, "zt", b)
                pool.tensor_tensor(zq[:, :], zt[:, :], ze[:, :], ALU.subtract).then_inc(S["zq"], 1)

            def rs2_(b, par):
                r = rs2
                ready(pool, "mv2", b)
                pool.sem_inc(pool_mark, 1)
                pool.tensor_scalar(r[:, 0:1], mv2[:, 1:2], EPS, None, ALU.add).then_inc(S["rs2"], 1)
                ready(pool, "rs2", b, 1)
                pool.tensor_tensor(r[:, 1:2], r[:, 0:1], halfm[:, :], ALU.pow).then_inc(S["rs2"], 1)
                ready(pool, "rs2", b, 2)
                pool.tensor_tensor(r[:, 2:3], r[:, 1:2], r[:, 1:2], ALU.mult).then_inc(S["rs2"], 1)
                ready(pool, "rs2", b, 3)
                pool.tensor_tensor(r[:, 3:4], mv2[:, 1:2], r[:, 2:3], ALU.mult).then_inc(S["rs2"], 1)
                ready(pool, "rs2", b, 4)
                pool.sem_inc(pool_mark, 1)
                pool.tensor_scalar(r[:, 4:5], r[:, 3:4], EPS, None, ALU.add).then_inc(S["rs2"], 1)
                ready(pool, "rs2", b, 5)
                pool.tensor_tensor(r[:, 5:6], r[:, 4:5], halfm[:, :], ALU.pow).then_inc(S["rs2"], 1)
                ready(pool, "rs2", b, 6)
                pool.tensor_tensor(r[:, 6:7], r[:, 5:6], r[:, 1:2], ALU.mult).then_inc(S["rs2"], 1)

            fills = [(Q0[:, :, :, :], 0.0), (K0[:, :, :, :], 0.0), (V0[:, :, :, :, DH0:DH0 + 1], 1.0),
                     (V1[:, :, :, DH1:DH1 + 1], 1.0), (halfm[:, :], -0.5), (K1[ROW_MAX:P, :, :, :], 1.0),
                     (Q0[ROW_MASK:ROW_MAX, :, :, :], 1.0), (K0[ROW_MAX:P, :, :, :], 1.0)]
            assert len(fills) == FILLS
            for n, (part, value) in enumerate(fills):
                if n:
                    pool.wait_ge(zeroed, n)
                pool.memset(part, value).then_inc(zeroed, 1)
            pool.wait_ge(zeroed, FILLS)
            pool.wait_ge(w_early, 16 * 6)
            pool.wait_ge(fac_ok, 7)

            def slot(u, par):
                step(keep_rows, u, par, 1)
                step(k1_low, u, par, 3)
                step(rs1_, u, par, 3)
                step(round_in, u, par, 3)
                step(round_out, u, par, 3)
                step(qk_rest, u, par, 1)
                step(rs2_, u, par, 3)
                step(q1_low, u, par, 3)
                step(rs3_, u, par, 4)
                step(rs0_, u, par, 0)
                step(qk_low, u, par, 1)

            slots(pool, slot)


_SPECS = ["x", "ctx", "ctxt", "mask", "ident", "wqk0", "wv0", "wo0", "cols", "row", "wf8", "wq1", "wk1", "wv1",
          "wo1", "wlow", "wup"]


def kernel(**inputs):
    import numpy as np
    import concourse.bacc as bacc
    from concourse.bass_utils import run_bass_kernel_spmd

    a = {k: np.asarray(v) for k, v in inputs.items()}

    def chunks(w):
        return w.T.reshape(NCH, P, w.shape[0]).transpose(1, 0, 2)

    def col(*parts):
        return np.concatenate([np.asarray(p).reshape(-1) for p in parts]).reshape(P, 1)

    rows_q = np.concatenate([np.ones(E0, np.float32), np.zeros(E0, np.float32)])
    wq0, wk0 = (a[n].reshape(H0, DH0, P).transpose(1, 0, 2).reshape(E0, P) for n in ("L0_xattn_Wq", "L0_xattn_Wk"))
    bq0, bk0 = (a[n].reshape(H0, DH0).T for n in ("L0_xattn_bq", "L0_xattn_bk"))
    wq1 = a["L1_xattn_wq"].reshape(KV, REP, DH1, DM).transpose(1, 2, 0, 3).reshape(DM, DM)
    wk1 = a["L1_xattn_wk"].reshape(KV, DH1, DM).transpose(1, 0, 2).reshape(P, DM)
    wo0 = a["L0_xattn_Wo"].T
    zero0 = np.zeros_like(wo0)
    low = np.concatenate([a["L1_ffn_A"].reshape(LOW, DM), a["L1_ffn_Wr"]], axis=0)
    arrays = {
        "x": a["x"],
        "ctx": a["ctx_4096"],
        "ctxt": a["ctx_4096"].transpose(0, 2, 1).reshape(BATCH, NCH, P, P).transpose(0, 2, 1, 3),
        "mask": a["mask_Bx1x4096_ff1"].reshape(BATCH, DM),
        "ident": np.eye(P, dtype=np.float32),
        "wqk0": np.concatenate([wq0.T, wk0.T], axis=1),
        "wv0": a["L0_xattn_Wv"].T,
        "wo0": np.stack([np.concatenate([wo0, zero0]), np.concatenate([zero0, wo0])], axis=1),
        "cols": np.concatenate([col(bq0, bk0), col(a["L0_xattn_bv"], a["L0_xattn_bv"]),
                                col(a["L0_xattn_bo"]), col(rows_q), a["L1_xattn_ln_w"].reshape(NCH, P).T], axis=1),
        "row": np.concatenate([a["g_xattn"], a["g_ffn"], a["L0_ffn_input_scale"].reshape(1),
                               a["L0_ffn_weight_scale"].reshape(1), a["L0_ffn_output_scale"].reshape(1),
                               a["L1_ffn_br"]]),
        "wf8": chunks(a["L0_ffn_w"]),
        "wq1": chunks(wq1),
        "wk1": chunks(wk1),
        "wv1": chunks(a["L1_xattn_wv"]),
        "wo1": chunks(a["L1_xattn_wo"]),
        "wlow": chunks(low),
        "wup": a["L1_ffn_B"].transpose(0, 2, 1).reshape(LOW, DM),
    }
    arrays = {k: np.ascontiguousarray(v) for k, v in arrays.items()}
    nc = bacc.Bacc("TRN2", target_bir_lowering=False, num_devices=1)
    t = {k: nc.dram_tensor("in_" + k, arrays[k].shape, F32, kind="ExternalInput").ap() for k in _SPECS}
    t["out"] = nc.dram_tensor("out_x", (BATCH, P, DM), F32, kind="ExternalOutput").ap()
    flamingo_block(nc, t)
    r = run_bass_kernel_spmd(nc, [{"in_" + k: arrays[k] for k in _SPECS}], core_ids=[0])
    return r.results[0]["out_x"]
```

```python
from contextlib import ExitStack

import concourse.bass as bass
import numpy as np
from concourse import mybir
from concourse.alu_op_type import AluOpType as ALU

ACT = mybir.ActivationFunctionType
AX_X = mybir.AxisListType.X
F32 = mybir.dt.float32
BF16 = mybir.dt.bfloat16
I32 = mybir.dt.int32

P = 128
BATCH = 8
DM = 512
NCH = DM // P
HALF = DM // 2
WIN = DM // P
H0 = 8
DH0 = 8
E0 = H0 * DH0
KV = 8
REP = 4
DH1 = 16
HQ = KV * REP
EXPERTS = 8
RANK = 16
LOW = EXPERTS * RANK
EXPERT_GAIN = EXPERTS * 2.0
EPS = 1e-5
FP8_MAX = 448.0
FP8_LEAST = 2.0 ** -6
FP8_STEP = 1.5 * 2.0 ** 20
MASKED = 998244352.0

PAIRS = [(0, 1), (0, 0), (0, 2), (1, 0), (1, 1), (2, 0)]
ROWS0 = len(PAIRS) * DH0
ROWS1 = len(PAIRS) * DH1
ROW_MASK = 64
ROW_MAX = 96
assert ROWS0 <= ROW_MASK and ROWS1 <= ROW_MAX

TILES = 8
SC0_LAG, ST0_LAG, SC1_LAG, ST1_LAG = 0, 1, 3, 4
LAST = 4
SLOTS = BATCH + LAST
FILLS = 5
HEAD = 2


def flamingo_block(nc, t):
    with ExitStack() as ctx:
        def sb(name, shape, dt=F32):
            return ctx.enter_context(nc.sbuf_tensor(name, shape, dt))

        def bank(name):
            return ctx.enter_context(nc.psum_tensor(name, [P, DM], F32))

        def sem(name):
            return ctx.enter_context(nc.semaphore(name))

        ident = sb("ident", [P, P])
        identb = sb("identb", [P, P], BF16)
        wqk0 = sb("wqk0", [P, 2 * E0])
        wv0 = sb("wv0", [P, E0])
        wo0 = sb("wo0", [P, 2, P])
        cols = sb("cols", [P, 4 + NCH])
        BQK, BV, BO, QROW, LNW = 0, 1, 2, 3, 4
        row = sb("row", [P, 15])
        wf8 = sb("wf8", [P, NCH, DM])
        wf8q = sb("wf8q", [P, NCH, DM], BF16); wf8m = sb("wf8m", [P, DM])
        wq1 = sb("wq1", [P, NCH, DM])
        wk1 = sb("wk1", [P, NCH, P])
        wv1 = sb("wv1", [P, NCH, P])
        wo1 = sb("wo1", [P, NCH, DM])
        wlow = sb("wlow", [P, NCH, LOW + EXPERTS])
        wup = sb("wup", [P, DM])
        gain = sb("gain", [P, 4])
        fac = sb("fac", [P, 8])
        INV_IN, INV_W, INV_OUT, F_OUT, G_OUT, G_UP, PROD = range(7)

        halfm = sb("halfm", [P, 1])

        xa = sb("xa", [P, 2, DM])
        ctxa = sb("ctxa", [P, 2, DM])
        maska = sb("maska", [P, 2, DM])
        keep = sb("keep", [P, DM])
        mrow = sb("mrow", [P, DM], BF16)
        bn0 = sb("bn0", [P, 6]); mv0 = sb("mv0", [P, 2]); ve0 = sb("ve0", [P, 1]); rs0 = sb("rs0", [P, 1])
        xln0 = sb("xln0", [P, DM])
        qk = sb("qk", [P, DM]); qkr = sb("qkr", [P, DM])
        s0 = sb("s0", [P, 3, DM], BF16)
        Q0 = sb("Q0", [P, 2, H0, DM], BF16)
        K0 = sb("K0", [P, 2, H0, DM], BF16)
        V0 = sb("V0", [P, 2, WIN, H0, DH0 + 1])
        nm0 = sb("nm0", [P, H0, WIN])
        nh0 = sb("nh0", [P, 2, H0, WIN], BF16)
        mt0 = sb("mt0", [2 * H0 * WIN, P], BF16)
        AT = sb("AT", [P, TILES, DM])
        os0 = sb("os0", [P, DM]); rc0 = sb("rc0", [P, 16])
        on0 = sb("on0", [P, WIN, E0])
        G = sb("G", [P, 2, 2, P])
        xb = sb("xb", [P, 2, DM])
        maskb = sb("maskb", [P, 2, DM])
        ctxt = sb("ctxt", [P, 2, NCH, P])
        x1 = sb("x1", [P, 2, DM])
        bn1 = sb("bn1", [P, 6]); mv1 = sb("mv1", [P, 2]); ve1 = sb("ve1", [P, 1]); rs1 = sb("rs1", [P, 2])
        ya = sb("ya", [P, DM]); ye = sb("ye", [P, DM])
        yq = sb("yq", [P, DM], BF16)
        yqt = sb("yqt", [P, NCH, P], BF16)
        za = sb("za", [P, DM]); ze = sb("ze", [P, DM])
        zq = sb("zq", [P, DM])
        x2 = sb("x2", [P, 2, DM])
        bn2 = sb("bn2", [P, 6]); mv2 = sb("mv2", [P, 2]); ve2 = sb("ve2", [P, 1]); rs2 = sb("rs2", [P, 1])
        xh = sb("xh", [P, DM]); xht = sb("xht", [P, NCH, P])
        s1q = sb("s1q", [P, 3, DM], BF16); q1r = sb("q1r", [P, DM])
        s1k = sb("s1k", [P, 3, P], BF16); k1r = sb("k1r", [P, P])
        Q1 = sb("Q1", [P, 2, KV, DM], BF16)
        K1 = sb("K1", [P, 2, KV, P], BF16)
        V1 = sb("V1", [P, 2, KV, DH1 + 1])
        nm1 = sb("nm1", [P, HQ]); nh1 = sb("nh1", [P, 2, HQ], BF16)
        mt1 = sb("mt1", [2 * HQ, P], BF16)
        os1 = sb("os1", [P, DM]); rc1 = sb("rc1", [P, 16])
        on1 = sb("on1", [P, KV, REP, DH1]); ont1 = sb("ont1", [P, NCH, P])
        x3 = sb("x3", [P, DM])
        bn3 = sb("bn3", [P, 6]); mv3 = sb("mv3", [P, 2]); ve3 = sb("ve3", [P, 1]); rs3 = sb("rs3", [P, 1])
        xl = sb("xl", [P, DM]); xlt = sb("xlt", [P, NCH, P])
        lg = sb("lg", [P, EXPERTS]); nml = sb("nml", [P, 1]); el = sb("el", [P, EXPERTS])
        sl = sb("sl", [P, 1]); rl = sb("rl", [P, 1]); wl = sb("wl", [P, EXPERTS])
        ls = sb("ls", [P, LOW]); lst = sb("lst", [P, P])
        xo = sb("xo", [P, 2, DM])

        SC = [bank("SC0"), bank("SC1")]
        ST = [bank("ST0"), bank("ST1")]
        O = bank("O")
        PA, PB, PC = bank("PA"), bank("PB"), bank("PC")
        V0P = ONT0 = XHT = ONT1 = WO = XLT = LG = PA[:, :]
        Y = YQT = Z = MT1 = OT1 = LS = UP = PB[:, :]
        QK = MT0 = OT0 = KV1 = QP1 = PC[:, :]

        w_early = sem("w_early")
        W = {n: sem("w_" + n) for n in ("wk1", "wv1", "wf8", "wq1", "wo1", "wlow", "wup")}
        zeroed = sem("zeroed"); ones_in = sem("ones_in"); gains_ok = sem("gains_ok"); fac_ok = sem("fac_ok")
        half_ok = sem("half_ok"); q1_ones = sem("q1_ones"); w8_step = sem("w8_step")
        wq1_ok = sem("wq1_ok"); idb_ok = sem("idb_ok")
        o_clear = sem("o_clear")
        sp_mark = sem("sp_mark"); pe_mark = sem("pe_mark"); dve_mark = sem("dve_mark"); pool_mark = sem("pool_mark")

        D = 16
        PER = dict(
            bn0=1, mv0=1, rs0=1, xln0=1, keep=1, mrow=1, mrow_in=D, qk_mm=1, qk=1, qk_hi=1, qk_r=1,
            qk_mid=1, qk_lo=1, qk_out=6 * D, q0_in=D, k0_in=D, v0_mm=1, v0=1, nh0=1, nl0=1, mt0_mm=1, mt0=1,
            mt0_out=D, mt0_in=D, os0=2, ot0_mm=2, rc0=2, on0=2, ont0_mm=1, gelu=1, kv1_mm=1, k1_hi=1,
            k1_r=1, k1_mid=1, k1_lo=1, k1_out=3 * D, k1_in=D, v1=1, y_mm=1, xr=1, x1=1, bn1=1, mv1=1, rs1=1,
            rsi1=1, ya=1, yc=1, ye=1, ym=1, yt=1, yq=1, yt_r=1, yq_r=1, yqt_mm=1, yqt=1, z_mm=1, za=1, zc=1,
            ze=1, zm=1, zt=1, zq=1, zt_r=1, zq_r=1, x2=1, bn2=1, mv2=1, rs2=1, ve0=1, ve1=1, ve2=1, ve3=1,
            xh=1, xht_mm=1, xht=1, q1_mm=1, q1_hi=1, q1_r=1, q1_mid=1, q1_lo=1, q1_out=3 * D, q1_in=D,
            q1_in_b=D, nh1=1, nl1=1, mt1_mm=1, mt1=1, mt1_out=D, mt1_in=D, os1=2, ot1_mm=2, rc1=2, on1=2,
            ont1_mm=1, ont1=1, wo_mm=1, x3=1, bn3=1, mv3=1, rs3=1, xl=1, xlt_mm=1, xlt=1, lg_mm=1, lg=1,
            nml=1, el=1, rl=1, wl=1, ls=1, ls_mm=1, lst=1, up_mm=1, xo=1, out=D, st0_done=1, st1_done=1)
        S = {n: sem("s_" + n) for n in PER}
        LD = {n: [sem(n + "_even"), sem(n + "_odd")] for n in
              ("ld_xa", "ld_ctxa", "ld_maska", "ld_xb", "ld_maskb", "ld_ctxt")}
        sc_ready, sc_read = sem("sc_ready"), sem("sc_read")
        st_ready, st_read = sem("st_ready"), sem("st_read")
        pv_done, o_read = sem("pv_done"), sem("o_read")

        d_q0 = nc.dram_tensor("d_q0", [len(PAIRS), E0, DM], BF16, kind="Internal").ap()
        d_k0 = nc.dram_tensor("d_k0", [len(PAIRS), E0, DM], BF16, kind="Internal").ap()
        d_m0 = nc.dram_tensor("d_m0", [2, H0 * WIN * P], BF16, kind="Internal").ap()
        d_q1 = nc.dram_tensor("d_q1", [len(PAIRS), P, DM], BF16, kind="Internal").ap()
        d_k1 = nc.dram_tensor("d_k1", [len(PAIRS), P, P], BF16, kind="Internal").ap()
        d_m1 = nc.dram_tensor("d_m1", [2, HQ * P], BF16, kind="Internal").ap()

        RAISED = """xln0 keep v0_mm kv1_mm xr x1 q0_in k0_in st0_done st1_done gelu q1_r xo qk_out os0 k1_out mt0_out
        mt1_out ot0_mm ot1_mm y_mm q1_out qk_mm qk_r mt0_mm mt1_mm ont0_mm ont1_mm k1_lo yq zq x3
        xht_mm q1_lo xlt_mm el ls_mm out yq_r zq_r nl0 nl1 mt0_in mt1_in q1_in q1_in_b k1_in ya z_mm
        xh q1_mm wo_mm xl lg_mm wl up_mm qk mrow_in qk_mid qk_lo yqt_mm x2 v0 k1_r mt0 on0 yqt za
        xht mt1 on1 ont1 xlt ls lst""".split()

        def ready(eng, name, b, k=None):
            per = PER[name]
            eng.wait_ge(S[name], b * per + ((HEAD * per if name in RAISED else 0) + (per if k is None else k)))

        def loaded(eng, name, b, par):
            eng.wait_ge(LD[name][par], b * 8 + (16 - 8 * par))

        def freed(eng, name, b, back):
            per = PER[name]
            assert name in RAISED and back <= HEAD
            eng.wait_ge(S[name], b * per + (HEAD - back + 1) * per)

        def at_least(eng, s, value):
            if not (isinstance(value, int) and value <= 0):
                eng.wait_ge(s, value)

        def count(b, layer, lag0, lag1):
            own, other = (lag0, lag1) if layer == 0 else (lag1, lag0)
            if isinstance(b, int):
                seen = b + own - other + (1 if layer == 0 else 0)
                return TILES * (b + min(max(seen, 0), BATCH))
            return b * (2 * TILES) + TILES * (own - other + (1 if layer == 0 else 0))

        def sc_no(b, layer):
            return count(b, layer, SC0_LAG, SC1_LAG)

        def st_no(b, layer):
            return count(b, layer, ST0_LAG, ST1_LAG)

        def half_no(b, layer):
            n = st_no(b, layer)
            if isinstance(b, int):
                return n // 4
            own, other = (ST0_LAG, ST1_LAG) if layer == 0 else (ST1_LAG, ST0_LAG)
            return b * (2 * TILES // 4) + TILES // 4 * (own - other + (1 if layer == 0 else 0))

        def take(pe, u, readers, n):
            here, before = readers[:n][::-1], readers[::-1]
            if not isinstance(u, int):
                name, lag, *k = here[0] if here else before[0]
                ready(pe, name, u - (lag if here else lag + 1), *k)
                return
            for name, lag, *k in here + [(r[0], r[1] + 1, *r[2:]) for r in before]:
                if 0 <= u - lag < BATCH:
                    ready(pe, name, u - lag, *k)
                    return
            for name, lag, *k in before:
                if u - 1 - lag >= BATCH:
                    ready(pe, name, BATCH - 1)

        def step(f, u, par, lag, *args):
            b = u - lag
            if not isinstance(b, int) or 0 <= b < BATCH:
                f(b, (par - lag) % 2, *args)

        def once(f, u, at, *args):
            if isinstance(u, int) and u == at:
                f(0, 0, *args)

        def is_first(b):
            return isinstance(b, int) and b == 0

        def slots(eng, slot):
            for u in range(LAST):
                slot(u, u % 2)
            with eng.Fori(0, (BATCH - LAST) // 2) as i:
                for par in range(2):
                    slot(i * 2 + (LAST + par), par)
            for u in range(BATCH, SLOTS):
                slot(u, u % 2)

        def fill(eng, tiles, value, done=zeroed):
            pair = {0.0: 0.0, 1.0: float(np.array([0x3F803F80], np.uint32).view(np.float32)[0])}
            eng.memset(tiles[:, :, :, :].rearrange("p a h w -> p (a h w)").bitcast(F32), pair[value])\
                .then_inc(done, 1)

        block = ctx.enter_context(nc.Block())

        @block.sync
        def _(sp):
            def settle():
                sp.sem_inc(sp_mark, 1)

            def ld_a(b, par):
                if not is_first(b):
                    freed(sp, "xln0", b, 2)
                    settle()
                    sp.dma_start(xa[:, par, :], t["x"][b, :, :]).then_inc(LD["ld_xa"][par], 16)
                freed(sp, "keep", b, 2)
                settle()
                sp.dma_start(maska[:, par, :], t["mask"][b, :].partition_broadcast(P))\
                    .then_inc(LD["ld_maska"][par], 16)
                freed(sp, "v0_mm", b, 2)
                settle()
                sp.dma_start(ctxa[:, par, :], t["ctx"][b, :, :]).then_inc(LD["ld_ctxa"][par], 16)

            def ld_b(b, par):
                freed(sp, "kv1_mm", b, 2)
                settle()
                sp.dma_start(ctxt[:, par, :, :], t["ctxt"][b, :, :, :]).then_inc(LD["ld_ctxt"][par], 16)
                freed(sp, "xr", b, 2)
                settle()
                sp.dma_start(maskb[:, par, :], t["mask"][b, :].partition_broadcast(P))\
                    .then_inc(LD["ld_maskb"][par], 16)
                freed(sp, "x1", b, 2)
                settle()
                sp.dma_start(xb[:, par, :], t["x"][b, :, :]).then_inc(LD["ld_xb"][par], 16)

            def part(src, n):
                p, w = src.shape
                return src.unsqueeze(1).to_broadcast([p, n, w])

            def qk0_out(b, par, k):
                ready(sp, ("qk_hi", "qk_mid", "qk_lo")[k], b)
                settle()
                if k == 0:
                    freed(sp, "q0_in", b, 1)
                    settle()
                    freed(sp, "k0_in", b, 1)
                settle()
                first = (slice(0, 3), slice(3, 5), slice(5, 6))[k]
                second = (slice(1, 6, 2), slice(0, 5, 4), slice(2, 3))[k]
                sp.dma_start(d_q0[first, :, :].rearrange("c r w -> r c w"), part(s0[0:E0, k, :], 3 - k))\
                    .then_inc(S["qk_out"], 16)
                sp.dma_start(d_k0[second, :, :].rearrange("c r w -> r c w"), part(s0[E0:P, k, :], 3 - k))\
                    .then_inc(S["qk_out"], 16)

            def qk0_in(b, par):
                if is_first(b):
                    sp.wait_ge(zeroed, FILLS)
                freed(sp, "st0_done", b, 2)
                settle()
                ready(sp, "qk_out", b)
                settle()
                sp.dma_start(Q0[0:ROWS0, par, :, :], d_q0.rearrange("c (d h) w -> (c d) h w", h=H0))\
                    .then_inc(S["q0_in"], 16)
                sp.dma_start(K0[0:ROWS0, par, :, :], d_k0.rearrange("c (d h) w -> (c d) h w", h=H0))\
                    .then_inc(S["k0_in"], 16)

            def mask_in(b, par):
                if is_first(b):
                    sp.wait_ge(zeroed, FILLS)
                ready(sp, "mrow", b)
                settle()
                freed(sp, "st0_done", b, 2)
                settle()
                sp.dma_start(K0[ROW_MASK:ROW_MASK + 1, par, :, :], part(mrow[E0:E0 + 1, :], H0))\
                    .then_inc(S["mrow_in"], 16)

            def m0_row(b, par):
                freed(sp, "mt0_in", b, 1)
                settle()
                ready(sp, "mt0", b)
                settle()
                sp.dma_start(d_m0.rearrange("a (r i) -> (a r) i", i=P), mt0[:, :]).then_inc(S["mt0_out"], 16)
                ready(sp, "mt0_out", b)
                settle()
                sp.dma_start(Q0[ROW_MAX:ROW_MAX + 2, par, :, :], d_m0.rearrange("a (h w) -> a h w", h=H0))\
                    .then_inc(S["mt0_in"], 16)

            def k1_out(b, par):
                if is_first(b):
                    sp.wait_ge(zeroed, FILLS)
                freed(sp, "k1_in", b, 1)
                settle()
                ready(sp, "k1_lo", b)
                settle()
                for k, blocks in enumerate((slice(1, 6, 2), slice(0, 5, 4), slice(2, 3))):
                    sp.dma_start(d_k1[blocks, :, :].rearrange("c r w -> r c w"), part(s1k[:, k, :], 3 - k))\
                        .then_inc(S["k1_out"], 16)
                freed(sp, "st1_done", b, 2)
                settle()
                ready(sp, "k1_out", b)
                settle()
                sp.dma_start(K1[0:ROWS1, par, :, :], d_k1.rearrange("c (d k) w -> (c d) k w", k=KV))\
                    .then_inc(S["k1_in"], 16)

            def q1_out(b, par, k):
                ready(sp, ("q1_hi", "q1_mid", "q1_lo")[k], b)
                settle()
                if k == 0:
                    freed(sp, "q1_in", b, 1)
                    settle()
                    freed(sp, "q1_in_b", b, 1)
                settle()
                blocks = (slice(0, 3), slice(3, 5), slice(5, 6))[k]
                sp.dma_start(d_q1[blocks, :, :].rearrange("c r w -> r c w"), part(s1q[:, k, :], 3 - k))\
                    .then_inc(S["q1_out"], 16)

            def q1_in(b, par):
                if is_first(b):
                    sp.wait_ge(q1_ones, 1)
                freed(sp, "st1_done", b, 2)
                settle()
                ready(sp, "q1_out", b)
                settle()
                rows = d_q1.rearrange("c (d k) w -> (c d) k w", k=KV)
                sp.dma_start(Q1[0:ROWS1, par, 0:KV // 2, :], rows[:, 0:KV // 2, :]).then_inc(S["q1_in"], 16)
                sp.dma_start(Q1[0:ROWS1, par, KV // 2:, :], rows[:, KV // 2:, :]).then_inc(S["q1_in_b"], 16)

            def m1_row(b, par):
                freed(sp, "mt1_in", b, 1)
                settle()
                ready(sp, "mt1", b)
                settle()
                sp.dma_start(d_m1.rearrange("a (r i) -> (a r) i", i=P), mt1[:, :]).then_inc(S["mt1_out"], 16)
                ready(sp, "mt1_out", b)
                settle()
                sp.dma_start(Q1[ROW_MAX:ROW_MAX + 2, par, :, :], d_m1.rearrange("a (k w) -> a k w", k=KV))\
                    .then_inc(S["mt1_in"], 16)

            def store(b, par):
                ready(sp, "xo", b)
                settle()
                sp.dma_start(t["out"][b, :, :], xo[:, par, :]).then_inc(S["out"], 16)

            for name in RAISED:
                sp.sem_inc(S[name], HEAD * PER[name])
            sp.dma_start(xa[:, 0, :], t["x"][0, :, :]).then_inc(LD["ld_xa"][0], 16)
            for dst, src in ((cols[:, :], t["cols"]), (wqk0[:, :], t["wqk0"]),
                             (row[:, :], t["row"].partition_broadcast(P)),
                             (wv0[:, :], t["wv0"]), (ident[:, :], t["ident"]), (wo0[:, :, :], t["wo0"])):
                sp.dma_start(dst, src).then_inc(w_early, 16)

            def load_w(b, par, k):
                name, dst = (("wk1", wk1), ("wv1", wv1), ("wf8", wf8), ("wq1", wq1), ("wo1", wo1), ("wlow", wlow),
                             ("wup", wup))[k]
                sp.dma_start(dst[:], t[name]).then_inc(W[name], 16)

            def ones_rows(b, par):
                sp.wait_ge(zeroed, FILLS)
                sp.wait_ge(q1_ones, 1)
                ones = Q1[ROW_MAX:ROW_MAX + 2, :, :, :]
                sp.dma_start(K0[ROW_MAX:ROW_MAX + 2, :, :, :], ones).then_inc(ones_in, 16)
                sp.dma_start(K1[ROW_MAX:ROW_MAX + 2, :, :, :], ones[:, :, :, 0:P]).then_inc(ones_in, 16)
                sp.wait_ge(ones_in, 2 * 16)

            def slot(u, par):
                step(ld_a, u, par, 0)
                once(load_w, u, 0, 0)
                once(load_w, u, 0, 1)
                once(load_w, u, 1, 3)
                step(q1_out, u, par, 3, 0)
                once(load_w, u, 0, 2)
                step(q1_out, u, par, 3, 1)
                step(q1_out, u, par, 3, 2)
                step(m0_row, u, par, 1)
                once(load_w, u, 2, 4)
                step(q1_in, u, par, 3)
                step(mask_in, u, par, 0)
                for k in range(0, 3):
                    step(qk0_out, u, par, 0, k)
                once(load_w, u, 3, 6)
                step(qk0_in, u, par, 0)
                step(ld_b, u, par, 1)
                step(m1_row, u, par, 3)
                once(load_w, u, 2, 5)
                step(k1_out, u, par, 2)
                once(ones_rows, u, 0)
                step(store, u, par, 4)

            slots(sp, slot)
            sp.wait_ge(S["out"], (BATCH + HEAD) * 16)

        @block.tensor
        def _(pe):
            mm = pe.matmul

            def qk_mm(b, par):
                ready(pe, "xln0", b)
                mm(QK[:, :], wqk0[:, :], xln0[:, :], start=True, stop=True).then_inc(S["qk_mm"], 1)

            def v0_mm(b, par):
                loaded(pe, "ld_ctxa", b, par)
                for w in range(WIN):
                    last = mm(V0P[:, w * E0:(w + 1) * E0], ctxa[:, par, w * P:(w + 1) * P], wv0[:, :],
                              start=True, stop=True)
                last.then_inc(S["v0_mm"], 1)

            def kv1_mm(b, par):
                loaded(pe, "ld_ctxt", b, par)
                if is_first(b):
                    pe.wait_ge(W["wk1"], 16)
                    pe.wait_ge(W["wv1"], 16)
                for c in range(NCH):
                    last = mm(KV1[:, 0:P], wk1[:, c, :], ctxt[:, par, c, :], start=c == 0, stop=c == NCH - 1)
                for c in range(NCH):
                    last = mm(KV1[:, P:2 * P], ctxt[:, par, c, :], wv1[:, c, :], start=c == 0, stop=c == NCH - 1)
                last.then_inc(S["kv1_mm"], 1)

            def sc0(b, par, tile):
                if tile == 0:
                    ready(pe, "q0_in", b)
                    ready(pe, "k0_in", b)
                    ready(pe, "mrow_in", b)
                at_least(pe, sc_read, sc_no(b, 0) + (tile - 1))
                w, h0 = tile // 2, tile % 2 * 4
                for g in range(4):
                    last = mm(SC[tile % 2][:, g * P:(g + 1) * P], Q0[0:ROW_MAX, par, h0 + g, w * P:(w + 1) * P],
                              K0[0:ROW_MAX, par, h0 + g, w * P:(w + 1) * P], start=True, stop=True)
                last.then_inc(sc_ready, 1)

            def sc1(b, par, kv):
                if kv == 0:
                    ready(pe, "q1_in", b)
                    ready(pe, "k1_in", b)
                if kv == KV // 2:
                    ready(pe, "q1_in_b", b)
                at_least(pe, sc_read, sc_no(b, 1) + (kv - 1))
                for r in range(REP):
                    last = mm(SC[kv % 2][:, r * P:(r + 1) * P], Q1[0:ROW_MAX, par, kv, r * P:(r + 1) * P],
                              K1[0:ROW_MAX, par, kv, :], start=True, stop=True)
                last.then_inc(sc_ready, 1)

            def mt0_mm(b, par):
                if is_first(b):
                    pe.wait_ge(idb_ok, 1)
                ready(pe, "nl0", b)
                pe.sem_inc(pe_mark, 1)
                pe.transpose(MT0.bitcast(BF16)[0:2 * H0 * WIN, 0:P], nh0[:, :, :, :].rearrange("p a h w -> p (a h w)"),
                             identb[:, :]).then_inc(S["mt0_mm"], 1)

            def mt1_mm(b, par):
                if is_first(b):
                    pe.wait_ge(idb_ok, 1)
                ready(pe, "nl1", b)
                pe.sem_inc(pe_mark, 1)
                pe.transpose(MT1.bitcast(BF16)[0:2 * HQ, 0:P], nh1[:, :, :].rearrange("p a h -> p (a h)"),
                             identb[:, :]).then_inc(S["mt1_mm"], 1)

            def st0(b, par, k):
                if k == 0:
                    ready(pe, "mt0_in", b)
                    if is_first(b):
                        pe.wait_ge(ones_in, 2 * 16)
                at_least(pe, st_read, st_no(b, 0) + (k - 1))
                w, h0 = k // 2, k % 2 * 4
                for g in range(4):
                    last = mm(ST[k % 2][:, g * P:(g + 1) * P], K0[:, par, h0 + g, w * P:(w + 1) * P],
                              Q0[:, par, h0 + g, w * P:(w + 1) * P], start=True, stop=True)
                last.then_inc(st_ready, 1)

            def pv0(b, par, k):
                w, h0 = k // 2, k % 2 * 4
                if k == 0:
                    ready(pe, "v0", b)
                pe.wait_ge(st_read, st_no(b, 0) + (k + 1))
                if k % 4 == 0:
                    at_least(pe, o_read, half_no(b, 0) + k // 4)
                for g in range(4):
                    last = mm(O[32 * g:32 * g + DH0 + 1, k % 4 * P:(k % 4 + 1) * P], V0[:, par, w, h0 + g, :],
                              AT[:, k, g * P:(g + 1) * P], start=True, stop=True)
                last.then_inc(pv_done, 1)

            def st1(b, par, k):
                if k == 0:
                    ready(pe, "mt1_in", b)
                at_least(pe, st_read, st_no(b, 1) + (k - 1))
                mm(ST[k % 2][:, :], K1[:, par, k, :], Q1[:, par, k, :], start=True, stop=True).then_inc(st_ready, 1)

            def pv1(b, par, half):
                if half == 0:
                    ready(pe, "v1", b)
                pe.wait_ge(st_read, st_no(b, 1) + (4 * half + 4))
                at_least(pe, o_read, half_no(b, 1) + half)
                for g in range(4):
                    k = 4 * half + g
                    last = mm(O[32 * g:32 * g + DH1 + 1, :], V1[:, par, k, :], AT[:, k, :], start=True, stop=True)
                last.then_inc(pv_done, 4)

            def ot0_mm(b, par, half):
                ready(pe, "os0", b, half + 1)
                for k in range(4):
                    last = pe.transpose(OT0[:, k * P:(k + 1) * P], os0[:, k * P:(k + 1) * P], ident[:, :])
                last.then_inc(S["ot0_mm"], 1)

            def ot1_mm(b, par, half):
                ready(pe, "os1", b, half + 1)
                for r in range(REP):
                    last = pe.transpose(OT1[:, r * P:(r + 1) * P], os1[:, r * P:(r + 1) * P], ident[:, :])
                last.then_inc(S["ot1_mm"], 1)

            def ont0_mm(b, par):
                ready(pe, "on0", b)
                for k in range(2):
                    last = pe.transpose(ONT0[:, k * P:(k + 1) * P],
                                        on0[:, 2 * k:2 * k + 2, :].rearrange("p w e -> p (w e)"), ident[:, :])
                last.then_inc(S["ont0_mm"], 1)

            def y_mm(b, par):
                ready(pe, "gelu", b)
                out = Y[:, :].rearrange("p (a o i) -> p a o i", a=2, o=2)
                for o in range(2):
                    last = mm(out[:, :, o, :], wo0[:, o, :], G[:, par, :, :], start=True, stop=True)
                last.then_inc(S["y_mm"], 1)

            def yqt_mm(b, par):
                if is_first(b):
                    pe.wait_ge(idb_ok, 1)
                ready(pe, "yq", b)
                ready(pe, "yq_r", b)
                for c in range(NCH):
                    last = pe.transpose(YQT.bitcast(BF16)[:, c * P:(c + 1) * P],
                                        yq[:, c * P:(c + 1) * P], identb[:, :])
                last.then_inc(S["yqt_mm"], 1)

            def z_mm(b, par):
                ready(pe, "yqt", b)
                if is_first(b):
                    pe.wait_ge(w8_step, 6 * NCH)
                for c in range(NCH):
                    last = mm(Z[:, :], yqt[:, c, :], wf8q[:, c, :], start=c == 0, stop=c == NCH - 1)
                last.then_inc(S["z_mm"], 1)

            def xht_mm(b, par):
                ready(pe, "xh", b)
                for c in range(NCH):
                    last = pe.transpose(XHT[:, c * P:(c + 1) * P], xh[:, c * P:(c + 1) * P], ident[:, :])
                last.then_inc(S["xht_mm"], 1)

            def q1_mm(b, par):
                ready(pe, "xht", b)
                if is_first(b):
                    pe.wait_ge(wq1_ok, 1)
                for r in range(REP):
                    for c in range(NCH):
                        last = mm(QP1[:, r * P:(r + 1) * P], wq1[:, c, r * P:(r + 1) * P], xht[:, c, :],
                                  start=c == 0, stop=c == NCH - 1)
                last.then_inc(S["q1_mm"], 1)

            def ont1_mm(b, par):
                ready(pe, "on1", b)
                flat = on1[:, :, :, :].rearrange("p k r d -> p (k r d)")
                for c in range(NCH):
                    last = pe.transpose(ONT1[:, c * P:(c + 1) * P], flat[:, c * P:(c + 1) * P], ident[:, :])
                last.then_inc(S["ont1_mm"], 1)

            def wo_mm(b, par):
                ready(pe, "ont1", b)
                if is_first(b):
                    pe.wait_ge(W["wo1"], 16)
                for c in range(NCH):
                    last = mm(WO[:, :], ont1[:, c, :], wo1[:, c, :], start=c == 0, stop=c == NCH - 1)
                last.then_inc(S["wo_mm"], 1)

            def xlt_mm(b, par):
                ready(pe, "xl", b)
                for c in range(NCH):
                    last = pe.transpose(XLT[:, c * P:(c + 1) * P], xl[:, c * P:(c + 1) * P], ident[:, :])
                last.then_inc(S["xlt_mm"], 1)

            def lg_mm(b, par):
                ready(pe, "xlt", b)
                if is_first(b):
                    pe.wait_ge(W["wlow"], 16)
                for c in range(NCH):
                    last = mm(LG[:, 0:LOW + EXPERTS], xlt[:, c, :], wlow[:, c, :], start=c == 0, stop=c == NCH - 1)
                last.then_inc(S["lg_mm"], 1)

            def ls_mm(b, par):
                ready(pe, "ls", b)
                pe.transpose(LS[:, 0:P], ls[:, :], ident[:, :]).then_inc(S["ls_mm"], 1)

            def up_mm(b, par):
                ready(pe, "lst", b)
                if is_first(b):
                    pe.wait_ge(W["wup"], 16)
                mm(UP[:, :], lst[:, :], wup[:, :], start=True, stop=True).then_inc(S["up_mm"], 1)

            pe.wait_ge(w_early, 16 * 6)
            pe.wait_ge(o_clear, 1)

            PA_READERS = [("v0", 1), ("ont1", 4), ("x3", 4), ("xlt", 4), ("ls", 4), ("xht", 2), ("gelu", 1)]
            PB_READERS = [("xr", 2), ("on1", 4, 1), ("on1", 4, 2), ("yqt", 2), ("za", 2), ("mt1", 3), ("lst",
                          4), ("xo", 4)]
            PC_READERS = [("q1_r", 3), ("mt0", 1), ("qk", 0), ("k1_r", 2), ("on0", 1, 1), ("on0", 1, 2)]

            def slot(u, par):
                step(st1, u, par, 4, 0)
                step(st1, u, par, 4, 1)
                take(pe, u, PC_READERS, 0)
                step(q1_mm, u, par, 3)
                step(st1, u, par, 4, 2)
                step(st1, u, par, 4, 3)
                take(pe, u, PB_READERS, 0)
                step(y_mm, u, par, 2)
                take(pe, u, PA_READERS, 0)
                step(v0_mm, u, par, 1)
                step(st1, u, par, 4, 4)
                step(st1, u, par, 4, 5)
                take(pe, u, PC_READERS, 1)
                step(mt0_mm, u, par, 1)
                step(pv1, u, par, 4, 0)
                step(st1, u, par, 4, 6)
                step(st1, u, par, 4, 7)
                take(pe, u, PC_READERS, 2)
                step(qk_mm, u, par, 0)
                take(pe, u, PB_READERS, 1)
                step(ot1_mm, u, par, 4, 0)
                step(pv1, u, par, 4, 1)
                take(pe, u, PC_READERS, 3)
                step(kv1_mm, u, par, 2)
                take(pe, u, PB_READERS, 2)
                step(ot1_mm, u, par, 4, 1)
                step(st0, u, par, 1, 0)
                step(st0, u, par, 1, 1)
                step(sc1, u, par, 3, 0)
                step(sc1, u, par, 3, 1)
                take(pe, u, PA_READERS, 1)
                step(ont1_mm, u, par, 4)
                take(pe, u, PB_READERS, 3)
                step(yqt_mm, u, par, 2)
                step(sc1, u, par, 3, 2)
                step(st0, u, par, 1, 2)
                step(sc1, u, par, 3, 3)
                take(pe, u, PB_READERS, 4)
                step(z_mm, u, par, 2)
                step(sc1, u, par, 3, 4)
                step(sc1, u, par, 3, 5)
                take(pe, u, PA_READERS, 2)
                step(wo_mm, u, par, 4)
                step(st0, u, par, 1, 3)
                step(st0, u, par, 1, 4)
                step(sc1, u, par, 3, 6)
                step(pv0, u, par, 1, 0)
                step(st0, u, par, 1, 5)
                for k in range(1, 4):
                    step(pv0, u, par, 1, k)
                step(st0, u, par, 1, 6)
                step(st0, u, par, 1, 7)
                step(sc1, u, par, 3, 7)
                take(pe, u, PC_READERS, 4)
                step(ot0_mm, u, par, 1, 0)
                take(pe, u, PA_READERS, 3)
                step(xlt_mm, u, par, 4)
                step(pv0, u, par, 1, 4)
                step(pv0, u, par, 1, 5)
                take(pe, u, PB_READERS, 5)
                step(mt1_mm, u, par, 3)
                take(pe, u, PA_READERS, 4)
                step(lg_mm, u, par, 4)
                step(sc0, u, par, 0, 0)
                step(sc0, u, par, 0, 1)
                step(pv0, u, par, 1, 6)
                step(pv0, u, par, 1, 7)
                step(sc0, u, par, 0, 2)
                step(sc0, u, par, 0, 3)
                take(pe, u, PC_READERS, 5)
                step(ot0_mm, u, par, 1, 1)
                step(sc0, u, par, 0, 4)
                take(pe, u, PB_READERS, 6)
                step(ls_mm, u, par, 4)
                take(pe, u, PA_READERS, 5)
                step(xht_mm, u, par, 2)
                step(sc0, u, par, 0, 5)
                take(pe, u, PB_READERS, 7)
                step(up_mm, u, par, 4)
                take(pe, u, PA_READERS, 6)
                step(ont0_mm, u, par, 1)
                step(sc0, u, par, 0, 6)
                step(sc0, u, par, 0, 7)

            slots(pe, slot)

        @block.scalar
        def _(act):
            def qk_hi(b, par):
                ready(act, "qk", b)
                freed(act, "qk_out", b, 1)
                act.activation(s0[:, 0, :], qk[:, :], ACT.Copy).then_inc(S["qk_hi"], 1)

            def qk_mid(b, par):
                ready(act, "qk_r", b)
                act.activation(s0[:, 1, :], qkr[:, :], ACT.Copy).then_inc(S["qk_mid"], 1)

            def v0(b, par):
                ready(act, "v0_mm", b)
                freed(act, "os0", b, 2)
                act.activation(V0[:, par, :, :, 0:DH0],
                               V0P[:, 0:WIN * E0].rearrange("p (w h d) -> p w h d", w=WIN, h=H0),
                               ACT.Copy).then_inc(S["v0"], 1)

            def k1_hi(b, par):
                ready(act, "kv1_mm", b)
                freed(act, "k1_out", b, 1)
                act.activation(s1k[:, 0, :], KV1[:, 0:P], ACT.Copy).then_inc(S["k1_hi"], 1)
                freed(act, "st1_done", b, 2)
                act.activation(V1[:, par, :, 0:DH1], KV1[:, P:2 * P].rearrange("p (k d) -> p k d", k=KV),
                               ACT.Copy).then_inc(S["v1"], 1)

            def k1_mid(b, par):
                ready(act, "k1_r", b)
                act.activation(s1k[:, 1, :], k1r[:, :], ACT.Copy).then_inc(S["k1_mid"], 1)

            def mt0_copy(b, par):
                ready(act, "mt0_mm", b)
                freed(act, "mt0_out", b, 1)
                act.activation(mt0[:, :], MT0.bitcast(BF16)[0:2 * H0 * WIN, 0:P], ACT.Copy).then_inc(S["mt0"], 1)

            def mt1_copy(b, par):
                ready(act, "mt1_mm", b)
                freed(act, "mt1_out", b, 1)
                act.activation(mt1[:, :], MT1.bitcast(BF16)[0:2 * HQ, 0:P], ACT.Copy).then_inc(S["mt1"], 1)

            def exp_tile(b, layer, tile, dh):
                n = st_no(b, layer)
                act.wait_ge(st_ready, n + (tile + 1))
                at_least(act, pv_done, n + (tile - 7))
                act.activation(AT[:, tile, :], ST[tile % 2][:, :], ACT.Exp, scale=float(dh) ** -0.5)\
                    .then_inc(st_read, 1)

            def exp0(b, par, tile):
                exp_tile(b, 0, tile, DH0)

            def exp1(b, par, tile):
                exp_tile(b, 1, tile, DH1)

            def os0_copy(b, par, half):
                act.wait_ge(pv_done, st_no(b, 0) + (4 * half + 4))
                if half == 0:
                    freed(act, "ot0_mm", b, 1)
                else:
                    ready(act, "ot0_mm", b, 1)
                act.activation(os0[:, :], O[:, :], ACT.Copy).then_inc(S["os0"], 1)
                ready(act, "os0", b, half + 1)
                act.sem_inc(o_read, 1)
                if half == 1:
                    act.sem_inc(S["st0_done"], 1)

            def os1_copy(b, par, half):
                act.wait_ge(pv_done, st_no(b, 1) + (4 * half + 4))
                if half == 0:
                    freed(act, "ot1_mm", b, 1)
                else:
                    ready(act, "ot1_mm", b, 1)
                act.activation(os1[:, :], O[:, :], ACT.Copy).then_inc(S["os1"], 1)
                ready(act, "os1", b, half + 1)
                act.sem_inc(o_read, 1)
                if half == 1:
                    act.sem_inc(S["st1_done"], 1)

            def gelu(b, par):
                ready(act, "ont0_mm", b)
                freed(act, "y_mm", b, 2)
                act.activation(G[:, par, :, :], ONT0[:, 0:2 * P].rearrange("p (a i) -> p a i", a=2), ACT.Gelu,
                               bias=cols[:, BV:BV + 1]).then_inc(S["gelu"], 1)

            def yqt_copy(b, par):
                ready(act, "yqt_mm", b)
                freed(act, "z_mm", b, 1)
                act.activation(yqt[:, :, :], YQT.bitcast(BF16)[:, 0:DM].rearrange("p (c i) -> p c i", c=NCH),
                               ACT.Copy).then_inc(S["yqt"], 1)

            def za_copy(b, par):
                if is_first(b):
                    act.wait_ge(fac_ok, 7)
                ready(act, "z_mm", b)
                freed(act, "zq", b, 1)
                freed(act, "zq_r", b, 1)
                act.activation(za[:, :], Z[:, :], ACT.Copy, scale=fac[:, F_OUT:F_OUT + 1]).then_inc(S["za"], 1)

            def xht_copy(b, par):
                ready(act, "xht_mm", b)
                freed(act, "q1_mm", b, 1)
                act.activation(xht[:, :, :], XHT[:, :].rearrange("p (c i) -> p c i", c=NCH), ACT.Copy)\
                    .then_inc(S["xht"], 1)

            def q1_hi(b, par):
                ready(act, "q1_mm", b)
                freed(act, "q1_out", b, 1)
                act.activation(s1q[:, 0, :], QP1[:, :], ACT.Copy).then_inc(S["q1_hi"], 1)

            def q1_mid(b, par):
                ready(act, "q1_r", b)
                act.activation(s1q[:, 1, :], q1r[:, :], ACT.Copy).then_inc(S["q1_mid"], 1)

            def ont1_copy(b, par):
                ready(act, "ont1_mm", b)
                freed(act, "wo_mm", b, 1)
                act.activation(ont1[:, :, :], ONT1[:, :].rearrange("p (c i) -> p c i", c=NCH), ACT.Copy)\
                    .then_inc(S["ont1"], 1)

            def xlt_copy(b, par):
                ready(act, "xlt_mm", b)
                freed(act, "lg_mm", b, 1)
                act.activation(xlt[:, :, :], XLT[:, :].rearrange("p (c i) -> p c i", c=NCH), ACT.Copy)\
                    .then_inc(S["xlt"], 1)

            def router_exp(b, par):
                ready(act, "nml", b)
                freed(act, "wl", b, 1)
                act.activation(el[:, :], lg[:, :], ACT.Exp, bias=nml[:, 0:1], accum_out=sl[:, 0:1])\
                    .then_inc(S["el"], 1)

            def lst_copy(b, par):
                ready(act, "ls_mm", b)
                freed(act, "up_mm", b, 1)
                act.activation(lst[:, :], LS[:, 0:P], ACT.Copy).then_inc(S["lst"], 1)

            act.wait_ge(w_early, 16 * 6)
            act.activation(gain[:, :], row[:, 0:4], ACT.Tanh).then_inc(gains_ok, 1)

            def slot(u, par):
                step(exp1, u, par, 4, 0)
                step(exp1, u, par, 4, 1)
                step(q1_hi, u, par, 3)
                step(exp1, u, par, 4, 2)
                step(exp1, u, par, 4, 3)
                step(q1_mid, u, par, 3)
                step(exp1, u, par, 4, 4)
                step(mt0_copy, u, par, 1)
                step(exp1, u, par, 4, 5)
                step(os1_copy, u, par, 4, 0)
                step(exp1, u, par, 4, 6)
                step(exp1, u, par, 4, 7)
                step(qk_hi, u, par, 0)
                step(v0, u, par, 1)
                step(os1_copy, u, par, 4, 1)
                step(qk_mid, u, par, 0)
                step(exp0, u, par, 1, 0)
                step(yqt_copy, u, par, 2)
                step(k1_hi, u, par, 2)
                step(exp0, u, par, 1, 1)
                step(ont1_copy, u, par, 4)
                step(za_copy, u, par, 2)
                for k in range(2, 5):
                    step(exp0, u, par, 1, k)
                step(k1_mid, u, par, 2)
                step(exp0, u, par, 1, 5)
                step(os0_copy, u, par, 1, 0)
                step(exp0, u, par, 1, 6)
                step(exp0, u, par, 1, 7)
                step(xlt_copy, u, par, 4)
                step(mt1_copy, u, par, 3)
                step(router_exp, u, par, 4)
                step(os0_copy, u, par, 1, 1)
                step(lst_copy, u, par, 4)
                step(xht_copy, u, par, 2)
                step(gelu, u, par, 1)

            slots(act, slot)

        @block.vector
        def _(dve):
            def binade(dst, src):
                return dve.tensor_scalar(dst.bitcast(I32), src.bitcast(I32), 0x7F800000, None, ALU.bitwise_and)

            def rounder(dst, src):
                return dve.tensor_scalar(dst, src, FP8_LEAST, FP8_STEP, ALU.max, ALU.mult)

            def stats(k, x, n, bn, mv, ve, b, scale=1.0, eps=EPS):
                if k == 0:
                    dve.bn_stats(bn[:, :], x).then_inc(S["bn%d" % n], 1)
                elif k == 1:
                    ready(dve, "bn%d" % n, b)
                    dve.sem_inc(dve_mark, 1)
                    dve.bn_aggr(mv[:, :], bn[:, :]).then_inc(S["mv%d" % n], 1)
                else:
                    ready(dve, "mv%d" % n, b)
                    dve.tensor_scalar(ve[:, :], mv[:, 1:2], scale, eps, ALU.mult, ALU.add)\
                        .then_inc(S["ve%d" % n], 1)

            def ln0_stats(b, par, k):
                if k == 0:
                    freed(dve, "xln0", b, 1)
                    loaded(dve, "ld_xa", b, par)
                stats(k, xa[:, par, :], 0, bn0, mv0, ve0, b)

            def normalise(out, x, mv, rs, s_out, s_rs, b):
                ready(dve, s_rs, b)
                dve.tensor_scalar(out, x, mv[:, 0:1], rs, ALU.subtract, ALU.mult).then_inc(S[s_out], 1)

            def ln0(b, par):
                freed(dve, "qk_mm", b, 1)
                normalise(xln0[:, :], xa[:, par, :], mv0, rs0[:, 0:1], "xln0", "rs0", b)

            def ln1(b, par):
                freed(dve, "yq", b, 1)
                freed(dve, "yq_r", b, 1)
                normalise(ya[:, :], x1[:, par, :], mv1, rs1[:, 1:2], "ya", "rsi1", b)

            def ln2(b, par):
                freed(dve, "xht_mm", b, 1)
                normalise(xh[:, :], x2[:, par, :], mv2, rs2[:, 0:1], "xh", "rs2", b)

            def ln3(b, par):
                freed(dve, "xlt_mm", b, 1)
                normalise(xl[:, :], x3[:, :], mv3, rs3[:, 0:1], "xl", "rs3", b)

            def qk_bias(b, par):
                if is_first(b):
                    dve.wait_ge(w_early, 16 * 6)
                ready(dve, "keep", b)
                freed(dve, "qk_r", b, 1)
                ready(dve, "qk_mm", b)
                dve.scalar_tensor_tensor(out=qk[:, :], in0=QK[:, :], scalar=cols[:, BQK:BQK + 1], in1=keep[:, :],
                                         op0=ALU.add, op1=ALU.mult).then_inc(S["qk"], 1)

            def max_tile(b, layer, tile, dst):
                if tile == 0:
                    freed(dve, ("nl0", "nl1")[layer], b, 1)
                dve.wait_ge(sc_ready, sc_no(b, layer) + (tile + 1))
                dve.tensor_reduce(dst, SC[tile % 2][:, :].rearrange("p (g j) -> p g j", g=4), AX_X, ALU.max,
                                  negate=True).then_inc(sc_read, 1)

            def max0(b, par, tile):
                max_tile(b, 0, tile, nm0[:, tile % 2 * 4:tile % 2 * 4 + 4, tile // 2])

            def max1(b, par, tile):
                max_tile(b, 1, tile, nm1[:, tile * REP:(tile + 1) * REP])

            def minus_max0(b, par, k):
                if k == 0:
                    freed(dve, "mt0_mm", b, 1)
                    dve.wait_ge(sc_read, sc_no(b, 0) + TILES)
                    dve.tensor_copy(nh0[:, 0, :, :], nm0[:, :, :]).then_inc(S["nh0"], 1)
                    return
                ready(dve, "nh0", b)
                dve.tensor_tensor(nh0[:, 1, :, :], nm0[:, :, :], nh0[:, 0, :, :], ALU.subtract)\
                    .then_inc(S["nl0"], 1)

            def minus_max1(b, par, k):
                if k == 0:
                    freed(dve, "mt1_mm", b, 1)
                    dve.wait_ge(sc_read, sc_no(b, 1) + TILES)
                    dve.tensor_copy(nh1[:, 0, :], nm1[:, :]).then_inc(S["nh1"], 1)
                    return
                ready(dve, "nh1", b)
                dve.tensor_tensor(nh1[:, 1, :], nm1[:, :], nh1[:, 0, :], ALU.subtract).then_inc(S["nl1"], 1)

            def norm0(b, par, k):
                half, k = k // 2, k % 2
                src = OT0[:, :].rearrange("p (w h d) -> p w h d", w=2, h=H0)
                rc = rc0[:, :].rearrange("p (w h) -> p w h", w=2)
                if k == 0:
                    ready(dve, "ot0_mm", b, half + 1)
                    dve.reciprocal(rc, src[:, :, :, DH0]).then_inc(S["rc0"], 1)
                    return
                if half == 0:
                    freed(dve, "ont0_mm", b, 1)
                ready(dve, "rc0", b, half + 1)
                dve.tensor_tensor(on0[:, 2 * half:2 * half + 2, :].rearrange("p w (h d) -> p w h d", h=H0),
                                  src[:, :, :, 0:DH0],
                                  rc.unsqueeze(3).to_broadcast([P, 2, H0, DH0]), ALU.mult)\
                    .then_inc(S["on0"], 1)

            def norm1(b, par, k):
                half, k = k // 2, k % 2
                src = OT1[:, :].rearrange("p (r g d) -> p g r d", r=REP, g=4)
                rc = rc1[:, :].rearrange("p (g r) -> p g r", g=4)
                if k == 0:
                    ready(dve, "ot1_mm", b, half + 1)
                    dve.reciprocal(rc, src[:, :, :, DH1]).then_inc(S["rc1"], 1)
                    return
                if half == 0:
                    freed(dve, "ont1_mm", b, 1)
                ready(dve, "rc1", b, half + 1)
                dve.tensor_tensor(on1[:, 4 * half:4 * half + 4, :, :], src[:, :, :, 0:DH1],
                                  rc.unsqueeze(3).to_broadcast([P, 4, REP, DH1]), ALU.mult)\
                    .then_inc(S["on1"], 1)

            def k1_rest(b, par):
                ready(dve, "v1", b)
                freed(dve, "k1_lo", b, 1)
                ready(dve, "k1_hi", b)
                dve.tensor_tensor(k1r[:, :], KV1[:, 0:P], s1k[:, 0, :], ALU.subtract).then_inc(S["k1_r"], 1)

            def add_att0(b, par, k):
                if k == 0:
                    freed(dve, "x2", b, 2)
                    loaded(dve, "ld_maskb", b, par)
                    ready(dve, "y_mm", b)
                    dve.scalar_tensor_tensor(out=x1[:, par, :], in0=Y[:, :], scalar=cols[:, BO:BO + 1],
                                             in1=maskb[:, par, :], op0=ALU.add, op1=ALU.mult).then_inc(S["xr"], 1)
                elif k == 1:
                    loaded(dve, "ld_xb", b, par)
                    ready(dve, "xr", b)
                    dve.scalar_tensor_tensor(out=x1[:, par, :], in0=x1[:, par, :], scalar=gain[:, 0:1],
                                             in1=xb[:, par, :], op0=ALU.mult, op1=ALU.add).then_inc(S["x1"], 1)
                else:
                    if k == 2:
                        freed(dve, "ya", b, 1)
                        ready(dve, "x1", b)
                    stats(k - 2, x1[:, par, :], 1, bn1, mv1, ve1, b)

            def quant_in(b, par, k):
                if k == 0:
                    ready(dve, "ya", b)
                    dve.tensor_scalar(ya[:, :], ya[:, :], FP8_MAX, -FP8_MAX, ALU.min, ALU.max).then_inc(S["yc"], 1)
                elif k == 1:
                    ready(dve, "yc", b)
                    binade(ye[:, :], ya[:, :]).then_inc(S["ye"], 1)
                elif k == 2:
                    ready(dve, "ye", b)
                    rounder(ye[:, :], ye[:, :]).then_inc(S["ym"], 1)
                elif k == 3:
                    ready(dve, "ym", b)
                    dve.tensor_tensor(ya[:, HALF:], ya[:, HALF:], ye[:, HALF:], ALU.add).then_inc(S["yt_r"], 1)
                else:
                    freed(dve, "yqt_mm", b, 1)
                    ready(dve, "yt_r", b)
                    dve.tensor_tensor(yq[:, HALF:], ya[:, HALF:], ye[:, HALF:], ALU.subtract)\
                        .then_inc(S["yq_r"], 1)

            def quant_out(b, par, k):
                if k == 0:
                    ready(dve, "za", b)
                    dve.tensor_scalar(za[:, :], za[:, :], FP8_MAX, -FP8_MAX, ALU.min, ALU.max).then_inc(S["zc"], 1)
                elif k == 1:
                    ready(dve, "zc", b)
                    binade(ze[:, :], za[:, :]).then_inc(S["ze"], 1)
                elif k == 2:
                    ready(dve, "ze", b)
                    rounder(ze[:, :], ze[:, :]).then_inc(S["zm"], 1)
                elif k == 3:
                    ready(dve, "zm", b)
                    dve.tensor_tensor(za[:, HALF:], za[:, HALF:], ze[:, HALF:], ALU.add).then_inc(S["zt_r"], 1)
                else:
                    freed(dve, "x2", b, 1)
                    ready(dve, "zt_r", b)
                    dve.tensor_tensor(zq[:, HALF:], za[:, HALF:], ze[:, HALF:], ALU.subtract)\
                        .then_inc(S["zq_r"], 1)

            def add_ffn0(b, par, k):
                if k == 0:
                    freed(dve, "x3", b, 2)
                    ready(dve, "zq", b)
                    ready(dve, "zq_r", b)
                    dve.scalar_tensor_tensor(out=x2[:, par, :], in0=zq[:, :], scalar=fac[:, G_OUT:G_OUT + 1],
                                             in1=x1[:, par, :], op0=ALU.mult, op1=ALU.add).then_inc(S["x2"], 1)
                    return
                if k == 1:
                    freed(dve, "xh", b, 1)
                    ready(dve, "x2", b)
                stats(k - 1, x2[:, par, :], 2, bn2, mv2, ve2, b, 1.0 + EPS, EPS * EPS)

            def q1_rest(b, par):
                freed(dve, "q1_lo", b, 1)
                ready(dve, "q1_hi", b)
                dve.tensor_tensor(q1r[:, :], QP1[:, :], s1q[:, 0, :], ALU.subtract).then_inc(S["q1_r"], 1)

            def q1_low(b, par):
                ready(dve, "q1_mid", b)
                dve.tensor_tensor(s1q[:, 2, :], q1r[:, :], s1q[:, 1, :], ALU.subtract).then_inc(S["q1_lo"], 1)

            def add_att1(b, par, k):
                if k == 0:
                    freed(dve, "xo", b, 1)
                    ready(dve, "wo_mm", b)
                    dve.scalar_tensor_tensor(out=x3[:, :], in0=WO[:, :], scalar=gain[:, 1:2], in1=x2[:, par, :],
                                             op0=ALU.mult, op1=ALU.add).then_inc(S["x3"], 1)
                    return
                if k == 1:
                    freed(dve, "xl", b, 1)
                    ready(dve, "x3", b)
                stats(k - 1, x3[:, :], 3, bn3, mv3, ve3, b)

            def router_max(b, par, k):
                if k == 0:
                    freed(dve, "el", b, 1)
                    ready(dve, "lg_mm", b)
                    dve.tensor_tensor(lg[:, :], LG[:, LOW:LOW + EXPERTS], row[:, 7:15], ALU.add).then_inc(S["lg"], 1)
                else:
                    ready(dve, "lg", b)
                    dve.tensor_reduce(nml[:, :], lg[:, :], AX_X, ALU.max, negate=True).then_inc(S["nml"], 1)

            def router_weigh(b, par, k):
                if k == 0:
                    ready(dve, "el", b)
                    dve.reciprocal(rl[:, :], sl[:, :]).then_inc(S["rl"], 1)
                elif k == 1:
                    ready(dve, "rl", b)
                    dve.tensor_scalar(wl[:, :], el[:, :], rl[:, 0:1], None, ALU.mult).then_inc(S["wl"], 1)
                else:
                    freed(dve, "ls_mm", b, 1)
                    ready(dve, "wl", b)
                    dve.tensor_tensor(ls[:, :].rearrange("p (e r) -> p e r", e=EXPERTS),
                                      LG[:, 0:LOW].rearrange("p (e r) -> p e r", e=EXPERTS),
                                      wl[:, :].unsqueeze(2).to_broadcast([P, EXPERTS, RANK]), ALU.mult)\
                        .then_inc(S["ls"], 1)

            def add_ffn1(b, par):
                freed(dve, "out", b, 2)
                ready(dve, "up_mm", b)
                dve.scalar_tensor_tensor(out=xo[:, par, :], in0=UP[:, :], scalar=fac[:, G_UP:G_UP + 1],
                                         in1=x3[:, :], op0=ALU.mult, op1=ALU.add).then_inc(S["xo"], 1)

            def scale_wq1(b, par):
                dve.wait_ge(W["wq1"], 16)
                for c in range(NCH):
                    last = dve.tensor_scalar(wq1[:, c, :], wq1[:, c, :], cols[:, LNW + c:LNW + c + 1], None, ALU.mult)
                last.then_inc(wq1_ok, 1)

            def round_w(b, par, c):
                if c == 0:
                    dve.wait_ge(W["wf8"], 16)
                n, w, m = 6 * c, wf8[:, c, :], wf8m[:, :]
                dve.tensor_scalar(w, w, fac[:, INV_W:INV_W + 1], FP8_MAX, ALU.mult, ALU.min).then_inc(w8_step, 1)
                dve.wait_ge(w8_step, n + 1)
                dve.tensor_scalar(w, w, -FP8_MAX, None, ALU.max).then_inc(w8_step, 1)
                dve.wait_ge(w8_step, n + 2)
                binade(m, w).then_inc(w8_step, 1)
                dve.wait_ge(w8_step, n + 3)
                rounder(m, m).then_inc(w8_step, 1)
                dve.wait_ge(w8_step, n + 4)
                dve.tensor_tensor(w, w, m, ALU.add).then_inc(w8_step, 1)
                dve.wait_ge(w8_step, n + 5)
                dve.tensor_tensor(wf8q[:, c, :], w, m, ALU.subtract).then_inc(w8_step, 1)

            def factors(b, par):
                dve.wait_ge(w_early, 16 * 6)
                dve.tensor_copy(identb[:, :], ident[:, :]).then_inc(idb_ok, 1)
                for k, s in ((INV_IN, 4), (INV_W, 5), (INV_OUT, 6)):
                    dve.reciprocal(fac[:, k:k + 1], row[:, s:s + 1]).then_inc(fac_ok, 1)
                dve.tensor_tensor(fac[:, PROD:PROD + 1], row[:, 4:5], row[:, 5:6], ALU.mult).then_inc(fac_ok, 1)
                dve.wait_ge(fac_ok, 4)
                dve.wait_ge(gains_ok, 1)
                dve.tensor_tensor(fac[:, F_OUT:F_OUT + 1], fac[:, PROD:PROD + 1], fac[:, INV_OUT:INV_OUT + 1],
                                  ALU.mult).then_inc(fac_ok, 1)
                dve.tensor_tensor(fac[:, G_OUT:G_OUT + 1], gain[:, 2:3], row[:, 6:7], ALU.mult).then_inc(fac_ok, 1)
                dve.tensor_scalar(fac[:, G_UP:G_UP + 1], gain[:, 3:4], EXPERT_GAIN, None, ALU.mult).then_inc(fac_ok, 1)
                dve.wait_ge(fac_ok, 7)

            dve.memset(O[:, :], 0.0).then_inc(o_clear, 1)
            fill(dve, K0, 0.0)
            dve.memset(V0[:, :, :, :, DH0:DH0 + 1], 1.0).then_inc(zeroed, 1)
            dve.memset(V1[:, :, :, DH1:DH1 + 1], 1.0).then_inc(zeroed, 1)

            def slot(u, par):
                step(ln0_stats, u, par, 0, 0)
                step(minus_max0, u, par, 1, 0)
                step(ln0_stats, u, par, 0, 1)
                step(q1_rest, u, par, 3)
                step(ln0_stats, u, par, 0, 2)
                step(add_att0, u, par, 2, 0)
                step(minus_max0, u, par, 1, 1)
                step(q1_low, u, par, 3)
                step(add_att0, u, par, 2, 1)
                step(ln0, u, par, 0)
                for k in range(2, 5):
                    step(add_att0, u, par, 2, k)
                step(qk_bias, u, par, 0)
                step(norm1, u, par, 4, 0)
                step(norm1, u, par, 4, 1)
                step(ln1, u, par, 2)
                once(scale_wq1, u, 1)
                for k in range(0, 4):
                    step(quant_in, u, par, 2, k)
                step(norm1, u, par, 4, 2)
                once(factors, u, 0)
                step(quant_in, u, par, 2, 4)
                step(norm1, u, par, 4, 3)
                step(max1, u, par, 3, 0)
                step(max1, u, par, 3, 1)
                once(round_w, u, 0, 0)
                step(max1, u, par, 3, 2)
                step(max1, u, par, 3, 3)
                step(k1_rest, u, par, 2)
                step(max1, u, par, 3, 4)
                step(quant_out, u, par, 2, 0)
                step(max1, u, par, 3, 5)
                step(quant_out, u, par, 2, 1)
                once(round_w, u, 1, 2)
                for k in range(2, 5):
                    step(quant_out, u, par, 2, k)
                step(add_att1, u, par, 4, 0)
                step(add_att1, u, par, 4, 1)
                once(round_w, u, 1, 3)
                step(add_att1, u, par, 4, 2)
                step(add_att1, u, par, 4, 3)
                step(max1, u, par, 3, 6)
                step(ln3, u, par, 4)
                step(max1, u, par, 3, 7)
                step(norm0, u, par, 1, 0)
                step(minus_max1, u, par, 3, 0)
                once(round_w, u, 0, 1)
                step(minus_max1, u, par, 3, 1)
                step(add_ffn0, u, par, 2, 0)
                step(norm0, u, par, 1, 1)
                step(add_ffn0, u, par, 2, 1)
                step(router_max, u, par, 4, 0)
                step(add_ffn0, u, par, 2, 2)
                step(router_max, u, par, 4, 1)
                step(max0, u, par, 0, 0)
                step(add_ffn0, u, par, 2, 3)
                step(max0, u, par, 0, 1)
                step(router_weigh, u, par, 4, 0)
                step(max0, u, par, 0, 2)
                step(router_weigh, u, par, 4, 1)
                step(ln2, u, par, 2)
                step(router_weigh, u, par, 4, 2)
                step(max0, u, par, 0, 3)
                step(norm0, u, par, 1, 2)
                step(max0, u, par, 0, 4)
                step(norm0, u, par, 1, 3)
                step(max0, u, par, 0, 5)
                step(add_ffn1, u, par, 4)
                step(max0, u, par, 0, 6)
                step(max0, u, par, 0, 7)

            slots(dve, slot)

        @block.gpsimd
        def _(pool):
            def root(rs, ve, s_ve, s_rs, b):
                ready(pool, s_ve, b)
                pool.tensor_tensor(rs[:, 0:1], ve[:, :], halfm[:, :], ALU.pow).then_inc(S[s_rs], 1)

            def rs0_(b, par):
                root(rs0, ve0, "ve0", "rs0", b)

            def rs1_(b, par):
                if is_first(b):
                    pool.wait_ge(fac_ok, 7)
                root(rs1, ve1, "ve1", "rs1", b)
                ready(pool, "rs1", b)
                pool.tensor_tensor(rs1[:, 1:2], rs1[:, 0:1], fac[:, INV_IN:INV_IN + 1], ALU.mult)\
                    .then_inc(S["rsi1"], 1)

            def rs2_(b, par):
                root(rs2, ve2, "ve2", "rs2", b)

            def rs3_(b, par):
                root(rs3, ve3, "ve3", "rs3", b)

            def keep_rows(b, par):
                if is_first(b):
                    pool.wait_ge(w_early, 16 * 6)
                freed(pool, "qk", b, 1)
                freed(pool, "mrow_in", b, 1)
                loaded(pool, "ld_maska", b, par)
                pool.sem_inc(pool_mark, 1)
                pool.tensor_scalar(keep[:, :], maska[:, par, :], 0.0, cols[:, QROW:QROW + 1], ALU.is_gt, ALU.max)\
                    .then_inc(S["keep"], 1)
                ready(pool, "keep", b)
                pool.sem_inc(pool_mark, 1)
                pool.tensor_scalar(mrow[:, :], keep[:, :], -1.0, MASKED, ALU.add, ALU.mult).then_inc(S["mrow"], 1)

            def qk_rest(b, par):
                freed(pool, "qk_mid", b, 1)
                freed(pool, "qk_lo", b, 1)
                ready(pool, "qk_hi", b)
                pool.tensor_tensor(qkr[:, :], qk[:, :], s0[:, 0, :], ALU.subtract).then_inc(S["qk_r"], 1)

            def qk_low(b, par):
                ready(pool, "qk_mid", b)
                pool.tensor_tensor(s0[:, 2, :], qkr[:, :], s0[:, 1, :], ALU.subtract).then_inc(S["qk_lo"], 1)

            def k1_low(b, par):
                ready(pool, "k1_mid", b)
                pool.tensor_tensor(s1k[:, 2, :], k1r[:, :], s1k[:, 1, :], ALU.subtract).then_inc(S["k1_lo"], 1)

            def round_in(b, par):
                ready(pool, "ym", b)
                pool.tensor_tensor(ya[:, 0:HALF], ya[:, 0:HALF], ye[:, 0:HALF], ALU.add).then_inc(S["yt"], 1)
                freed(pool, "yqt_mm", b, 1)
                ready(pool, "yt", b)
                pool.tensor_tensor(yq[:, 0:HALF], ya[:, 0:HALF], ye[:, 0:HALF], ALU.subtract).then_inc(S["yq"], 1)

            def round_out(b, par):
                ready(pool, "zm", b)
                pool.tensor_tensor(za[:, 0:HALF], za[:, 0:HALF], ze[:, 0:HALF], ALU.add).then_inc(S["zt"], 1)
                freed(pool, "x2", b, 1)
                ready(pool, "zt", b)
                pool.tensor_tensor(zq[:, 0:HALF], za[:, 0:HALF], ze[:, 0:HALF], ALU.subtract).then_inc(S["zq"], 1)

            def fill_q1(b, par):
                fill(pool, Q1, 1.0, q1_ones)

            pool.memset(halfm[:, :], -0.5).then_inc(half_ok, 1)
            fill(pool, Q0, 1.0)
            fill(pool, K1, 0.0)
            pool.wait_ge(half_ok, 1)

            def slot(u, par):
                step(round_out, u, par, 3)
                step(k1_low, u, par, 3)
                step(rs2_, u, par, 3)
                once(fill_q1, u, 1)
                step(rs0_, u, par, 0)
                step(keep_rows, u, par, 0)
                step(rs1_, u, par, 2)
                step(qk_rest, u, par, 0)
                step(round_in, u, par, 2)
                step(qk_low, u, par, 0)
                step(rs3_, u, par, 4)

            slots(pool, slot)


_SPECS = ["x", "ctx", "ctxt", "mask", "ident", "wqk0", "wv0", "wo0", "cols", "row", "wf8", "wq1", "wk1", "wv1",
          "wo1", "wlow", "wup"]


def kernel(**inputs):
    import numpy as np
    import concourse.bacc as bacc
    from concourse.bass_utils import run_bass_kernel_spmd

    a = {k: np.asarray(v) for k, v in inputs.items()}

    def chunks(w):
        return w.T.reshape(NCH, P, w.shape[0]).transpose(1, 0, 2)

    def col(*parts):
        return np.concatenate([np.asarray(p).reshape(-1) for p in parts]).reshape(P, 1)

    rows_q = np.concatenate([np.ones(E0, np.float32), np.zeros(E0, np.float32)])
    wq0, wk0 = (a[n].reshape(H0, DH0, P).transpose(1, 0, 2).reshape(E0, P) for n in ("L0_xattn_Wq", "L0_xattn_Wk"))
    bq0, bk0 = (a[n].reshape(H0, DH0).T for n in ("L0_xattn_bq", "L0_xattn_bk"))
    wq1 = a["L1_xattn_wq"].reshape(KV, REP, DH1, DM).transpose(1, 2, 0, 3).reshape(DM, DM)
    wk1 = a["L1_xattn_wk"].reshape(KV, DH1, DM).transpose(1, 0, 2).reshape(P, DM)
    wo0 = a["L0_xattn_Wo"].T
    zero0 = np.zeros_like(wo0)
    low = np.concatenate([a["L1_ffn_A"].reshape(LOW, DM), a["L1_ffn_Wr"]], axis=0)
    arrays = {
        "x": a["x"],
        "ctx": a["ctx_4096"],
        "ctxt": a["ctx_4096"].transpose(0, 2, 1).reshape(BATCH, NCH, P, P).transpose(0, 2, 1, 3),
        "mask": a["mask_Bx1x4096_ff1"].reshape(BATCH, DM),
        "ident": np.eye(P, dtype=np.float32),
        "wqk0": np.concatenate([wq0.T, wk0.T], axis=1),
        "wv0": a["L0_xattn_Wv"].T,
        "wo0": np.stack([np.concatenate([wo0, zero0]), np.concatenate([zero0, wo0])], axis=1),
        "cols": np.concatenate([col(bq0, bk0), col(a["L0_xattn_bv"], a["L0_xattn_bv"]),
                                col(a["L0_xattn_bo"]), col(rows_q), a["L1_xattn_ln_w"].reshape(NCH, P).T], axis=1),
        "row": np.concatenate([a["g_xattn"], a["g_ffn"], a["L0_ffn_input_scale"].reshape(1),
                               a["L0_ffn_weight_scale"].reshape(1), a["L0_ffn_output_scale"].reshape(1),
                               a["L1_ffn_br"]]),
        "wf8": chunks(a["L0_ffn_w"]),
        "wq1": chunks(wq1),
        "wk1": chunks(wk1),
        "wv1": chunks(a["L1_xattn_wv"]),
        "wo1": chunks(a["L1_xattn_wo"]),
        "wlow": chunks(low),
        "wup": a["L1_ffn_B"].transpose(0, 2, 1).reshape(LOW, DM),
    }
    arrays = {k: np.ascontiguousarray(v) for k, v in arrays.items()}
    nc = bacc.Bacc("TRN2", target_bir_lowering=False, num_devices=1)
    t = {k: nc.dram_tensor("in_" + k, arrays[k].shape, F32, kind="ExternalInput").ap() for k in _SPECS}
    t["out"] = nc.dram_tensor("out_x", (BATCH, P, DM), F32, kind="ExternalOutput").ap()
    flamingo_block(nc, t)
    r = run_bass_kernel_spmd(nc, [{"in_" + k: arrays[k] for k in _SPECS}], core_ids=[0])
    return r.results[0]["out_x"]
```
